# Optimizing a Trainium2 kernel written in Bass

```python
import numpy as np
import jax
import jax.numpy as jnp

def _softmax(x, axis=-1):
    return jax.nn.softmax(x, axis=axis)

def _gelu(x):
    return jax.nn.gelu(x, approximate=True)

def _silu(x):
    return jax.nn.silu(x)

def _sigmoid(x):
    return jax.nn.sigmoid(x)

def _layernorm(x, axis=-1, eps=1e-05):
    m = jnp.mean(x, axis=axis, keepdims=True)
    v = jnp.var(x, axis=axis, keepdims=True)
    return (x - m) / jnp.sqrt(v + eps)

def _scatter_add(tgt, idx, src, axis=0):
    return tgt.at[idx].add(src)

def _segment_sum(src, seg, n):
    return jax.ops.segment_sum(src, seg, n)
kernel_name = 'mk_perceiver_d4_seqx_r4_2e2c43'

def setup_inputs(seed: int=0):
    np.random.seed(seed)
    _w = jnp.asarray

    def _rec_inputs():
        import jax
        import jax.numpy as jnp
        _rk = jax.random.key(seed)
        x = -0.0002928 + 1 * jax.random.normal(jax.random.fold_in(_rk, 1), (2, 256, 256), jnp.float32)
        _lenS = 256 - jax.random.randint(jax.random.fold_in(_rk, 7), (2,), 0, max(1, 256 // 4) + 1, jnp.int32)
        _lenS2 = 4096 - jax.random.randint(jax.random.fold_in(_rk, 8), (2,), 0, max(1, 4096 // 4) + 1, jnp.int32)
        _ctx_1024P = jax.random.normal(jax.random.fold_in(_rk, 11), (2, 16, 256), jnp.float32)
        _ctx_1024c = jax.random.dirichlet(jax.random.fold_in(_rk, 511), 0.3 * jnp.ones((16,), jnp.float32), (2, 4096))
        _ctx_1024t = jnp.einsum('bsk,bkd->bsd', _ctx_1024c, _ctx_1024P)
        _ctx_1024t = _ctx_1024t * jax.lax.rsqrt(jnp.mean(jnp.square(_ctx_1024t)) + 1e-12) * 0.953939
        ctx_1024 = -1.39393e-06 + 0.999914 * (_ctx_1024t + 0.3 * jax.random.normal(jax.random.fold_in(_rk, 611), (2, 4096, 256), jnp.float32))
        itok_BxS_0_255 = jax.random.randint(jax.random.fold_in(_rk, 13), (2, 256), 0, 64, jnp.int32)
        _validS = jnp.arange(256)[None, :] < _lenS[:, None]
        _validS2 = jnp.arange(4096)[None, :] < _lenS2[:, None]
        _causal = jnp.tril(jnp.ones((256, 256), dtype=bool))
        mask_BxS2_ik1 = jnp.where(jnp.broadcast_to(_validS2[:, :], (2, 4096)), 1, 0).astype(jnp.int32)
        mask_BxS2_bk0 = jnp.logical_not(jnp.broadcast_to(_validS2[:, :], (2, 4096)))
        return (x, ctx_1024, itok_BxS_0_255, mask_BxS2_ik1, mask_BxS2_bk0)
    x, ctx_1024, itok_BxS_0_255, mask_BxS2_ik1, mask_BxS2_bk0 = _rec_inputs()

    def _L0_xattn_setup():
        import jax, jax.numpy as jnp
        import numpy as np
        EMBED_DIM = 256
        NUM_HEADS = 16
        HEAD_DIM = EMBED_DIM // NUM_HEADS
        key = jax.random.key(seed)
        ks = jax.random.split(key, 8)
        B, S, D = (2, 512, EMBED_DIM)
        scale = 1.0 / np.sqrt(D)
        return {'query': jax.random.normal(ks[0], (B, S, D), dtype=jnp.float32), 'key': jax.random.normal(ks[1], (B, S, D), dtype=jnp.float32), 'value': jax.random.normal(ks[2], (B, S, D), dtype=jnp.float32), 'Wq': jax.random.normal(ks[3], (D, D), dtype=jnp.float32) * scale, 'Wk': jax.random.normal(ks[4], (D, D), dtype=jnp.float32) * scale, 'Wv': jax.random.normal(ks[5], (D, D), dtype=jnp.float32) * scale, 'Wo': jax.random.normal(ks[6], (D, D), dtype=jnp.float32) * scale, 'attention_mask': jax.random.randint(ks[7], (B, S), 0, 2, dtype=jnp.int32)}
    _L0_xattn_all = _L0_xattn_setup()
    _L0_xattn_in = {k: v for k, v in _L0_xattn_all.items() if k in ('Wq', 'Wk', 'Wv', 'Wo')}
    del _L0_xattn_all

    def _L0_attn_setup():
        import jax, jax.numpy as jnp
        import numpy as np
        from functools import partial
        B_, L_, H_, DIN_, K_, N_, R_ = (2, 512, 256, 512, 4, 16, 64)

        def _selective_scan(x, delta, A, Bm, Cm, D):
            dA = jnp.exp(jnp.einsum('bld,dn->bldn', delta, A))
            dBx = jnp.einsum('bld,bln->bldn', delta * x, Bm)
            b, l, d, n = dA.shape

            def step(z, inp):
                dA_t, dBx_t, c_t = inp
                z = dA_t * z + dBx_t
                y = jnp.einsum('bdn,bn->bd', z, c_t)
                return (z, y)
            z0 = jnp.zeros((b, d, n), x.dtype)
            _, ys = jax.lax.scan(step, z0, (jnp.moveaxis(dA, 1, 0), jnp.moveaxis(dBx, 1, 0), jnp.moveaxis(Cm, 1, 0)))
            y = jnp.moveaxis(ys, 0, 1)
            return y + x * D
        key = jax.random.key(seed)
        ks = jax.random.split(key, 9)
        s = lambda f: 1.0 / f ** 0.5
        A = jnp.tile(jnp.arange(1, N_ + 1, dtype=jnp.float32)[None, :], (DIN_, 1))
        return {'hidden_states': jax.random.normal(ks[0], (B_, L_, H_), jnp.float32), 'w_in': jax.random.normal(ks[1], (2 * DIN_, H_), jnp.float32) * s(H_), 'w_conv': jax.random.normal(ks[2], (DIN_, 1, K_), jnp.float32) * s(DIN_), 'w_xproj': jax.random.normal(ks[3], (R_ + 2 * N_, DIN_), jnp.float32) * s(DIN_), 'w_dt': jax.random.normal(ks[4], (DIN_, R_), jnp.float32) * s(R_), 'b_dt': jnp.zeros((DIN_,), jnp.float32), 'A_log': jnp.log(A), 'D': jnp.ones((DIN_,), jnp.float32), 'w_out': jax.random.normal(ks[5], (H_, DIN_), jnp.float32) * s(DIN_)}
    _L0_attn_all = _L0_attn_setup()
    _L0_attn_in = {k: v for k, v in _L0_attn_all.items() if k in ('w_in', 'w_conv', 'w_xproj', 'w_dt', 'b_dt', 'A_log', 'D', 'w_out')}
    del _L0_attn_all

    def _L0_ffn_setup():
        import jax, jax.numpy as jnp
        import numpy as np
        B, S, H, E, K = (2, 256, 256, 8, 2)
        F = 4 * H
        key = jax.random.key(seed)
        ks = jax.random.split(key, 8)
        std = 0.02
        return {'x': jax.random.normal(ks[0], (B, S, H), jnp.float32), 'gate_w': jax.random.normal(ks[1], (E, H), jnp.float32) * (std / np.sqrt(H)), 'gate_bias': jnp.zeros((E,), jnp.float32), 'Wu': jax.random.normal(ks[2], (E, F, H), jnp.float32) * std, 'bu': jnp.zeros((E, F), jnp.float32), 'Wd': jax.random.normal(ks[3], (E, H, F), jnp.float32) * std, 'bd': jnp.zeros((E, H), jnp.float32), 'sWu': jax.random.normal(ks[4], (F, H), jnp.float32) * std, 'sbu': jnp.zeros((F,), jnp.float32), 'sWd': jax.random.normal(ks[5], (H, F), jnp.float32) * std, 'sbd': jnp.zeros((H,), jnp.float32)}
    _L0_ffn_all = _L0_ffn_setup()
    _L0_ffn_in = {k: v for k, v in _L0_ffn_all.items() if k in ('gate_w', 'gate_bias', 'Wu', 'bu', 'Wd', 'bd', 'sWu', 'sbu', 'sWd', 'sbd')}
    del _L0_ffn_all

    def _L1_xattn_setup():
        import jax, jax.numpy as jnp
        import numpy as np
        D_MODEL = 256
        B, S = (4, 512)
        key = jax.random.key(seed)
        ks = jax.random.split(key, 10)
        s = 1.0 / np.sqrt(D_MODEL)
        return {'k': jax.random.normal(ks[0], (B, S, D_MODEL), jnp.float32), 'v': jax.random.normal(ks[1], (B, S, D_MODEL), jnp.float32), 'q': jax.random.normal(ks[2], (B, S, D_MODEL), jnp.float32), 'Wk': jax.random.normal(ks[3], (D_MODEL, D_MODEL), jnp.float32) * s, 'Wv': jax.random.normal(ks[4], (D_MODEL, D_MODEL), jnp.float32) * s, 'bv': jnp.zeros((D_MODEL,), jnp.float32), 'Wq': jax.random.normal(ks[5], (D_MODEL, D_MODEL), jnp.float32) * s, 'bq': jnp.zeros((D_MODEL,), jnp.float32), 'Wo': jax.random.normal(ks[6], (D_MODEL, D_MODEL), jnp.float32) * s, 'bo': jnp.zeros((D_MODEL,), jnp.float32)}
    _L1_xattn_all = _L1_xattn_setup()
    _L1_xattn_in = {k: v for k, v in _L1_xattn_all.items() if k in ('Wk', 'Wv', 'bv', 'Wq', 'bq', 'Wo', 'bo')}
    del _L1_xattn_all

    def _L1_attn_setup():
        import jax, jax.numpy as jnp
        import numpy as np
        D_K, D_MODEL, NUM_HEADS = (64, 256, 16)

        def _xavier(key, shape):
            fan_in, fan_out = (shape[-2], shape[-1])
            limit = float(np.sqrt(6.0 / (fan_in + fan_out)))
            return jax.random.uniform(key, shape, jnp.float32, -limit, limit)
        key = jax.random.key(seed)
        kx, kq, kk, kv, ko = jax.random.split(key, 5)
        x = jax.random.normal(kx, (2, 512, D_MODEL), dtype=jnp.float32)
        w_q = _xavier(kq, (NUM_HEADS, D_MODEL, D_K))
        w_k = _xavier(kk, (NUM_HEADS, D_MODEL, D_K))
        w_v = _xavier(kv, (NUM_HEADS, D_MODEL, D_K))
        w_o = _xavier(ko, (NUM_HEADS * D_K, D_MODEL))
        return {'x': x, 'w_q': w_q, 'w_k': w_k, 'w_v': w_v, 'w_o': w_o}
    _L1_attn_all = _L1_attn_setup()
    _L1_attn_in = {k: v for k, v in _L1_attn_all.items() if k in ('w_q', 'w_k', 'w_v', 'w_o')}
    del _L1_attn_all

    def _L1_ffn_setup():
        import jax, jax.numpy as jnp
        import numpy as np
        D_IN, D_HID = (256, 1024)

        def _ternary(key, shape):
            return jax.random.randint(key, shape, -1, 2).astype(jnp.float32)

        def _tlin(x, w, s):
            return jnp.einsum('bsi,oi->bso', x, w) * s
        key = jax.random.key(seed)
        ks = jax.random.split(key, 12)
        inv = lambda fan: 1.0 / np.sqrt(fan).astype(np.float32)
        return {'x': jax.random.normal(ks[0], (4, 512, D_IN), dtype=jnp.float32), 'w1_w': _ternary(ks[1], (D_HID, D_IN)), 'w1_s': jax.random.uniform(ks[2], (D_HID,), dtype=jnp.float32) * inv(D_IN), 'w2_w': _ternary(ks[3], (D_HID, D_IN)), 'w2_s': jax.random.uniform(ks[4], (D_HID,), dtype=jnp.float32) * inv(D_IN), 'h1_w': _ternary(ks[5], (D_HID, D_HID)), 'h1_s': jax.random.uniform(ks[6], (D_HID,), dtype=jnp.float32) * inv(D_HID), 'h2_w': _ternary(ks[7], (D_HID, D_HID)), 'h2_s': jax.random.uniform(ks[8], (D_HID,), dtype=jnp.float32) * inv(D_HID), 'w3_w': _ternary(ks[9], (D_IN, D_HID)), 'w3_s': jax.random.uniform(ks[10], (D_IN,), dtype=jnp.float32) * inv(D_HID)}
    _L1_ffn_all = _L1_ffn_setup()
    _L1_ffn_in = {k: v for k, v in _L1_ffn_all.items() if k in ('w1_w', 'w1_s', 'w2_w', 'w2_s', 'h1_w', 'h1_s', 'h2_w', 'h2_s', 'w3_w', 'w3_s')}
    del _L1_ffn_all

    def _L2_xattn_setup():
        import jax, jax.numpy as jnp
        import numpy as np
        N_LAYERS = 4
        H = 16
        LOOKBACK = 128
        EPS = 1e-06
        ROPE_BASE = 10000.0
        NEG = jnp.float32(-1e+30)

        def rmsnorm(x, w):
            return x * jax.lax.rsqrt(jnp.mean(x * x, axis=-1, keepdims=True) + EPS) * w

        def rope_cache(L, hd):
            inv = 1.0 / ROPE_BASE ** (jnp.arange(0, hd, 2, dtype=jnp.float32) / hd)
            t = jnp.arange(L, dtype=jnp.float32)
            f = t[:, None] * inv[None, :]
            emb = jnp.concatenate([f, f], axis=-1)
            return (jnp.cos(emb), jnp.sin(emb))

        def apply_rope(x, cos, sin):
            d = x.shape[-1]
            x1, x2 = (x[..., :d // 2], x[..., d // 2:])
            rot = jnp.concatenate([-x2, x1], axis=-1)
            return x * cos + rot * sin

        def split_heads(x, n_heads):
            B, L, D = x.shape
            return x.reshape(B, L, n_heads, D // n_heads).transpose(0, 2, 1, 3)

        def merge_heads(x):
            B, h, L, d = x.shape
            return x.transpose(0, 2, 1, 3).reshape(B, L, h * d)

        def sdpa(q, k, v, bias):
            scale = q.shape[-1] ** (-0.5)
            s = jnp.einsum('bhqd,bhkd->bhqk', q, k) * scale + bias
            p = jax.nn.softmax(s, axis=-1)
            return jnp.einsum('bhqk,bhkd->bhqd', p, v)

        def forward(x, memory, seg_ids, Wqkv, bqkv, Wo, bo, Wq_c, Wkv_c, Wo_c, Wg, Wu, Wd, n1, n2, n3, nf):
            B, L, D = x.shape
            S = memory.shape[1]
            hd = D // H
            cos, sin = rope_cache(L, hd)
            i = jnp.arange(L)
            causal_bias = jnp.where(i[None, :] <= i[:, None], 0.0, NEG)[None, None]
            j = jnp.arange(S)
            allowed = (j[None, None, :] <= seg_ids[:, :, None]) & (j[None, None, :] > seg_ids[:, :, None] - LOOKBACK)
            cross_bias = jnp.where(allowed, 0.0, NEG)[:, None]
            for l in range(N_LAYERS):
                h = rmsnorm(x, n1[l])
                qkv = h @ Wqkv[l].T + bqkv[l]
                q, k, v = jnp.split(qkv, 3, axis=-1)
                q = apply_rope(split_heads(q, H), cos, sin)
                k = apply_rope(split_heads(k, H), cos, sin)
                v = split_heads(v, H)
                o = merge_heads(sdpa(q, k, v, causal_bias)) @ Wo[l].T + bo[l]
                x = x + o
                h2 = rmsnorm(x, n2[l])
                qc = split_heads(h2 @ Wq_c[l].T, H)
                kv = memory @ Wkv_c[l].T
                kc, vc = jnp.split(kv, 2, axis=-1)
                kc, vc = (split_heads(kc, H), split_heads(vc, H))
                oc = merge_heads(sdpa(qc, kc, vc, cross_bias)) @ Wo_c[l].T
                x = x + oc
                h3 = rmsnorm(x, n3[l])
                x = x + jax.nn.silu(h3 @ Wg[l].T) * (h3 @ Wu[l].T) @ Wd[l].T
            return rmsnorm(x, nf)
        key = jax.random.key(seed)
        ks = jax.random.split(key, 16)
        B, L, S, D, F = (2, 512, 64, 256, 1024)
        w = 0.02
        inp = {'x': jax.random.normal(ks[0], (B, L, D), jnp.float32), 'memory': jax.random.normal(ks[1], (B, S, D), jnp.float32), 'seg_ids': jnp.sort(jax.random.randint(ks[2], (B, L), 0, S), axis=-1), 'Wqkv': jax.random.normal(ks[3], (N_LAYERS, 3 * D, D), jnp.float32) * w, 'bqkv': jnp.zeros((N_LAYERS, 3 * D), jnp.float32), 'Wo': jax.random.normal(ks[4], (N_LAYERS, D, D), jnp.float32) * w, 'bo': jnp.zeros((N_LAYERS, D), jnp.float32), 'Wq_c': jax.random.normal(ks[5], (N_LAYERS, D, D), jnp.float32) * w, 'Wkv_c': jax.random.normal(ks[6], (N_LAYERS, 2 * D, D), jnp.float32) * w, 'Wo_c': jax.random.normal(ks[7], (N_LAYERS, D, D), jnp.float32) * w, 'Wg': jax.random.normal(ks[8], (N_LAYERS, F, D), jnp.float32) * w, 'Wu': jax.random.normal(ks[9], (N_LAYERS, F, D), jnp.float32) * w, 'Wd': jax.random.normal(ks[10], (N_LAYERS, D, F), jnp.float32) * w, 'n1': jnp.ones((N_LAYERS, D), jnp.float32), 'n2': jnp.ones((N_LAYERS, D), jnp.float32), 'n3': jnp.ones((N_LAYERS, D), jnp.float32), 'nf': jnp.ones((D,), jnp.float32)}
        return inp
    _L2_xattn_all = _L2_xattn_setup()
    _L2_xattn_in = {k: v for k, v in _L2_xattn_all.items() if k in ('Wqkv', 'bqkv', 'Wo', 'bo', 'Wq_c', 'Wkv_c', 'Wo_c', 'Wg', 'Wu', 'Wd', 'n1', 'n2', 'n3', 'nf')}
    del _L2_xattn_all

    def _L2_attn_setup():
        import jax, jax.numpy as jnp
        import numpy as np
        import math
        NUM_HEADS = 16
        NUM_BUCKETS = 32
        MAX_DISTANCE = 128
        ALPHA = 32.0

        def _rel_bucket(rel_pos):
            nb = NUM_BUCKETS // 2
            buckets = (rel_pos > 0).astype(jnp.int32) * nb
            rel_pos = jnp.abs(rel_pos)
            max_exact = nb // 2
            is_small = rel_pos < max_exact
            large = max_exact + (jnp.log(rel_pos.astype(jnp.float32) / max_exact + 1e-06) / math.log(MAX_DISTANCE / max_exact) * (nb - max_exact)).astype(jnp.int32)
            large = jnp.minimum(large, nb - 1)
            return buckets + jnp.where(is_small, rel_pos, large)
        key = jax.random.key(seed)
        ks = jax.random.split(key, 12)
        T, B, E = (256, 4, 256)
        hd = E // NUM_HEADS
        s = 0.02
        f32 = jnp.float32
        return {'query': jax.random.normal(ks[0], (T, B, E), f32), 'q_w': jax.random.normal(ks[1], (E, E), f32) * s, 'q_b': jnp.zeros((E,), f32), 'k_w': jax.random.normal(ks[2], (E, E), f32) * s, 'k_b': jnp.zeros((E,), f32), 'v_w': jax.random.normal(ks[3], (E, E), f32) * s, 'v_b': jnp.zeros((E,), f32), 'out_w': jax.random.normal(ks[4], (E, E), f32) * s, 'out_b': jnp.zeros((E,), f32), 'rel_emb': jax.random.normal(ks[5], (NUM_BUCKETS, NUM_HEADS), f32) * 0.1, 'grep_w': jax.random.normal(ks[6], (hd, 8), f32) * s, 'grep_b': jnp.zeros((8,), f32), 'grep_a': jnp.ones((1, NUM_HEADS, 1, 1), f32), 'bias_k': jax.random.normal(ks[7], (1, 1, E), f32) * s, 'bias_v': jax.random.normal(ks[8], (1, 1, E), f32) * s}
    _L2_attn_all = _L2_attn_setup()
    _L2_attn_in = {k: v for k, v in _L2_attn_all.items() if k in ('q_w', 'q_b', 'k_w', 'k_b', 'v_w', 'v_b', 'out_w', 'out_b', 'rel_emb', 'grep_w', 'grep_b', 'grep_a', 'bias_k', 'bias_v')}
    del _L2_attn_all

    def _L2_ffn_setup():
        import jax, jax.numpy as jnp
        import numpy as np
        E = 8
        TOP_K = 2
        ROUTE_SCALE = 1.0
        ALPHA = 1.702
        LIMIT = 7.0
        D = 256
        F = 256
        B, S = (2, 256)

        def swiglu(h):
            g = jnp.minimum(h[..., ::2], LIMIT)
            l = jnp.clip(h[..., 1::2], -LIMIT, LIMIT)
            return g * jax.nn.sigmoid(ALPHA * g) * (l + 1.0)
        if __name__ == '__main__':
            out = reference(**setup_inputs())
            print(out.shape, out.dtype)
        key = jax.random.key(seed)
        ks = jax.random.split(key, 16)
        sd = 1.0 / np.sqrt(D)
        sf = 1.0 / np.sqrt(F)
        return {'x': jax.random.normal(ks[0], (B, S, D), jnp.float32), 'gate_w': jax.random.normal(ks[1], (E, D), jnp.float32) * sd, 'gate_b': jax.random.normal(ks[2], (E,), jnp.float32) * 0.01, 'w1': jax.random.normal(ks[3], (E, 2 * F, D), jnp.float32) * sd, 'b1': jax.random.normal(ks[4], (E, 2 * F), jnp.float32) * 0.01, 'w3': jax.random.normal(ks[5], (E, 2 * F, D), jnp.float32) * sd, 'b3': jax.random.normal(ks[6], (E, 2 * F), jnp.float32) * 0.01, 'w2': jax.random.normal(ks[7], (E, D, F), jnp.float32) * sf, 'b2': jax.random.normal(ks[8], (E, D), jnp.float32) * 0.01, 'sw1': jax.random.normal(ks[9], (2 * F, D), jnp.float32) * sd, 'sb1': jax.random.normal(ks[10], (2 * F,), jnp.float32) * 0.01, 'sw3': jax.random.normal(ks[11], (2 * F, D), jnp.float32) * sd, 'sb3': jax.random.normal(ks[12], (2 * F,), jnp.float32) * 0.01, 'sw2': jax.random.normal(ks[13], (D, F), jnp.float32) * sf, 'sb2': jax.random.normal(ks[14], (D,), jnp.float32) * 0.01}
    _L2_ffn_all = _L2_ffn_setup()
    _L2_ffn_in = {k: v for k, v in _L2_ffn_all.items() if k in ('gate_w', 'gate_b', 'w1', 'b1', 'w3', 'b3', 'w2', 'b2', 'sw1', 'sb1', 'sw3', 'sb3', 'sw2', 'sb2')}
    del _L2_ffn_all

    def _L3_xattn_setup():
        import jax, jax.numpy as jnp
        import numpy as np
        DIM, DIM_HEAD, HEADS, SCALE = (256, 64, 8, 8.0)
        INNER = DIM_HEAD * HEADS
        LN_EPS = 1e-05
        L2_EPS = 1e-12

        def layer_norm(x, w, b):
            mu = jnp.mean(x, axis=-1, keepdims=True)
            var = jnp.mean(jnp.square(x - mu), axis=-1, keepdims=True)
            return (x - mu) * jax.lax.rsqrt(var + LN_EPS) * w + b

        def l2norm(t):
            n = jnp.sqrt(jnp.sum(jnp.square(t), axis=-1, keepdims=True))
            return t / jnp.maximum(n, L2_EPS)
        key = jax.random.key(seed)
        ks = jax.random.split(key, 8)
        b, n, m = (8, 2048, 64)
        x = jax.random.normal(ks[0], (b, n, DIM), dtype=jnp.float32)
        latents = jax.random.normal(ks[1], (b, m, DIM), dtype=jnp.float32)
        mask = jax.random.randint(ks[2], (b, n), 0, 2) > 0
        Wq = jax.random.normal(ks[3], (DIM, INNER), dtype=jnp.float32) * DIM ** (-0.5)
        Wkv = jax.random.normal(ks[4], (DIM, 2 * INNER), dtype=jnp.float32) * DIM ** (-0.5)
        Wo = jax.random.normal(ks[5], (INNER, DIM), dtype=jnp.float32) * INNER ** (-0.5)
        return {'x': x, 'latents': latents, 'mask': mask, 'ln_x_w': jnp.ones((DIM,)), 'ln_x_b': jnp.zeros((DIM,)), 'ln_l_w': jnp.ones((DIM,)), 'ln_l_b': jnp.zeros((DIM,)), 'Wq': Wq, 'Wkv': Wkv, 'q_scale': jnp.ones((DIM_HEAD,)), 'k_scale': jnp.ones((DIM_HEAD,)), 'Wo': Wo, 'ln_o_w': jnp.ones((DIM,)), 'ln_o_b': jnp.zeros((DIM,))}
    _L3_xattn_all = _L3_xattn_setup()
    _L3_xattn_in = {k: v for k, v in _L3_xattn_all.items() if k in ('ln_x_w', 'ln_x_b', 'ln_l_w', 'ln_l_b', 'Wq', 'Wkv', 'q_scale', 'k_scale', 'Wo', 'ln_o_w', 'ln_o_b')}
    del _L3_xattn_all

    def _L3_attn_setup():
        import math
        import jax, jax.numpy as jnp
        import numpy as np
        B, T, E, H, L = (2, 512, 256, 16, 256)
        key = jax.random.key(seed)
        ks = jax.random.split(key, 11)
        w = lambda k, shape: jax.random.normal(k, shape, jnp.float32) * 0.02
        return {'x': jax.random.normal(ks[0], (B, T, E), jnp.float32), 'Wq': w(ks[1], (E, E)), 'bq': jnp.zeros((E,), jnp.float32), 'Wk': w(ks[2], (E, E)), 'bk': jnp.zeros((E,), jnp.float32), 'Wv': w(ks[3], (E, E)), 'bv': jnp.zeros((E,), jnp.float32), 'Wl': w(ks[4], (E, L)), 'bl': jnp.zeros((L,), jnp.float32), 'Wo': w(ks[5], (L, E)), 'bo': jnp.zeros((E,), jnp.float32)}
    _L3_attn_all = _L3_attn_setup()
    _L3_attn_in = {k: v for k, v in _L3_attn_all.items() if k in ('Wq', 'bq', 'Wk', 'bk', 'Wv', 'bv', 'Wl', 'bl', 'Wo', 'bo')}
    del _L3_attn_all

    def _L3_ffn_setup():
        import jax, jax.numpy as jnp
        import numpy as np
        DIM = 256
        NUM_EXPERTS = 8
        HIDDEN = 1024
        CAP_FACTOR = 2.0
        B, S = (4, 512)
        key = jax.random.key(seed)
        ks = jax.random.split(key, 6)
        scale_r = 1.0 / np.sqrt(DIM)
        scale_1 = 1.0 / np.sqrt(DIM)
        scale_2 = 1.0 / np.sqrt(HIDDEN)
        return {'x': jax.random.normal(ks[0], (B, S, DIM), dtype=jnp.float32), 'router_w': jax.random.uniform(ks[1], (NUM_EXPERTS, DIM), jnp.float32, -scale_r, scale_r), 'w1': jax.random.uniform(ks[2], (NUM_EXPERTS, DIM, HIDDEN), jnp.float32, -scale_1, scale_1), 'b1': jax.random.uniform(ks[3], (NUM_EXPERTS, HIDDEN), jnp.float32, -scale_1, scale_1), 'w2': jax.random.uniform(ks[4], (NUM_EXPERTS, HIDDEN, DIM), jnp.float32, -scale_2, scale_2), 'b2': jax.random.uniform(ks[5], (NUM_EXPERTS, DIM), jnp.float32, -scale_2, scale_2)}
    _L3_ffn_all = _L3_ffn_setup()
    _L3_ffn_in = {k: v for k, v in _L3_ffn_all.items() if k in ('router_w', 'w1', 'b1', 'w2', 'b2')}
    del _L3_ffn_all
    return {'x': x, 'ctx_1024': ctx_1024, 'itok_BxS_0_255': itok_BxS_0_255, 'mask_BxS2_ik1': mask_BxS2_ik1, 'mask_BxS2_bk0': mask_BxS2_bk0, 'L0_xattn_Wq': _L0_xattn_in['Wq'], 'L0_xattn_Wk': _L0_xattn_in['Wk'], 'L0_xattn_Wv': _L0_xattn_in['Wv'], 'L0_xattn_Wo': _L0_xattn_in['Wo'], 'L0_attn_w_in': _L0_attn_in['w_in'], 'L0_attn_w_conv': _L0_attn_in['w_conv'], 'L0_attn_w_xproj': _L0_attn_in['w_xproj'], 'L0_attn_w_dt': _L0_attn_in['w_dt'], 'L0_attn_b_dt': _L0_attn_in['b_dt'], 'L0_attn_A_log': _L0_attn_in['A_log'], 'L0_attn_D': _L0_attn_in['D'], 'L0_attn_w_out': _L0_attn_in['w_out'], 'L0_ffn_gate_w': _L0_ffn_in['gate_w'], 'L0_ffn_gate_bias': _L0_ffn_in['gate_bias'], 'L0_ffn_Wu': _L0_ffn_in['Wu'], 'L0_ffn_bu': _L0_ffn_in['bu'], 'L0_ffn_Wd': _L0_ffn_in['Wd'], 'L0_ffn_bd': _L0_ffn_in['bd'], 'L0_ffn_sWu': _L0_ffn_in['sWu'], 'L0_ffn_sbu': _L0_ffn_in['sbu'], 'L0_ffn_sWd': _L0_ffn_in['sWd'], 'L0_ffn_sbd': _L0_ffn_in['sbd'], 'L1_xattn_Wk': _L1_xattn_in['Wk'], 'L1_xattn_Wv': _L1_xattn_in['Wv'], 'L1_xattn_bv': _L1_xattn_in['bv'], 'L1_xattn_Wq': _L1_xattn_in['Wq'], 'L1_xattn_bq': _L1_xattn_in['bq'], 'L1_xattn_Wo': _L1_xattn_in['Wo'], 'L1_xattn_bo': _L1_xattn_in['bo'], 'L1_attn_w_q': _L1_attn_in['w_q'], 'L1_attn_w_k': _L1_attn_in['w_k'], 'L1_attn_w_v': _L1_attn_in['w_v'], 'L1_attn_w_o': _L1_attn_in['w_o'], 'L1_ffn_w1_w': _L1_ffn_in['w1_w'], 'L1_ffn_w1_s': _L1_ffn_in['w1_s'], 'L1_ffn_w2_w': _L1_ffn_in['w2_w'], 'L1_ffn_w2_s': _L1_ffn_in['w2_s'], 'L1_ffn_h1_w': _L1_ffn_in['h1_w'], 'L1_ffn_h1_s': _L1_ffn_in['h1_s'], 'L1_ffn_h2_w': _L1_ffn_in['h2_w'], 'L1_ffn_h2_s': _L1_ffn_in['h2_s'], 'L1_ffn_w3_w': _L1_ffn_in['w3_w'], 'L1_ffn_w3_s': _L1_ffn_in['w3_s'], 'L2_xattn_Wqkv': _L2_xattn_in['Wqkv'], 'L2_xattn_bqkv': _L2_xattn_in['bqkv'], 'L2_xattn_Wo': _L2_xattn_in['Wo'], 'L2_xattn_bo': _L2_xattn_in['bo'], 'L2_xattn_Wq_c': _L2_xattn_in['Wq_c'], 'L2_xattn_Wkv_c': _L2_xattn_in['Wkv_c'], 'L2_xattn_Wo_c': _L2_xattn_in['Wo_c'], 'L2_xattn_Wg': _L2_xattn_in['Wg'], 'L2_xattn_Wu': _L2_xattn_in['Wu'], 'L2_xattn_Wd': _L2_xattn_in['Wd'], 'L2_xattn_n1': _L2_xattn_in['n1'], 'L2_xattn_n2': _L2_xattn_in['n2'], 'L2_xattn_n3': _L2_xattn_in['n3'], 'L2_xattn_nf': _L2_xattn_in['nf'], 'L2_attn_q_w': _L2_attn_in['q_w'], 'L2_attn_q_b': _L2_attn_in['q_b'], 'L2_attn_k_w': _L2_attn_in['k_w'], 'L2_attn_k_b': _L2_attn_in['k_b'], 'L2_attn_v_w': _L2_attn_in['v_w'], 'L2_attn_v_b': _L2_attn_in['v_b'], 'L2_attn_out_w': _L2_attn_in['out_w'], 'L2_attn_out_b': _L2_attn_in['out_b'], 'L2_attn_rel_emb': _L2_attn_in['rel_emb'], 'L2_attn_grep_w': _L2_attn_in['grep_w'], 'L2_attn_grep_b': _L2_attn_in['grep_b'], 'L2_attn_grep_a': _L2_attn_in['grep_a'], 'L2_attn_bias_k': _L2_attn_in['bias_k'], 'L2_attn_bias_v': _L2_attn_in['bias_v'], 'L2_ffn_gate_w': _L2_ffn_in['gate_w'], 'L2_ffn_gate_b': _L2_ffn_in['gate_b'], 'L2_ffn_w1': _L2_ffn_in['w1'], 'L2_ffn_b1': _L2_ffn_in['b1'], 'L2_ffn_w3': _L2_ffn_in['w3'], 'L2_ffn_b3': _L2_ffn_in['b3'], 'L2_ffn_w2': _L2_ffn_in['w2'], 'L2_ffn_b2': _L2_ffn_in['b2'], 'L2_ffn_sw1': _L2_ffn_in['sw1'], 'L2_ffn_sb1': _L2_ffn_in['sb1'], 'L2_ffn_sw3': _L2_ffn_in['sw3'], 'L2_ffn_sb3': _L2_ffn_in['sb3'], 'L2_ffn_sw2': _L2_ffn_in['sw2'], 'L2_ffn_sb2': _L2_ffn_in['sb2'], 'L3_xattn_ln_x_w': _L3_xattn_in['ln_x_w'], 'L3_xattn_ln_x_b': _L3_xattn_in['ln_x_b'], 'L3_xattn_ln_l_w': _L3_xattn_in['ln_l_w'], 'L3_xattn_ln_l_b': _L3_xattn_in['ln_l_b'], 'L3_xattn_Wq': _L3_xattn_in['Wq'], 'L3_xattn_Wkv': _L3_xattn_in['Wkv'], 'L3_xattn_q_scale': _L3_xattn_in['q_scale'], 'L3_xattn_k_scale': _L3_xattn_in['k_scale'], 'L3_xattn_Wo': _L3_xattn_in['Wo'], 'L3_xattn_ln_o_w': _L3_xattn_in['ln_o_w'], 'L3_xattn_ln_o_b': _L3_xattn_in['ln_o_b'], 'L3_attn_Wq': _L3_attn_in['Wq'], 'L3_attn_bq': _L3_attn_in['bq'], 'L3_attn_Wk': _L3_attn_in['Wk'], 'L3_attn_bk': _L3_attn_in['bk'], 'L3_attn_Wv': _L3_attn_in['Wv'], 'L3_attn_bv': _L3_attn_in['bv'], 'L3_attn_Wl': _L3_attn_in['Wl'], 'L3_attn_bl': _L3_attn_in['bl'], 'L3_attn_Wo': _L3_attn_in['Wo'], 'L3_attn_bo': _L3_attn_in['bo'], 'L3_ffn_router_w': _L3_ffn_in['router_w'], 'L3_ffn_w1': _L3_ffn_in['w1'], 'L3_ffn_b1': _L3_ffn_in['b1'], 'L3_ffn_w2': _L3_ffn_in['w2'], 'L3_ffn_b2': _L3_ffn_in['b2']}

def reference(x, ctx_1024, itok_BxS_0_255, mask_BxS2_ik1, mask_BxS2_bk0, L0_xattn_Wq, L0_xattn_Wk, L0_xattn_Wv, L0_xattn_Wo, L0_attn_w_in, L0_attn_w_conv, L0_attn_w_xproj, L0_attn_w_dt, L0_attn_b_dt, L0_attn_A_log, L0_attn_D, L0_attn_w_out, L0_ffn_gate_w, L0_ffn_gate_bias, L0_ffn_Wu, L0_ffn_bu, L0_ffn_Wd, L0_ffn_bd, L0_ffn_sWu, L0_ffn_sbu, L0_ffn_sWd, L0_ffn_sbd, L1_xattn_Wk, L1_xattn_Wv, L1_xattn_bv, L1_xattn_Wq, L1_xattn_bq, L1_xattn_Wo, L1_xattn_bo, L1_attn_w_q, L1_attn_w_k, L1_attn_w_v, L1_attn_w_o, L1_ffn_w1_w, L1_ffn_w1_s, L1_ffn_w2_w, L1_ffn_w2_s, L1_ffn_h1_w, L1_ffn_h1_s, L1_ffn_h2_w, L1_ffn_h2_s, L1_ffn_w3_w, L1_ffn_w3_s, L2_xattn_Wqkv, L2_xattn_bqkv, L2_xattn_Wo, L2_xattn_bo, L2_xattn_Wq_c, L2_xattn_Wkv_c, L2_xattn_Wo_c, L2_xattn_Wg, L2_xattn_Wu, L2_xattn_Wd, L2_xattn_n1, L2_xattn_n2, L2_xattn_n3, L2_xattn_nf, L2_attn_q_w, L2_attn_q_b, L2_attn_k_w, L2_attn_k_b, L2_attn_v_w, L2_attn_v_b, L2_attn_out_w, L2_attn_out_b, L2_attn_rel_emb, L2_attn_grep_w, L2_attn_grep_b, L2_attn_grep_a, L2_attn_bias_k, L2_attn_bias_v, L2_ffn_gate_w, L2_ffn_gate_b, L2_ffn_w1, L2_ffn_b1, L2_ffn_w3, L2_ffn_b3, L2_ffn_w2, L2_ffn_b2, L2_ffn_sw1, L2_ffn_sb1, L2_ffn_sw3, L2_ffn_sb3, L2_ffn_sw2, L2_ffn_sb2, L3_xattn_ln_x_w, L3_xattn_ln_x_b, L3_xattn_ln_l_w, L3_xattn_ln_l_b, L3_xattn_Wq, L3_xattn_Wkv, L3_xattn_q_scale, L3_xattn_k_scale, L3_xattn_Wo, L3_xattn_ln_o_w, L3_xattn_ln_o_b, L3_attn_Wq, L3_attn_bq, L3_attn_Wk, L3_attn_bk, L3_attn_Wv, L3_attn_bv, L3_attn_Wl, L3_attn_bl, L3_attn_Wo, L3_attn_bo, L3_ffn_router_w, L3_ffn_w1, L3_ffn_b1, L3_ffn_w2, L3_ffn_b2):
    import jax
    import jax.numpy as jnp

    def _L0_xattn_ref(query, key, value, Wq, Wk, Wv, Wo, attention_mask):
        import jax, jax.numpy as jnp
        import numpy as np
        EMBED_DIM = 256
        NUM_HEADS = 16
        HEAD_DIM = EMBED_DIM // NUM_HEADS
        B, Sq, D = query.shape
        Sk = key.shape[1]
        H, hd = (NUM_HEADS, HEAD_DIM)
        q = (query @ Wq).reshape(B, Sq, H, hd).transpose(0, 2, 1, 3)
        k = (key @ Wk).reshape(B, Sk, H, hd).transpose(0, 2, 1, 3)
        v = (value @ Wv).reshape(B, Sk, H, hd).transpose(0, 2, 1, 3)
        scores = jnp.einsum('bhqd,bhkd->bhqk', q, k) / jnp.sqrt(jnp.float32(hd))
        mask = attention_mask[:, None, None, :]
        scores = jnp.where(mask == 0, -jnp.inf, scores)
        weights = jax.nn.softmax(scores, axis=-1)
        out = jnp.einsum('bhqk,bhkd->bhqd', weights, v)
        out = out.transpose(0, 2, 1, 3).reshape(B, Sq, D)
        return out @ Wo

    def _L0_attn_ref(hidden_states, w_in, w_conv, w_xproj, w_dt, b_dt, A_log, D, w_out):
        import jax, jax.numpy as jnp
        import numpy as np
        from functools import partial
        B_, L_, H_, DIN_, K_, N_, R_ = (2, 512, 256, 512, 4, 16, 64)

        def _selective_scan(x, delta, A, Bm, Cm, D):
            dA = jnp.exp(jnp.einsum('bld,dn->bldn', delta, A))
            dBx = jnp.einsum('bld,bln->bldn', delta * x, Bm)
            b, l, d, n = dA.shape

            def step(z, inp):
                dA_t, dBx_t, c_t = inp
                z = dA_t * z + dBx_t
                y = jnp.einsum('bdn,bn->bd', z, c_t)
                return (z, y)
            z0 = jnp.zeros((b, d, n), x.dtype)
            _, ys = jax.lax.scan(step, z0, (jnp.moveaxis(dA, 1, 0), jnp.moveaxis(dBx, 1, 0), jnp.moveaxis(Cm, 1, 0)))
            y = jnp.moveaxis(ys, 0, 1)
            return y + x * D
        b, l, h = hidden_states.shape
        d_in, n = A_log.shape
        hs_res = hidden_states @ w_in.T
        hs, res = (hs_res[..., :d_in], hs_res[..., d_in:])
        xc = jnp.moveaxis(hs, 1, 2)
        xc = jax.lax.conv_general_dilated(xc, w_conv, window_strides=(1,), padding=[(K_ - 1, 0)], dimension_numbers=('NCH', 'OIH', 'NCH'), feature_group_count=d_in)
        hs = jax.nn.silu(jnp.moveaxis(xc, 1, 2))
        A = -jnp.exp(A_log)
        x_dbl = hs @ w_xproj.T
        dt, Bm, Cm = (x_dbl[..., :R_], x_dbl[..., R_:R_ + n], x_dbl[..., R_ + n:])
        delta = jax.nn.softplus(dt @ w_dt.T + b_dt)
        y = _selective_scan(hs, delta, A, Bm, Cm, D)
        y = y * jax.nn.silu(res)
        return y @ w_out.T

    def _L0_ffn_ref(x, gate_w, gate_bias, Wu, bu, Wd, bd, sWu, sbu, sWd, sbd):
        import jax, jax.numpy as jnp
        import numpy as np
        B, S, H, E, K = (2, 256, 256, 8, 2)
        F = 4 * H
        b, s, h = x.shape
        x_flat = x.reshape(-1, h)
        T = x_flat.shape[0]
        scores = jax.nn.sigmoid(x_flat @ gate_w.T + gate_bias)
        top_scores, top_idx = jax.lax.top_k(scores, K)
        top_scores = top_scores / (top_scores.sum(-1, keepdims=True) + 1e-06)
        w = jnp.zeros((T, E), x.dtype).at[jnp.arange(T)[:, None], top_idx].add(top_scores)
        h1 = jnp.einsum('th,efh->etf', x_flat, Wu) + bu[:, None, :]
        a1 = jax.nn.gelu(h1, approximate=False)
        y = jnp.einsum('etf,ehf->eth', a1, Wd) + bd[:, None, :]
        combined = jnp.einsum('te,eth->th', w, y)
        sh = jax.nn.gelu(x_flat @ sWu.T + sbu, approximate=False)
        shared = (sh @ sWd.T + sbd) * 0.1
        return (combined + shared).reshape(b, s, h)

    def _L1_xattn_ref(k, v, q, Wk, Wv, bv, Wq, bq, Wo, bo):
        import jax, jax.numpy as jnp
        import numpy as np
        D_MODEL = 256
        B, S = (4, 512)
        kp = jnp.einsum('bsd,ed->bse', k, Wk)
        vp = jnp.einsum('bsd,ed->bse', v, Wv) + bv
        qp = jnp.einsum('bsd,ed->bse', q, Wq) + bq
        scale = 1.0 / jnp.sqrt(jnp.float32(kp.shape[-1]))
        scores = jnp.einsum('bqd,bkd->bqk', qp, kp) * scale
        probs = jax.nn.softmax(scores, axis=-1)
        ctx = jnp.einsum('bqk,bkd->bqd', probs, vp)
        return jnp.einsum('bqd,ed->bqe', ctx, Wo) + bo

    def _L1_attn_ref(x, w_q, w_k, w_v, w_o):
        import jax, jax.numpy as jnp
        import numpy as np
        D_K, D_MODEL, NUM_HEADS = (64, 256, 16)

        def _xavier(key, shape):
            fan_in, fan_out = (shape[-2], shape[-1])
            limit = float(np.sqrt(6.0 / (fan_in + fan_out)))
            return jax.random.uniform(key, shape, jnp.float32, -limit, limit)
        scale = 1.0 / jnp.sqrt(jnp.asarray(D_K, dtype=jnp.float32))
        q = jnp.einsum('bsd,hdk->bhsk', x, w_q)
        k = jnp.einsum('bsd,hdk->bhsk', x, w_k)
        v = jnp.einsum('bsd,hdk->bhsk', x, w_v)
        scores = jnp.einsum('bhqk,bhmk->bhqm', q, k) * scale
        weights = jax.nn.softmax(scores, axis=-1)
        z = jnp.einsum('bhqm,bhmk->bhqk', weights, v)
        b, h, s, dk = z.shape
        z = jnp.transpose(z, (0, 2, 1, 3)).reshape(b, s, h * dk)
        z = jnp.einsum('bse,ed->bsd', z, w_o)
        return x + z

    def _L1_ffn_ref(x, w1_w, w1_s, w2_w, w2_s, h1_w, h1_s, h2_w, h2_s, w3_w, w3_s):
        import jax, jax.numpy as jnp
        import numpy as np
        D_IN, D_HID = (256, 1024)

        def _ternary(key, shape):
            return jax.random.randint(key, shape, -1, 2).astype(jnp.float32)

        def _tlin(x, w, s):
            return jnp.einsum('bsi,oi->bso', x, w) * s
        h = jax.nn.silu(_tlin(x, w1_w, w1_s)) * _tlin(x, w2_w, w2_s)
        h = jax.nn.gelu(_tlin(h, h1_w, h1_s), approximate=False)
        h = jax.nn.gelu(_tlin(h, h2_w, h2_s), approximate=False)
        return _tlin(h, w3_w, w3_s)

    def _L2_xattn_ref(x, memory, seg_ids, Wqkv, bqkv, Wo, bo, Wq_c, Wkv_c, Wo_c, Wg, Wu, Wd, n1, n2, n3, nf):
        import jax, jax.numpy as jnp
        import numpy as np
        N_LAYERS = 4
        H = 16
        LOOKBACK = 128
        EPS = 1e-06
        ROPE_BASE = 10000.0
        NEG = jnp.float32(-1e+30)

        def rmsnorm(x, w):
            return x * jax.lax.rsqrt(jnp.mean(x * x, axis=-1, keepdims=True) + EPS) * w

        def rope_cache(L, hd):
            inv = 1.0 / ROPE_BASE ** (jnp.arange(0, hd, 2, dtype=jnp.float32) / hd)
            t = jnp.arange(L, dtype=jnp.float32)
            f = t[:, None] * inv[None, :]
            emb = jnp.concatenate([f, f], axis=-1)
            return (jnp.cos(emb), jnp.sin(emb))

        def apply_rope(x, cos, sin):
            d = x.shape[-1]
            x1, x2 = (x[..., :d // 2], x[..., d // 2:])
            rot = jnp.concatenate([-x2, x1], axis=-1)
            return x * cos + rot * sin

        def split_heads(x, n_heads):
            B, L, D = x.shape
            return x.reshape(B, L, n_heads, D // n_heads).transpose(0, 2, 1, 3)

        def merge_heads(x):
            B, h, L, d = x.shape
            return x.transpose(0, 2, 1, 3).reshape(B, L, h * d)

        def sdpa(q, k, v, bias):
            scale = q.shape[-1] ** (-0.5)
            s = jnp.einsum('bhqd,bhkd->bhqk', q, k) * scale + bias
            p = jax.nn.softmax(s, axis=-1)
            return jnp.einsum('bhqk,bhkd->bhqd', p, v)

        def forward(x, memory, seg_ids, Wqkv, bqkv, Wo, bo, Wq_c, Wkv_c, Wo_c, Wg, Wu, Wd, n1, n2, n3, nf):
            B, L, D = x.shape
            S = memory.shape[1]
            hd = D // H
            cos, sin = rope_cache(L, hd)
            i = jnp.arange(L)
            causal_bias = jnp.where(i[None, :] <= i[:, None], 0.0, NEG)[None, None]
            j = jnp.arange(S)
            allowed = (j[None, None, :] <= seg_ids[:, :, None]) & (j[None, None, :] > seg_ids[:, :, None] - LOOKBACK)
            cross_bias = jnp.where(allowed, 0.0, NEG)[:, None]
            for l in range(N_LAYERS):
                h = rmsnorm(x, n1[l])
                qkv = h @ Wqkv[l].T + bqkv[l]
                q, k, v = jnp.split(qkv, 3, axis=-1)
                q = apply_rope(split_heads(q, H), cos, sin)
                k = apply_rope(split_heads(k, H), cos, sin)
                v = split_heads(v, H)
                o = merge_heads(sdpa(q, k, v, causal_bias)) @ Wo[l].T + bo[l]
                x = x + o
                h2 = rmsnorm(x, n2[l])
                qc = split_heads(h2 @ Wq_c[l].T, H)
                kv = memory @ Wkv_c[l].T
                kc, vc = jnp.split(kv, 2, axis=-1)
                kc, vc = (split_heads(kc, H), split_heads(vc, H))
                oc = merge_heads(sdpa(qc, kc, vc, cross_bias)) @ Wo_c[l].T
                x = x + oc
                h3 = rmsnorm(x, n3[l])
                x = x + jax.nn.silu(h3 @ Wg[l].T) * (h3 @ Wu[l].T) @ Wd[l].T
            return rmsnorm(x, nf)
        return forward(x, memory, seg_ids, Wqkv, bqkv, Wo, bo, Wq_c, Wkv_c, Wo_c, Wg, Wu, Wd, n1, n2, n3, nf)

    def _L2_attn_ref(query, q_w, q_b, k_w, k_b, v_w, v_b, out_w, out_b, rel_emb, grep_w, grep_b, grep_a, bias_k, bias_v):
        import jax, jax.numpy as jnp
        import numpy as np
        import math
        NUM_HEADS = 16
        NUM_BUCKETS = 32
        MAX_DISTANCE = 128
        ALPHA = 32.0

        def _rel_bucket(rel_pos):
            nb = NUM_BUCKETS // 2
            buckets = (rel_pos > 0).astype(jnp.int32) * nb
            rel_pos = jnp.abs(rel_pos)
            max_exact = nb // 2
            is_small = rel_pos < max_exact
            large = max_exact + (jnp.log(rel_pos.astype(jnp.float32) / max_exact + 1e-06) / math.log(MAX_DISTANCE / max_exact) * (nb - max_exact)).astype(jnp.int32)
            large = jnp.minimum(large, nb - 1)
            return buckets + jnp.where(is_small, rel_pos, large)
        tgt_len, bsz, embed_dim = query.shape
        nh = NUM_HEADS
        hd = embed_dim // nh
        scaling = hd ** (-0.5)
        q = query @ q_w + q_b
        k = query @ k_w + k_b
        v = query @ v_w + v_b
        q = q * scaling / ALPHA
        k = jnp.concatenate([k, jnp.tile(bias_k, (1, bsz, 1))], axis=0)
        v = jnp.concatenate([v, jnp.tile(bias_v, (1, bsz, 1))], axis=0)
        q = jnp.transpose(q.reshape(tgt_len, bsz, nh, hd), (1, 0, 2, 3)).reshape(bsz * nh, tgt_len, hd)
        k = jnp.transpose(k.reshape(-1, bsz, nh, hd), (1, 0, 2, 3)).reshape(bsz * nh, -1, hd)
        v = jnp.transpose(v.reshape(-1, bsz, nh, hd), (1, 0, 2, 3)).reshape(bsz * nh, -1, hd)
        src_len = k.shape[1]
        attn_weights = jnp.einsum('bth,bsh->bts', q, k)
        rel_pos = jnp.arange(src_len)[None, :] - jnp.arange(tgt_len)[:, None]
        buckets = _rel_bucket(rel_pos)
        pb = rel_emb[buckets]
        pb = jnp.transpose(pb, (2, 0, 1))
        pb = jnp.tile(pb[None], (bsz, 1, 1, 1)).reshape(bsz * nh, tgt_len, src_len)
        query_layer = q.reshape(bsz, nh, tgt_len, hd) * ALPHA / scaling
        gate = jax.nn.sigmoid((query_layer @ grep_w + grep_b).sum(-1, keepdims=True))
        gate = (gate * grep_a).reshape(bsz * nh, tgt_len, 1)
        attn_weights = attn_weights + gate * pb
        probs = jax.nn.softmax(attn_weights, axis=-1)
        attn = jnp.einsum('bts,bsh->bth', probs, v)
        attn = attn.reshape(bsz, nh, tgt_len, hd)
        attn = jnp.transpose(attn, (2, 0, 1, 3)).reshape(tgt_len, bsz, embed_dim)
        return attn @ out_w + out_b

    def _L2_ffn_ref(x, gate_w, gate_b, w1, b1, w3, b3, w2, b2, sw1, sb1, sw3, sb3, sw2, sb2):
        import jax, jax.numpy as jnp
        import numpy as np
        E = 8
        TOP_K = 2
        ROUTE_SCALE = 1.0
        ALPHA = 1.702
        LIMIT = 7.0
        D = 256
        F = 256
        B, S = (2, 256)

        def swiglu(h):
            g = jnp.minimum(h[..., ::2], LIMIT)
            l = jnp.clip(h[..., 1::2], -LIMIT, LIMIT)
            return g * jax.nn.sigmoid(ALPHA * g) * (l + 1.0)
        if __name__ == '__main__':
            out = reference(**setup_inputs())
            print(out.shape, out.dtype)
        inp_shape = x.shape
        xt = x.reshape(-1, D)
        logits = xt @ gate_w.T
        scores = jax.nn.softmax(logits.astype(jnp.float32), axis=-1)
        biased = scores + gate_b.astype(jnp.float32)
        idx = jax.lax.top_k(biased, TOP_K)[1]
        weights = (jnp.take_along_axis(scores, idx, axis=-1) * ROUTE_SCALE).astype(x.dtype)
        cw = jnp.sum(jax.nn.one_hot(idx, E, dtype=x.dtype) * weights[..., None], axis=1)
        h1 = jnp.einsum('td,efd->etf', xt, w1) + b1[:, None, :]
        h3 = jnp.einsum('td,efd->etf', xt, w3) + b3[:, None, :]
        a = swiglu(h1 * h3)
        y = jnp.einsum('etf,edf->etd', a, w2) + b2[:, None, :]
        routed = jnp.einsum('te,etd->td', cw, y)
        sh = swiglu((xt @ sw1.T + sb1) * (xt @ sw3.T + sb3))
        shared = sh @ sw2.T + sb2
        return (routed + shared).reshape(inp_shape)

    def _L3_xattn_ref(x, latents, mask, ln_x_w, ln_x_b, ln_l_w, ln_l_b, Wq, Wkv, q_scale, k_scale, Wo, ln_o_w, ln_o_b):
        import jax, jax.numpy as jnp
        import numpy as np
        DIM, DIM_HEAD, HEADS, SCALE = (256, 64, 8, 8.0)
        INNER = DIM_HEAD * HEADS
        LN_EPS = 1e-05
        L2_EPS = 1e-12

        def layer_norm(x, w, b):
            mu = jnp.mean(x, axis=-1, keepdims=True)
            var = jnp.mean(jnp.square(x - mu), axis=-1, keepdims=True)
            return (x - mu) * jax.lax.rsqrt(var + LN_EPS) * w + b

        def l2norm(t):
            n = jnp.sqrt(jnp.sum(jnp.square(t), axis=-1, keepdims=True))
            return t / jnp.maximum(n, L2_EPS)
        b, n, _ = x.shape
        m = latents.shape[1]
        x = layer_norm(x, ln_x_w, ln_x_b)
        latents = layer_norm(latents, ln_l_w, ln_l_b)
        q = latents @ Wq
        kv_input = jnp.concatenate([x, latents], axis=1)
        kv = kv_input @ Wkv
        k, v = jnp.split(kv, 2, axis=-1)

        def to_heads(t):
            return t.reshape(t.shape[0], t.shape[1], HEADS, DIM_HEAD).transpose(0, 2, 1, 3)
        q, k, v = map(to_heads, (q, k, v))
        q = l2norm(q) * q_scale
        k = l2norm(k) * k_scale
        sim = jnp.einsum('bhid,bhjd->bhij', q, k) * SCALE
        full_mask = jnp.concatenate([mask, jnp.ones((b, m), dtype=bool)], axis=1)[:, None, None, :]
        max_neg = -jnp.finfo(sim.dtype).max
        sim = jnp.where(full_mask, sim, max_neg)
        attn = jax.nn.softmax(sim.astype(jnp.float32), axis=-1).astype(sim.dtype)
        out = jnp.einsum('bhij,bhjd->bhid', attn, v)
        out = out.transpose(0, 2, 1, 3).reshape(b, m, INNER)
        return layer_norm(out @ Wo, ln_o_w, ln_o_b)

    def _L3_attn_ref(x, Wq, bq, Wk, bk, Wv, bv, Wl, bl, Wo, bo):
        import math
        import jax, jax.numpy as jnp
        import numpy as np
        B, T, E, H, L = (2, 512, 256, 16, 256)
        b, t, e = x.shape
        hd = e // H
        lhd = L // H
        scale = 1.0 / math.sqrt(hd)
        q = (x @ Wq + bq).reshape(b, t, H, hd).transpose(0, 2, 1, 3)
        k = ((x @ Wk + bk) @ Wl + bl).reshape(b, t, H, lhd).transpose(0, 2, 1, 3)
        v = ((x @ Wv + bv) @ Wl + bl).reshape(b, t, H, lhd).transpose(0, 2, 1, 3)
        attn = jax.nn.softmax(jnp.einsum('bhqd,bhkd->bhqk', q, k) * scale, axis=-1)
        out = jnp.einsum('bhqk,bhkd->bhqd', attn, v)
        out = out.transpose(0, 2, 1, 3).reshape(b, t, L)
        return out @ Wo + bo

    def _L3_ffn_ref(x, router_w, w1, b1, w2, b2):
        import jax, jax.numpy as jnp
        import numpy as np
        DIM = 256
        NUM_EXPERTS = 8
        HIDDEN = 1024
        CAP_FACTOR = 2.0
        B, S = (4, 512)
        Bz, Sz, Dz = x.shape
        E = router_w.shape[0]
        capacity = max(1, int(Sz * CAP_FACTOR / E) + 1)
        scores = jax.nn.softmax(jnp.einsum('bsd,ed->bse', x, router_w), axis=-1)
        scores_t = jnp.swapaxes(scores, 1, 2)
        gate_vals, sel_idx = jax.lax.top_k(scores_t, capacity)
        b_idx = jnp.arange(Bz)[:, None, None]
        tokens = x[b_idx, sel_idx]
        h = jnp.einsum('becd,edh->bech', tokens, w1) + b1[None, :, None, :]
        h = jax.nn.gelu(h, approximate=False)
        y = jnp.einsum('bech,ehd->becd', h, w2) + b2[None, :, None, :]
        gated = y * gate_vals[..., None]
        out = jnp.zeros_like(x).at[b_idx, sel_idx].add(gated)
        return out
    x = x + _L0_xattn_ref(_layernorm(x, axis=-1), ctx_1024, ctx_1024, L0_xattn_Wq, L0_xattn_Wk, L0_xattn_Wv, L0_xattn_Wo, mask_BxS2_ik1)
    x = x + _L0_attn_ref(_layernorm(x, axis=-1), L0_attn_w_in, L0_attn_w_conv, L0_attn_w_xproj, L0_attn_w_dt, L0_attn_b_dt, L0_attn_A_log, L0_attn_D, L0_attn_w_out)
    x = x + _L0_ffn_ref(_layernorm(x, axis=-1), L0_ffn_gate_w, L0_ffn_gate_bias, L0_ffn_Wu, L0_ffn_bu, L0_ffn_Wd, L0_ffn_bd, L0_ffn_sWu, L0_ffn_sbu, L0_ffn_sWd, L0_ffn_sbd)
    x = x + _L1_xattn_ref(ctx_1024, ctx_1024, _layernorm(x, axis=-1), L1_xattn_Wk, L1_xattn_Wv, L1_xattn_bv, L1_xattn_Wq, L1_xattn_bq, L1_xattn_Wo, L1_xattn_bo)
    x = x + _L1_attn_ref(_layernorm(x, axis=-1), L1_attn_w_q, L1_attn_w_k, L1_attn_w_v, L1_attn_w_o)
    x = x + _L1_ffn_ref(_layernorm(x, axis=-1), L1_ffn_w1_w, L1_ffn_w1_s, L1_ffn_w2_w, L1_ffn_w2_s, L1_ffn_h1_w, L1_ffn_h1_s, L1_ffn_h2_w, L1_ffn_h2_s, L1_ffn_w3_w, L1_ffn_w3_s)
    x = x + _L2_xattn_ref(_layernorm(x, axis=-1), ctx_1024, itok_BxS_0_255, L2_xattn_Wqkv, L2_xattn_bqkv, L2_xattn_Wo, L2_xattn_bo, L2_xattn_Wq_c, L2_xattn_Wkv_c, L2_xattn_Wo_c, L2_xattn_Wg, L2_xattn_Wu, L2_xattn_Wd, L2_xattn_n1, L2_xattn_n2, L2_xattn_n3, L2_xattn_nf)
    x = x + _L2_attn_ref(_layernorm(x, axis=-1), L2_attn_q_w, L2_attn_q_b, L2_attn_k_w, L2_attn_k_b, L2_attn_v_w, L2_attn_v_b, L2_attn_out_w, L2_attn_out_b, L2_attn_rel_emb, L2_attn_grep_w, L2_attn_grep_b, L2_attn_grep_a, L2_attn_bias_k, L2_attn_bias_v)
    x = x + _L2_ffn_ref(_layernorm(x, axis=-1), L2_ffn_gate_w, L2_ffn_gate_b, L2_ffn_w1, L2_ffn_b1, L2_ffn_w3, L2_ffn_b3, L2_ffn_w2, L2_ffn_b2, L2_ffn_sw1, L2_ffn_sb1, L2_ffn_sw3, L2_ffn_sb3, L2_ffn_sw2, L2_ffn_sb2)
    x = x + _L3_xattn_ref(ctx_1024, _layernorm(x, axis=-1), mask_BxS2_bk0, L3_xattn_ln_x_w, L3_xattn_ln_x_b, L3_xattn_ln_l_w, L3_xattn_ln_l_b, L3_xattn_Wq, L3_xattn_Wkv, L3_xattn_q_scale, L3_xattn_k_scale, L3_xattn_Wo, L3_xattn_ln_o_w, L3_xattn_ln_o_b)
    x = x + _L3_attn_ref(_layernorm(x, axis=-1), L3_attn_Wq, L3_attn_bq, L3_attn_Wk, L3_attn_bk, L3_attn_Wv, L3_attn_bv, L3_attn_Wl, L3_attn_bl, L3_attn_Wo, L3_attn_bo)
    x = x + _L3_ffn_ref(_layernorm(x, axis=-1), L3_ffn_router_w, L3_ffn_w1, L3_ffn_b1, L3_ffn_w2, L3_ffn_b2)
    return x

_drawn_inputs = setup_inputs


def setup_inputs(seed=0):
    import zlib

    import numpy as np

    out = dict(_drawn_inputs(seed))
    spreads = {'L0_attn_b_dt': (0.0, 0.1),
     'L0_attn_D': (1.0, 0.2),
     'L0_ffn_gate_bias': (0.0, 0.1),
     'L0_ffn_bu': (0.0, 0.1),
     'L0_ffn_bd': (0.0, 0.1),
     'L0_ffn_sbu': (0.0, 0.1),
     'L0_ffn_sbd': (0.0, 0.1),
     'L1_xattn_bv': (0.0, 0.1),
     'L1_xattn_bq': (0.0, 0.1),
     'L1_xattn_bo': (0.0, 0.1),
     'L2_xattn_bqkv': (0.0, 0.1),
     'L2_xattn_bo': (0.0, 0.1),
     'L2_xattn_n1': (1.0, 0.2),
     'L2_xattn_n2': (1.0, 0.2),
     'L2_xattn_n3': (1.0, 0.2),
     'L2_xattn_nf': (1.0, 0.2),
     'L2_attn_q_b': (0.0, 0.1),
     'L2_attn_k_b': (0.0, 0.1),
     'L2_attn_v_b': (0.0, 0.1),
     'L2_attn_out_b': (0.0, 0.1),
     'L2_attn_grep_b': (0.0, 0.1),
     'L2_attn_grep_a': (1.0, 0.2),
     'L3_xattn_ln_x_w': (1.0, 0.2),
     'L3_xattn_ln_x_b': (0.0, 0.1),
     'L3_xattn_ln_l_w': (1.0, 0.2),
     'L3_xattn_ln_l_b': (0.0, 0.1),
     'L3_xattn_q_scale': (1.0, 0.2),
     'L3_xattn_k_scale': (1.0, 0.2),
     'L3_xattn_ln_o_w': (1.0, 0.2),
     'L3_xattn_ln_o_b': (0.0, 0.1),
     'L3_attn_bq': (0.0, 0.1),
     'L3_attn_bk': (0.0, 0.1),
     'L3_attn_bv': (0.0, 0.1),
     'L3_attn_bl': (0.0, 0.1),
     'L3_attn_bo': (0.0, 0.1)}
    factors = {}
    for name, (base, spread) in spreads.items():
        noise = np.random.default_rng([zlib.crc32(name.encode()), seed]).standard_normal(out[name].shape)
        drawn = base * np.exp(spread * noise) if base else spread * noise
        out[name] = jnp.asarray(drawn.astype(out[name].dtype))
    for name, factor in factors.items():
        out[name] = (out[name] * factor).astype(out[name].dtype)
    return out
```

```python
from contextlib import ExitStack, contextmanager

import concourse.bass as bass
import numpy as np
from concourse import mybir

P = 128
D = 256
B = 2
S = 256
T = B * S
SK = 4096
KB = 256
F32 = mybir.dt.float32
ACT = mybir.ActivationFunctionType
ALU = mybir.AluOpType
AX = mybir.AxisListType.X
NEG = -1e30
START_MAX = -1e31

VECS = [("L0_attn_b_dt", 4), ("L0_attn_D", 4), ("L1_xattn_bv", 2), ("L1_xattn_bq", 2), ("L1_xattn_bo", 2),
        ("L1_ffn_w1_s", 8), ("L1_ffn_w2_s", 8), ("L1_ffn_h1_s", 8), ("L1_ffn_h2_s", 8), ("L1_ffn_w3_s", 2),
        ("L2_xattn_nf", 2), ("L2_attn_out_b", 2), ("L3_xattn_ln_x_w", 2), ("L3_xattn_ln_x_b", 2),
        ("L3_xattn_ln_l_w", 2), ("L3_xattn_ln_l_b", 2), ("q_scale2", 1), ("k_scale2", 1),
        ("L3_xattn_ln_o_w", 2), ("L3_xattn_ln_o_b", 2), ("L3_attn_bq_strips", 4), ("L3_attn_bk", 2),
        ("L3_attn_bv", 2), ("L3_attn_bl_strips", 4), ("L3_attn_bl", 2), ("L3_attn_bo", 2), ("conv", 16),
        ("A_log", 64)]
VEC_AT, _n = {}, 0
for _name, _c in VECS:
    VEC_AT[_name] = (_n, _n + _c)
    _n += _c
N_VECS = _n

LAYER_VECS = {"bq": (0, 4), "bq_turned": (4, 8), "bk": (8, 12), "bk_turned": (12, 16), "bv": (16, 18),
              "bo": (18, 20), "n1": (20, 22), "n2": (22, 24), "n3": (24, 26)}

SEMS = ["loaded", "stored", "products", "act_done", "vec_done", "vec_step", "evacuated", "pool_done",
        "scored", "shifted", "exps", "turned", "unturned", "weighted", "merged"]


class Core:

    def __init__(self, nc, d, ctx):
        self.nc, self.d, self.ctx, self.count = nc, d, ctx, 0
        self.sems = [ctx.enter_context(nc.semaphore(n)) for n in SEMS]
        (self.loaded, self.stored, self.products, self.act_done, self.vec_done, self.vec_step, self.evacuated,
         self.pool_done, self.scored, self.shifted, self.exps, self.turned, self.unturned, self.weighted,
         self.merged) = self.sems
        nums = [s.num for s in self.sems]
        assert nums == list(range(nums[0], nums[0] + len(nums)))
        self.sem_range = range(nums[0], nums[0] + len(nums))

    def name(self, what):
        self.count += 1
        return f"{what}_{self.count}"

    def sb(self, stack, what, shape, dt=F32):
        return stack.enter_context(self.nc.sbuf_tensor(self.name(what), shape, dt))

    def ps(self, stack, what, shape, dt=F32):
        return stack.enter_context(self.nc.psum_tensor(self.name(what), shape, dt))

    @contextmanager
    def stage(self):
        with self.nc.Block() as block:
            yield block
        self.nc.sync.sem_clear(self.sem_range)
        self.nc.all_engine_barrier()

    def vec(self, name):
        a, b = VEC_AT[name]
        return self.vecs[:, a:b]


class Steps:

    def __init__(self, eng, sem):
        self.eng, self.sem, self.n = eng, sem, 0

    def __call__(self, instruction):
        instruction.then_inc(self.sem, 1)
        self.n += 1
        self.eng.wait_ge(self.sem, self.n)


def rows(w):
    return w.rearrange("(c p) m -> p c m", p=P)


def load(k, pairs):
    with k.stage() as block:
        @block.sync
        def _(sp):
            for dst, src in pairs:
                sp.dma_start(dst, src).then_inc(k.loaded, 16)
            sp.wait_ge(k.loaded, 16 * len(pairs))


def project(k, dst, src, kc, w, mc, n, loads=(), func=ACT.Identity, bias=None, scale=1.0, vec=None):
    nc = k.nc
    with ExitStack() as own:
        ps = k.ps(own, "proj_ps", [P, 4, 512])
        with k.stage() as block:
            @block.sync
            def _(sp):
                for to, fr in loads:
                    sp.dma_start(to, fr).then_inc(k.loaded, 16)

            @block.tensor
            def _(pe):
                if loads:
                    pe.wait_ge(k.loaded, 16 * len(loads))
                for m in range(mc):
                    if m >= 4:
                        pe.wait_ge(k.evacuated, m - 3)
                    for c in range(kc):
                        mm = nc.tensor.matmul(ps[:, m % 4, 0:n], w[:, c, m * P:(m + 1) * P], src[:, c, :],
                                              start=(c == 0), stop=(c == kc - 1))
                    mm.then_inc(k.products, 1)

            @block.scalar
            def _(act):
                if vec is None:
                    if loads:
                        act.wait_ge(k.loaded, 16 * len(loads))
                    for m in range(mc):
                        act.wait_ge(k.products, m + 1)
                        nc.scalar.activation(
                            dst[:, m, :], ps[:, m % 4, 0:n], func,
                            bias=0.0 if bias is None else bias[:, m:m + 1],
                            scale=scale if isinstance(scale, float) else scale[:, m:m + 1],
                        ).then_inc(k.evacuated, 1)

            @block.vector
            def _(v):
                if vec is not None:
                    col, op0, other, op1 = vec
                    if loads:
                        v.wait_ge(k.loaded, 16 * len(loads))
                    for m in range(mc):
                        v.wait_ge(k.products, m + 1)
                        nc.vector.scalar_tensor_tensor(
                            out=dst[:, m, :], in0=ps[:, m % 4, 0:n],
                            scalar=col if isinstance(col, float) else col[:, m:m + 1],
                            in1=other[:, m, :], op0=op0, op1=op1).then_inc(k.evacuated, 1)


def project_tokens(k, dst, src, kc, w, tiles, nf, loads=(), bias_rows=None):
    nc = k.nc
    nb = (nf + 511) // 512
    fb = nf // nb
    with ExitStack() as own:
        ps = k.ps(own, "tok_ps", [P, 4, 512])
        with k.stage() as block:
            @block.sync
            def _(sp):
                for to, fr in loads:
                    sp.dma_start(to, fr).then_inc(k.loaded, 16)

            @block.tensor
            def _(pe):
                if loads:
                    pe.wait_ge(k.loaded, 16 * len(loads))
                i = 0
                for t in range(tiles):
                    for f in range(nb):
                        if i >= 4:
                            pe.wait_ge(k.evacuated, i - 3)
                        for c in range(kc):
                            mm = nc.tensor.matmul(ps[:, i % 4, 0:fb], src[:, c, t * P:(t + 1) * P],
                                                  w[:, c, f * fb:(f + 1) * fb], start=(c == 0), stop=(c == kc - 1))
                        mm.then_inc(k.products, 1)
                        i += 1

            @block.scalar
            def _(act):
                if bias_rows is None:
                    for i in range(tiles * nb):
                        act.wait_ge(k.products, i + 1)
                        nc.scalar.activation(dst[:, i // nb, (i % nb) * fb:(i % nb + 1) * fb], ps[:, i % 4, 0:fb],
                                             ACT.Identity).then_inc(k.evacuated, 1)

            @block.vector
            def _(v):
                if bias_rows is not None:
                    if loads:
                        v.wait_ge(k.loaded, 16 * len(loads))
                    for i in range(tiles * nb):
                        v.wait_ge(k.products, i + 1)
                        nc.vector.tensor_tensor(dst[:, i // nb, (i % nb) * fb:(i % nb + 1) * fb], ps[:, i % 4, 0:fb],
                                                bias_rows[:, (i % nb) * fb:(i % nb + 1) * fb],
                                                ALU.add).then_inc(k.evacuated, 1)


def norm(k, dst, src, n, eps, mean=True, w=None, b=None, plus=None, load_src=None):
    nc = k.nc
    with ExitStack() as own:
        ps = k.ps(own, "norm_ps", [P, 2, 512])
        centred = k.sb(own, "centred", [P, 2, n])
        squares = k.sb(own, "squares", [P, 2, n])
        stat = k.sb(own, "stat", [P, 2, n])
        cen = centred if mean else src
        with k.stage() as block:
            @block.sync
            def _(sp):
                if load_src is not None:
                    sp.dma_start(src, load_src).then_inc(k.loaded, 16)

            @block.tensor
            def _(pe):
                if load_src is not None:
                    pe.wait_ge(k.loaded, 16)
                if mean:
                    for c in range(2):
                        mm = nc.tensor.matmul(ps[:, 0, 0:n], k.mean_mat[:], src[:, c, :], start=(c == 0), stop=(c == 1))
                    mm.then_inc(k.products, 1)
                pe.wait_ge(k.vec_done, 1)
                for c in range(2):
                    mm = nc.tensor.matmul(ps[:, 1, 0:n], k.mean_mat[:], squares[:, c, :], start=(c == 0), stop=(c == 1))
                mm.then_inc(k.products, 1)

            @block.scalar
            def _(act):
                act.wait_ge(k.vec_done, 2)
                nc.scalar.activation(stat[:, 1, :], stat[:, 0, :], ACT.Sqrt).then_inc(k.act_done, 1)

            @block.vector
            def _(v):
                step = Steps(v, k.vec_step)
                if load_src is not None:
                    v.wait_ge(k.loaded, 16)
                if mean:
                    v.wait_ge(k.products, 1)
                    step(nc.vector.tensor_tensor(centred[:], src, ps[:, 0, 0:n].unsqueeze(1).broadcast_to([P, 2, n]),
                                                 ALU.subtract))
                nc.vector.tensor_tensor(squares[:], cen[:, :, :], cen[:, :, :], ALU.mult).then_inc(k.vec_done, 1)
                v.wait_ge(k.products, 2 if mean else 1)
                nc.vector.tensor_scalar(stat[:, 0, :], ps[:, 1, 0:n], eps, None, ALU.add).then_inc(k.vec_done, 1)
                v.wait_ge(k.act_done, 1)
                step(nc.vector.reciprocal(stat[:, 0, :], stat[:, 1, :]))
                scaled = squares if plus is not None or w is not None else dst
                step(nc.vector.tensor_tensor(scaled[:, :, :], cen[:, :, :], stat[:, 0, :].unsqueeze(1).broadcast_to([P, 2, n]),
                                             ALU.mult))
                if w is not None:
                    for c in range(2):
                        if plus is not None:
                            step(nc.vector.scalar_tensor_tensor(out=dst[:, c, :], in0=squares[:, c, :], scalar=w[:, c:c + 1],
                                                                in1=plus[:, c, :], op0=ALU.mult, op1=ALU.add))
                            if b is not None:
                                step(nc.vector.tensor_scalar(dst[:, c, :], dst[:, c, :], b[:, c:c + 1], None, ALU.add))
                        elif b is not None:
                            step(nc.vector.tensor_scalar(dst[:, c, :], squares[:, c, :], w[:, c:c + 1], b[:, c:c + 1],
                                                         ALU.mult, ALU.add))
                        else:
                            step(nc.vector.tensor_scalar(dst[:, c, :], squares[:, c, :], w[:, c:c + 1], None, ALU.mult))


def copy_batch(k, dst, src, b):
    with k.stage() as block:
        @block.vector
        def _(v):
            k.nc.vector.tensor_copy(dst, src[:, :, bass.ds(b * S, S)])


def unit_norm(k, t, chunks, n, scale, ones_blocks):
    nc = k.nc
    with ExitStack() as own:
        ps = k.ps(own, "len_ps", [P, chunks, 512])
        sq = k.sb(own, "len_sq", [P, chunks, n])
        ln = k.sb(own, "len_root", [P, chunks, n])
        with k.stage() as block:
            @block.vector
            def _(v):
                step = Steps(v, k.vec_step)
                nc.vector.tensor_tensor(sq[:], t, t, ALU.mult).then_inc(k.vec_done, 1)
                v.wait_ge(k.act_done, 1)
                step(nc.vector.tensor_scalar(ln[:], ln[:], 1e-12, None, ALU.max))
                step(nc.vector.reciprocal(ln[:], ln[:]))
                step(nc.vector.tensor_tensor(ln[:], ln[:], t, ALU.mult))
                nc.vector.tensor_scalar(t, ln[:], scale, None, ALU.mult)

            @block.tensor
            def _(pe):
                pe.wait_ge(k.vec_done, 1)
                for c in range(chunks):
                    mm = nc.tensor.matmul(ps[:, c, 0:n], ones_blocks, sq[:, c, :], start=True, stop=True)
                mm.then_inc(k.products, 1)

            @block.scalar
            def _(act):
                act.wait_ge(k.products, 1)
                nc.scalar.activation(ln[:], ps[:, :, 0:n], ACT.Sqrt).then_inc(k.act_done, 1)


def rope(k, t, turned):
    nc = k.nc
    with k.stage() as block:
        @block.vector
        def _(v):
            step = Steps(v, k.vec_step)
            step(nc.vector.tensor_tensor(t[:], t[:], k.cos[:].unsqueeze(1).broadcast_to([P, 4, S]), ALU.mult))
            step(nc.vector.tensor_tensor(turned[:], turned[:], k.sin[:].unsqueeze(1).broadcast_to([P, 4, S]), ALU.mult))
            nc.vector.tensor_tensor(t[:], t[:], turned[:], ALU.add)


class Heads:

    def __init__(self, n, dim, scale):
        self.n, self.dim, self.scale = n, dim, scale
        self.wide = max(1, dim // P)
        self.rows = {16: 32, 64: 64, 256: P}[dim]
        self.places = P // self.rows
        self.chunks = n * self.wide // self.places
        self.per = min(4, n // self.places)
        self.groups = [(place, c0) for place in range(self.places)
                       for c0 in range(0, n // self.places, self.per)]

    def members(self, group):
        place, c0 = group
        return [(c, c * self.places + place) for c in range(c0, c0 + self.per)]

    def of_group(self, flat, group):
        place, c0 = group
        return flat.rearrange("p (c s x) -> p c s x", s=self.places, c=self.n // self.places)[:, c0:c0 + self.per, place, :]


def attention_state(k, own, hd):
    return {"o": k.sb(own, "att_o", [P, 2, hd.n * hd.dim]), "m": k.sb(own, "att_m", [P, 2, hd.n]),
            "l": k.sb(own, "att_l", [P, 2, hd.n])}


def attention_start(k, st):
    with k.stage() as block:
        @block.vector
        def _(v):
            k.nc.vector.memset(st["o"][:], 0.0)
            k.nc.vector.memset(st["m"][:], START_MAX)
            k.nc.vector.memset(st["l"][:], 0.0)


def attend(k, hd, st, q, kt, val, mask=None, mask_by_query=False):
    nc = k.nc
    units = [(qt, g) for qt in range(2) for g in hd.groups]
    per, dim = hd.per, hd.dim
    nu = len(units)
    with ExitStack() as own:
        score_ps = k.ps(own, "score_ps", [P, 2, 4, KB])
        turn_ps = k.ps(own, "turn_ps", [P, 8, P])
        out_ps = k.ps(own, "out_ps", [P, 2, 512])
        masked = k.sb(own, "masked", [P, per, KB]) if mask is not None else None
        prob = k.sb(own, "prob", [P, 2, per, KB])
        prob_t = k.sb(own, "prob_t", [P, 2, per * 2, P])
        top = k.sb(own, "top", [P, 2, per])
        new_max = k.sb(own, "new_max", [P, 2, per])
        drop = k.sb(own, "drop", [P, 2, per])
        fade = k.sb(own, "fade", [P, 2, per])
        part = k.sb(own, "part", [P, 2, per])
        with k.stage() as block:
            @block.tensor
            def _(pe):
                def scores(u):
                    qt, g = units[u]
                    if u >= 2:
                        pe.wait_ge(k.shifted, u - 1)
                    for i, (c, _) in enumerate(hd.members(g)):
                        p0 = g[0] * hd.rows
                        for w in range(hd.wide):
                            mm = nc.tensor.matmul(
                                score_ps[:, u % 2, i, :], q[p0:p0 + hd.rows, c * hd.wide + w, qt * P:(qt + 1) * P],
                                kt[p0:p0 + hd.rows, c * hd.wide + w, :], start=(w == 0), stop=(w == hd.wide - 1))
                    mm.then_inc(k.scored, 1)

                def values(u):
                    _, g = units[u]
                    pe.wait_ge(k.exps, u + 1)
                    if u >= 1:
                        pe.wait_ge(k.unturned, u)
                    for i in range(per):
                        for c in range(2):
                            mm = nc.tensor.transpose(turn_ps[:, 2 * i + c, :], prob[:, u % 2, i, c * P:(c + 1) * P], k.ident[:])
                    mm.then_inc(k.turned, 1)
                    pe.wait_ge(k.unturned, u + 1)
                    if u >= 2:
                        pe.wait_ge(k.merged, u - 1)
                    for i, (_, h) in enumerate(hd.members(g)):
                        for c in range(2):
                            mm = nc.tensor.matmul(out_ps[:, u % 2, i * dim:(i + 1) * dim], prob_t[:, u % 2, 2 * i + c, :],
                                                  val[:, c, h * dim:(h + 1) * dim], start=(c == 0), stop=(c == 1))
                    mm.then_inc(k.weighted, 1)

                for u in range(nu + 1):
                    if u < nu:
                        scores(u)
                    if u >= 1:
                        values(u - 1)

            @block.scalar
            def _(act):
                for u in range(nu + 1):
                    if u < nu:
                        act.wait_ge(k.shifted, u + 1)
                        nc.scalar.activation(fade[:, u % 2, :], drop[:, u % 2, :], ACT.Exp, scale=hd.scale)
                        nc.scalar.activation(prob[:, u % 2], prob[:, u % 2], ACT.Exp, scale=hd.scale).then_inc(k.exps, 1)
                    if u >= 1:
                        act.wait_ge(k.turned, u)
                        if u >= 3:
                            act.wait_ge(k.weighted, u - 2)
                        nc.scalar.activation(prob_t[:, (u - 1) % 2], turn_ps[:, 0:2 * per, :],
                                             ACT.Identity).then_inc(k.unturned, 1)

            @block.vector
            def _(v):
                step = Steps(v, k.vec_step)

                def maxima(u):
                    qt, g = units[u]
                    j = u % 2
                    m = hd.of_group(st["m"][:, qt, :], g)[:, :, 0]
                    v.wait_ge(k.scored, u + 1)
                    src = score_ps[:, j, 0:per, :]
                    if mask is not None:
                        rows_mask = mask[:, qt if mask_by_query else 0, :]
                        if u >= 1:
                            v.wait_ge(k.shifted, u)
                        step(nc.vector.tensor_tensor(masked[:], src, rows_mask.unsqueeze(1).broadcast_to([P, per, KB]), ALU.add))
                        src = masked[:]
                    step(nc.vector.tensor_reduce(top[:, j, :], src, AX, ALU.max))
                    step(nc.vector.tensor_tensor(new_max[:, j, :], m, top[:, j, :], ALU.max))
                    if u >= 2:
                        v.wait_ge(k.turned, u - 1)
                    step(nc.vector.tensor_tensor(drop[:, j, :], m, new_max[:, j, :], ALU.subtract))
                    step(nc.vector.tensor_copy(m, new_max[:, j, :]))
                    nc.vector.tensor_tensor(prob[:, j], src, new_max[:, j, :].unsqueeze(2).broadcast_to([P, per, KB]),
                                            ALU.subtract).then_inc(k.shifted, 1)

                def merge(u):
                    qt, g = units[u]
                    j = u % 2
                    l = hd.of_group(st["l"][:, qt, :], g)[:, :, 0]
                    o = hd.of_group(st["o"][:, qt, :], g)
                    v.wait_ge(k.exps, u + 1)
                    step(nc.vector.reduce_sum(part[:, j, :], prob[:, j], AX))
                    step(nc.vector.tensor_tensor(l, l, fade[:, j, :], ALU.mult))
                    step(nc.vector.tensor_tensor(l, l, part[:, j, :], ALU.add))
                    step(nc.vector.tensor_tensor(o, o, fade[:, j, :].unsqueeze(2).broadcast_to([P, per, dim]), ALU.mult))
                    v.wait_ge(k.weighted, u + 1)
                    nc.vector.tensor_tensor(o, o, out_ps[:, j, 0:per * dim].rearrange("p (a x) -> p a x", a=per),
                                            ALU.add).then_inc(k.merged, 1)
                    v.wait_ge(k.merged, u + 1)

                for u in range(nu + 1):
                    if u < nu:
                        maxima(u)
                    if u >= 1:
                        merge(u - 1)


def attention_end(k, hd, st, dst, b, bias=None):
    nc = k.nc
    nf = hd.n * hd.dim
    with ExitStack() as own:
        ps = k.ps(own, "end_ps", [P, 4, 512])
        with k.stage() as block:
            @block.vector
            def _(v):
                step = Steps(v, k.vec_step)
                step(nc.vector.reciprocal(st["l"][:], st["l"][:]))
                for qt in range(2):
                    o = st["o"][:, qt, :].rearrange("p (h x) -> p h x", h=hd.n)
                    nc.vector.tensor_tensor(o, o, st["l"][:, qt, :].unsqueeze(2).broadcast_to([P, hd.n, hd.dim]),
                                            ALU.mult).then_inc(k.vec_done, 1)

            @block.tensor
            def _(pe):
                pe.wait_ge(k.vec_done, 2)
                for c in range(nf // P):
                    if c >= 4:
                        pe.wait_ge(k.evacuated, c - 3)
                    for qt in range(2):
                        mm = nc.tensor.transpose(ps[:, c % 4, qt * P:(qt + 1) * P], st["o"][:, qt, c * P:(c + 1) * P], k.ident[:])
                    mm.then_inc(k.products, 1)

            @block.scalar
            def _(act):
                for c in range(nf // P):
                    act.wait_ge(k.products, c + 1)
                    nc.scalar.activation(dst[:, c, bass.ds(b * S, S)], ps[:, c % 4, 0:S], ACT.Identity,
                                         bias=0.0 if bias is None else bias[:, c:c + 1]).then_inc(k.evacuated, 1)


def key_mask(k, dst, src_row, raw):
    with k.stage() as block:
        @block.sync
        def _(sp):
            sp.dma_start(raw, src_row.unsqueeze(0).broadcast_to([P, KB])).then_inc(k.loaded, 16)

        @block.vector
        def _(v):
            v.wait_ge(k.loaded, 16)
            k.nc.vector.tensor_scalar(dst, raw, 0.0, NEG, ALU.is_equal, ALU.mult)




def l0_cross(k, x):
    nc, d = k.nc, k.d
    hd = Heads(16, 16, 0.25)
    with ExitStack() as own:
        h = k.sb(own, "h", [P, 2, T])
        q = k.sb(own, "q", [P, 4, T])
        qb = k.sb(own, "qb", [P, 4, S])
        ot = k.sb(own, "ot", [P, 2, T])
        wq, wk = k.sb(own, "wq", [P, 2, 512]), k.sb(own, "wk", [P, 2, 512])
        wv, wo = k.sb(own, "wv", [P, 2, D]), k.sb(own, "wo", [P, 2, D])
        ctx = k.sb(own, "ctx", [P, 2, KB])
        kt = k.sb(own, "kt", [P, 4, KB])
        val = k.sb(own, "val", [P, 2, D])
        raw = k.sb(own, "raw", [P, KB], mybir.dt.int32)
        mask = k.sb(own, "mask", [P, 1, KB])
        st = attention_state(k, own, hd)
        norm(k, h[:], x[:], T, 1e-5)
        project(k, q, h, 2, wq, 4, T, loads=[(wq[:], rows(d["L0_xattn_Wq_strips"])), (wk[:], rows(d["L0_xattn_Wk_strips"])),
                                             (wv[:], rows(d["L0_xattn_Wv"])), (wo[:], rows(d["L0_xattn_Wo"]))])
        with nc.Fori(0, B) as b:
            copy_batch(k, qb[:], q, b)
            attention_start(k, st)
            with nc.Fori(0, SK // KB) as j:
                key_mask(k, mask[:, 0, :], d["mask_BxS2_ik1"][b, bass.ds(j * KB, KB)], raw[:])
                project(k, kt, ctx, 2, wk, 4, KB, loads=[(ctx[:], rows(d["ctx_t"][b])[:, :, bass.ds(j * KB, KB)])])
                project_tokens(k, val, ctx, 2, wv, 2, D)
                attend(k, hd, st, qb, kt, val, mask)
            attention_end(k, hd, st, ot, b)
        project(k, x, ot, 2, wo, 2, T, vec=(0.0, ALU.add, x, ALU.add))


def l0_scan(k, x):
    nc, d = k.nc, k.d
    NS = 16
    with ExitStack() as own:
        h = k.sb(own, "h", [P, 2, T])
        gate = k.sb(own, "gate", [P, 4, T])
        hs = k.sb(own, "hs", [P, 4, T])
        delta = k.sb(own, "delta", [P, 4, T])
        y = k.sb(own, "y", [P, 4, T])
        u = k.sb(own, "u", [P, 4, T])
        w_in = k.sb(own, "w_in", [P, 2, 1024])
        w_out = k.sb(own, "w_out", [P, 4, D])
        xp = k.sb(own, "xp", [P, 4, P])
        w_dt = k.sb(own, "w_dt", [64, 4 * P])
        dbl = k.sb(own, "dbl", [P, 1, T])
        a_neg = k.sb(own, "a_neg", [P, 64])
        conv = k.vec("conv")
        norm(k, h[:], x[:], T, 1e-5)
        project(k, hs, h, 2, w_in, 4, T, loads=[(w_in[:], rows(d["L0_attn_w_in_t"])), (w_out[:], rows(d["L0_attn_w_out_t"])),
                                                (xp[:], rows(d["L0_attn_w_xproj_t"])), (w_dt[:], d["L0_attn_w_dt_t"])])
        project(k, gate, h, 2, w_in[:, :, 512:1024], 4, T, func=ACT.Silu)
        with ExitStack() as inner:
            padded = k.sb(inner, "padded", [P, 4, B, S + 3])
            acc = k.sb(inner, "acc", [P, 4, B, S])
            with k.stage() as block:
                @block.vector
                def _(v):
                    step = Steps(v, k.vec_step)
                    step(nc.vector.memset(padded[:], 0.0))
                    for c in range(4):
                        step(nc.vector.tensor_copy(padded[:, c, :, 3:S + 3], hs[:, c, :].rearrange("p (b s) -> p b s", b=B)))
                        step(nc.vector.tensor_scalar(acc[:, c], padded[:, c, :, 0:S], conv[:, 4 * c:4 * c + 1], None, ALU.mult))
                        for i in range(1, 4):
                            ins = nc.vector.scalar_tensor_tensor(out=acc[:, c], in0=padded[:, c, :, i:S + i],
                                                                 scalar=conv[:, 4 * c + i:4 * c + i + 1], in1=acc[:, c],
                                                                 op0=ALU.mult, op1=ALU.add)
                            if i < 3:
                                step(ins)
                        ins.then_inc(k.vec_done, 1)

                @block.scalar
                def _(act):
                    for c in range(4):
                        act.wait_ge(k.vec_done, c + 1)
                        nc.scalar.activation(hs[:, c, :], acc[:, c].rearrange("p b s -> p (b s)"), ACT.Silu)
        project(k, dbl, hs, 4, xp, 1, T)
        with ExitStack() as inner:
            ps = k.ps(inner, "dt_ps", [P, 4, 512])
            z = k.sb(inner, "z", [P, 4, T])
            e = k.sb(inner, "e", [P, 4, T])
            with k.stage() as block:
                @block.sync
                def _(sp):
                    sp.dma_start(d["bc_rows"], dbl[64:96, 0, :]).then_inc(k.stored, 16)
                    sp.wait_ge(k.stored, 16)

                @block.tensor
                def _(pe):
                    for c in range(4):
                        mm = nc.tensor.matmul(ps[:, c, :], w_dt[:, c * P:(c + 1) * P], dbl[0:64, 0, :], start=True, stop=True)
                    mm.then_inc(k.products, 1)

                @block.scalar
                def _(act):
                    nc.scalar.activation(a_neg[:], k.vec("A_log"), ACT.Exp).then_inc(k.act_done, 1)
                    act.wait_ge(k.products, 1)
                    for c in range(4):
                        nc.scalar.activation(z[:, c, :], ps[:, c, :], ACT.Identity, bias=k.vec("L0_attn_b_dt")[:, c:c + 1])\
                            .then_inc(k.act_done, 1)
                    act.wait_ge(k.act_done, 5)
                    nc.scalar.activation(e[:], z[:], ACT.Abs).then_inc(k.act_done, 1)
                    act.wait_ge(k.act_done, 6)
                    nc.scalar.activation(e[:], e[:], ACT.Exp, scale=-1.0).then_inc(k.act_done, 1)
                    act.wait_ge(k.act_done, 7)
                    nc.scalar.activation(e[:], e[:], ACT.Ln, bias=1.0).then_inc(k.act_done, 1)

                @block.vector
                def _(v):
                    step = Steps(v, k.vec_step)
                    v.wait_ge(k.act_done, 8)
                    nc.vector.tensor_scalar(a_neg[:], a_neg[:], -1.0, None, ALU.mult)
                    step(nc.vector.scalar_tensor_tensor(out=delta[:], in0=z[:], scalar=0.0, in1=e[:], op0=ALU.max, op1=ALU.add))
                    nc.vector.tensor_tensor(u[:], delta[:], hs[:], ALU.mult)
                    for c in range(4):
                        nc.vector.tensor_scalar(y[:, c, :], hs[:, c, :], k.vec("L0_attn_D")[:, c:c + 1], None, ALU.mult)
        with ExitStack() as inner:
            bb = k.sb(inner, "bb", [P, T])
            cb = k.sb(inner, "cb", [P, T])
            decay = k.sb(inner, "decay", [P, 4, T])
            drive = k.sb(inner, "drive", [P, 4, T])
            state = k.sb(inner, "state", [P, 4, T])
            a_n = k.sb(inner, "a_n", [P, 4])
            with nc.Fori(0, NS) as n:
                with k.stage() as block:
                    @block.sync
                    def _(sp):
                        sp.dma_start(bb[:], d["bc_rows"][n].unsqueeze(0).broadcast_to([P, T])).then_inc(k.loaded, 16)
                        sp.dma_start(cb[:], d["bc_rows"][n + NS].unsqueeze(0).broadcast_to([P, T])).then_inc(k.loaded, 16)

                    @block.scalar
                    def _(act):
                        nc.scalar.activation(a_n[:], a_neg[:, bass.ds(n * 4, 4)], ACT.Identity).then_inc(k.act_done, 1)
                        act.wait_ge(k.act_done, 1)
                        for c in range(4):
                            nc.scalar.activation(decay[:, c, :], delta[:, c, :], ACT.Exp, scale=a_n[:, c:c + 1])\
                                .then_inc(k.act_done, 1)

                    @block.gpsimd
                    def _(pool):
                        pool.wait_ge(k.loaded, 32)
                        for c in range(4):
                            nc.gpsimd.tensor_tensor(drive[:, c, :], u[:, c, :], bb[:], ALU.mult).then_inc(k.pool_done, 1)

                    @block.vector
                    def _(v):
                        step = Steps(v, k.vec_step)
                        v.wait_ge(k.loaded, 32)
                        for c in range(4):
                            v.wait_ge(k.act_done, c + 2)
                            v.wait_ge(k.pool_done, c + 1)
                            for b in range(B):
                                s = slice(b * S, (b + 1) * S)
                                step(nc.vector.tensor_tensor_scan(state[:, c, s], decay[:, c, s], drive[:, c, s], 0.0,
                                                                  ALU.mult, ALU.add))
                            step(nc.vector.tensor_tensor(state[:, c, :], state[:, c, :], cb[:], ALU.mult))
                            nc.vector.tensor_tensor(y[:, c, :], y[:, c, :], state[:, c, :], ALU.add)
        with k.stage() as block:
            @block.vector
            def _(v):
                nc.vector.tensor_tensor(y[:], y[:], gate[:], ALU.mult)
        project(k, x, y, 4, w_out, 2, T, vec=(0.0, ALU.add, x, ALU.add))


def router(k, own, h, w_name, bias_name=None):
    d = k.d
    wg = k.sb(own, "wg", [P, 2, 8])
    logits = k.sb(own, "logits", [P, 4, 8])
    bias = k.sb(own, "gate_bias", [P, 8])
    loads = [(wg[:], rows(d[w_name]))]
    if bias_name is not None:
        loads.append((bias[:], d[bias_name].unsqueeze(0).broadcast_to([P, 8])))
    project_tokens(k, logits, h, 2, wg, 4, 8, loads=loads)
    return logits, bias


def softmax8(k, s):
    nc = k.nc
    with ExitStack() as own:
        r = k.sb(own, "row", [P, 4])
        with k.stage() as block:
            @block.vector
            def _(v):
                step = Steps(v, k.vec_step)
                step(nc.vector.tensor_reduce(r[:], s[:], AX, ALU.max))
                nc.vector.tensor_tensor(s[:], s[:], r[:].unsqueeze(2).broadcast_to([P, 4, 8]), ALU.subtract).then_inc(k.vec_done, 1)
                v.wait_ge(k.act_done, 1)
                step(nc.vector.reduce_sum(r[:], s[:], AX))
                step(nc.vector.reciprocal(r[:], r[:]))
                nc.vector.tensor_tensor(s[:], s[:], r[:].unsqueeze(2).broadcast_to([P, 4, 8]), ALU.mult)

            @block.scalar
            def _(act):
                act.wait_ge(k.vec_done, 1)
                nc.scalar.activation(s[:], s[:], ACT.Exp).then_inc(k.act_done, 1)


def gates_by_expert(k, w, wt):
    nc = k.nc
    with ExitStack() as own:
        ps = k.ps(own, "gate_ps", [P, 512])
        with k.stage() as block:
            @block.tensor
            def _(pe):
                for t in range(4):
                    mm = nc.tensor.transpose(ps[0:8, t * P:(t + 1) * P], w[:, t, :], k.ident[:])
                mm.then_inc(k.products, 1)

            @block.vector
            def _(v):
                v.wait_ge(k.products, 1)
                nc.vector.tensor_copy(wt[:], ps[0:8, :])


def store_gates(k, wt, shared=None):
    nc, d = k.nc, k.d
    with ExitStack() as own:
        row = k.sb(own, "shared_row", [1, T])
        with k.stage() as block:
            @block.vector
            def _(v):
                if shared is not None:
                    nc.vector.memset(row[:], shared).then_inc(k.vec_done, 1)

            @block.sync
            def _(sp):
                sp.dma_start(d["gate_rows"][0:8, :], wt[:]).then_inc(k.stored, 16)
                if shared is not None:
                    sp.wait_ge(k.vec_done, 1)
                    sp.dma_start(d["gate_rows"][8:9, :], row[:]).then_inc(k.stored, 16)
                sp.wait_ge(k.stored, 32 if shared is not None else 16)


def experts_gelu(k, x, h, n, up, down, vecs):
    nc, d = k.nc, k.d
    with ExitStack() as own:
        wu = k.sb(own, "wu", [P, 2, 1024])
        wd = k.sb(own, "wd", [P, 8, D])
        bv = k.sb(own, "bv", [P, 10])
        gate = k.sb(own, "gate", [P, T])
        a = k.sb(own, "a", [P, 8, T])
        y = k.sb(own, "y", [P, 2, T])
        ps = k.ps(own, "moe_ps", [P, 6, 512])
        with nc.Fori(0, n) as e:
            with k.stage() as block:
                @block.sync
                def _(sp):
                    sp.dma_start(bv[:], d[vecs][e]).then_inc(k.loaded, 16)
                    sp.dma_start(wu[:], rows(d[up][e])).then_inc(k.loaded, 16)
                    sp.wait_ge(k.loaded, 32)
                    sp.dma_start(gate[:], d["gate_rows"][e].unsqueeze(0).broadcast_to([P, T])).then_inc(k.loaded, 16)
                    sp.dma_start(wd[:], rows(d[down][e])).then_inc(k.loaded, 16)

                @block.tensor
                def _(pe):
                    pe.wait_ge(k.loaded, 32)
                    for m in range(8):
                        if m >= 4:
                            pe.wait_ge(k.act_done, m - 3)
                        for c in range(2):
                            mm = nc.tensor.matmul(ps[:, m % 4, :], wu[:, c, m * P:(m + 1) * P], h[:, c, :],
                                                  start=(c == 0), stop=(c == 1))
                        mm.then_inc(k.products, 1)
                    pe.wait_ge(k.loaded, 64)
                    for f in range(8):
                        pe.wait_ge(k.act_done, f + 1)
                        for m in range(2):
                            mm = nc.tensor.matmul(ps[:, 4 + m, :], wd[:, f, m * P:(m + 1) * P], a[:, f, :],
                                                  start=(f == 0), stop=(f == 7))
                    mm.then_inc(k.products, 1)

                @block.scalar
                def _(act):
                    act.wait_ge(k.loaded, 32)
                    for m in range(8):
                        act.wait_ge(k.products, m + 1)
                        nc.scalar.activation(a[:, m, :], ps[:, m % 4, :], ACT.Gelu, bias=bv[:, m:m + 1]).then_inc(k.act_done, 1)

                @block.vector
                def _(v):
                    step = Steps(v, k.vec_step)
                    v.wait_ge(k.loaded, 64)
                    v.wait_ge(k.products, 9)
                    for m in range(2):
                        step(nc.vector.scalar_tensor_tensor(out=y[:, m, :], in0=ps[:, 4 + m, :], scalar=bv[:, 8 + m:9 + m],
                                                            in1=gate[:], op0=ALU.add, op1=ALU.mult))
                    nc.vector.tensor_tensor(x[:], x[:], y[:], ALU.add)


def l0_experts(k, x):
    nc = k.nc
    with ExitStack() as own:
        h = k.sb(own, "h", [P, 2, T])
        norm(k, h[:], x[:], T, 1e-5)
        s, bias = router(k, own, h, "L0_ffn_gate_w_t", "L0_ffn_gate_bias")
        top = k.sb(own, "top", [P, 4, 8])
        den = k.sb(own, "den", [P, 4])
        w = k.sb(own, "w", [P, 4, 8])
        wt = k.sb(own, "wt", [8, T])
        with k.stage() as block:
            @block.vector
            def _(v):
                step = Steps(v, k.vec_step)
                nc.vector.tensor_tensor(s[:], s[:], bias[:].unsqueeze(1).broadcast_to([P, 4, 8]), ALU.add).then_inc(k.vec_done, 1)
                v.wait_ge(k.act_done, 1)
                for t in range(4):
                    step(nc.vector.max(top[:, t, :], s[:, t, :]))
                step(nc.vector.tensor_tensor(den[:], top[:, :, 0], top[:, :, 1], ALU.add))
                step(nc.vector.tensor_scalar(den[:], den[:], 1e-6, None, ALU.add))
                step(nc.vector.reciprocal(den[:], den[:]))
                step(nc.vector.tensor_tensor(w[:], s[:], top[:, :, 1:2].broadcast_to([P, 4, 8]), ALU.is_ge))
                step(nc.vector.tensor_tensor(w[:], w[:], s[:], ALU.mult))
                nc.vector.tensor_tensor(w[:], w[:], den[:].unsqueeze(2).broadcast_to([P, 4, 8]), ALU.mult)

            @block.scalar
            def _(act):
                act.wait_ge(k.vec_done, 1)
                nc.scalar.activation(s[:], s[:], ACT.Sigmoid).then_inc(k.act_done, 1)
        gates_by_expert(k, w, wt)
        store_gates(k, wt, 0.1)
        experts_gelu(k, x, h, 9, "L0_ffn_up", "L0_ffn_down", "L0_ffn_vecs")




def l1_cross(k, x):
    nc, d = k.nc, k.d
    hd = Heads(1, 256, 1.0 / 16)
    with ExitStack() as own:
        h = k.sb(own, "h", [P, 2, T])
        q = k.sb(own, "q", [P, 2, T])
        qb = k.sb(own, "qb", [P, 2, S])
        ot = k.sb(own, "ot", [P, 2, T])
        wq, wk, wv, wo = (k.sb(own, n, [P, 2, D]) for n in ("wq", "wk", "wv", "wo"))
        ctx = k.sb(own, "ctx", [P, 2, KB])
        kt = k.sb(own, "kt", [P, 2, KB])
        val = k.sb(own, "val", [P, 2, D])
        st = attention_state(k, own, hd)
        norm(k, h[:], x[:], T, 1e-5)
        project(k, q, h, 2, wq, 2, T, bias=k.vec("L1_xattn_bq"), loads=[
            (wq[:], rows(d["L1_xattn_Wq_t"])), (wk[:], rows(d["L1_xattn_Wk_t"])),
            (wv[:], rows(d["L1_xattn_Wv_t"])), (wo[:], rows(d["L1_xattn_Wo_t"]))])
        with nc.Fori(0, B) as b:
            copy_batch(k, qb[:], q, b)
            attention_start(k, st)
            with nc.Fori(0, SK // KB) as j:
                project(k, kt, ctx, 2, wk, 2, KB, loads=[(ctx[:], rows(d["ctx_t"][b])[:, :, bass.ds(j * KB, KB)])])
                project_tokens(k, val, ctx, 2, wv, 2, D)
                attend(k, hd, st, qb, kt, val)
            attention_end(k, hd, st, ot, b, bias=k.vec("L1_xattn_bv"))
        project(k, x, ot, 2, wo, 2, T, vec=(k.vec("L1_xattn_bo"), ALU.add, x, ALU.add))


def l1_self(k, x):
    nc, d = k.nc, k.d
    hd = Heads(16, 64, 0.125)
    with ExitStack() as own:
        h = k.sb(own, "h", [P, 2, T])
        hb = k.sb(own, "hb", [P, 2, S])
        qb, kt = k.sb(own, "qb", [P, 8, S]), k.sb(own, "kt", [P, 8, S])
        val = k.sb(own, "val", [P, 2, 1024])
        ot = k.sb(own, "ot", [P, 8, T])
        wq, wk, wv = (k.sb(own, n, [P, 2, 1024]) for n in ("wq", "wk", "wv"))
        wo = k.sb(own, "wo", [P, 8, D])
        st = attention_state(k, own, hd)
        norm(k, h[:], x[:], T, 1e-5)
        load(k, [(wq[:], rows(d["L1_attn_w_q_t"])), (wk[:], rows(d["L1_attn_w_k_t"])), (wv[:], rows(d["L1_attn_w_v_t"])),
                 (wo[:], rows(d["L1_attn_w_o"]))])
        with nc.Fori(0, B) as b:
            copy_batch(k, hb[:], h, b)
            project(k, qb, hb, 2, wq, 8, S)
            project(k, kt, hb, 2, wk, 8, S)
            project_tokens(k, val, hb, 2, wv, 2, 1024)
            attention_start(k, st)
            attend(k, hd, st, qb, kt, val)
            attention_end(k, hd, st, ot, b)
        project(k, h, ot, 8, wo, 2, T, vec=(0.0, ALU.add, h, ALU.add))
        with k.stage() as block:
            @block.vector
            def _(v):
                nc.vector.tensor_tensor(x[:], x[:], h[:], ALU.add)


def l1_ffn(k, x):
    d = k.d
    with ExitStack() as own:
        h = k.sb(own, "h", [P, 2, T])
        w = k.sb(own, "w", [P, 8, 1024])
        a1, a2 = k.sb(own, "a1", [P, 8, T]), k.sb(own, "a2", [P, 8, T])
        norm(k, h[:], x[:], T, 1e-5)
        project(k, a1, h, 2, w, 8, T, loads=[(w[:, 0:2, :], rows(d["L1_ffn_w1_t"]))], func=ACT.Silu, scale=k.vec("L1_ffn_w1_s"))
        project(k, a1, h, 2, w, 8, T, loads=[(w[:, 0:2, :], rows(d["L1_ffn_w2_t"]))],
                vec=(k.vec("L1_ffn_w2_s"), ALU.mult, a1, ALU.mult))
        project(k, a2, a1, 8, w, 8, T, loads=[(w[:], rows(d["L1_ffn_h1_t"]))], func=ACT.Gelu, scale=k.vec("L1_ffn_h1_s"))
        project(k, a1, a2, 8, w, 8, T, loads=[(w[:], rows(d["L1_ffn_h2_t"]))], func=ACT.Gelu, scale=k.vec("L1_ffn_h2_s"))
        project(k, x, a1, 8, w, 2, T, loads=[(w[:, :, 0:D], rows(d["L1_ffn_w3_t"]))],
                vec=(k.vec("L1_ffn_w3_s"), ALU.mult, x, ALU.add))




def window_mask(k, dst, seg, offset, work):
    nc = k.nc
    with k.stage() as block:
        @block.vector
        def _(v):
            step = Steps(v, k.vec_step)
            step(nc.vector.tensor_scalar(work[:, 0, :], k.iota[:], offset, None, ALU.add))
            for t in range(2):
                step(nc.vector.tensor_scalar(work[:, 1, :], work[:, 0, :], seg[:, t:t + 1], None, ALU.subtract))
                step(nc.vector.tensor_scalar(dst[:, t, :], work[:, 1, :], 0.0, NEG, ALU.is_gt, ALU.mult))
                step(nc.vector.tensor_scalar(work[:, 1, :], work[:, 1, :], -128.0, NEG, ALU.is_le, ALU.mult))
                step(nc.vector.tensor_tensor(dst[:, t, :], dst[:, t, :], work[:, 1, :], ALU.add))
            nc.vector.tensor_scalar(offset, offset, float(KB), None, ALU.add)


def l2_cross(k, x):
    nc, d = k.nc, k.d
    hd = Heads(16, 16, 0.25)
    with ExitStack() as own:
        xx = k.sb(own, "xx", [P, 2, T])
        h = k.sb(own, "h", [P, 2, T])
        hb = k.sb(own, "hb", [P, 2, S])
        qb, qr, kt = (k.sb(own, n, [P, 4, S]) for n in ("qb", "qr", "kt"))
        val = k.sb(own, "val", [P, 2, D])
        ot = k.sb(own, "ot", [P, 2, T])
        wqk = k.sb(own, "wqk", [P, 2, 2048])
        wv, wo, wvc, woc = (k.sb(own, n, [P, 2, D]) for n in ("wv", "wo", "wvc", "woc"))
        wqc, wkc = k.sb(own, "wqc", [P, 2, 512]), k.sb(own, "wkc", [P, 2, 512])
        lv = k.sb(own, "lv", [P, 26])
        ctx = k.sb(own, "ctx", [P, 2, KB])
        mask = k.sb(own, "mask", [P, 2, KB])
        work = k.sb(own, "work", [P, 2, KB])
        seg_i = k.sb(own, "seg_i", [P, 2], mybir.dt.int32)
        seg = k.sb(own, "seg", [P, 2])
        offset = k.sb(own, "offset", [P, 1])
        st = attention_state(k, own, hd)

        def col(name):
            a, b = LAYER_VECS[name]
            return lv[:, a:b]

        norm(k, xx[:], x[:], T, 1e-5)
        with nc.Fori(0, 4) as layer:
            load(k, [(wqk[:], rows(d["L2_qk_strips"][layer])), (wv[:], rows(d["L2_wv"][layer])), (wo[:], rows(d["L2_wo"][layer])),
                     (wqc[:], rows(d["L2_qc_strips"][layer])), (wkc[:], rows(d["L2_kc_strips"][layer])),
                     (wvc[:], rows(d["L2_wvc"][layer])), (woc[:], rows(d["L2_woc"][layer])), (lv[:], d["L2_vecs"][layer])])
            norm(k, h[:], xx[:], T, 1e-6, mean=False, w=col("n1"))
            with nc.Fori(0, B) as b:
                copy_batch(k, hb[:], h, b)
                project(k, qb, hb, 2, wqk[:, :, 0:512], 4, S, bias=col("bq"))
                project(k, qr, hb, 2, wqk[:, :, 512:1024], 4, S, bias=col("bq_turned"))
                rope(k, qb, qr)
                project(k, kt, hb, 2, wqk[:, :, 1024:1536], 4, S, bias=col("bk"))
                project(k, qr, hb, 2, wqk[:, :, 1536:2048], 4, S, bias=col("bk_turned"))
                rope(k, kt, qr)
                project_tokens(k, val, hb, 2, wv, 2, D)
                attention_start(k, st)
                attend(k, hd, st, qb, kt, val, k.causal, mask_by_query=True)
                attention_end(k, hd, st, ot, b, bias=col("bv"))
            project(k, xx, ot, 2, wo, 2, T, vec=(col("bo"), ALU.add, xx, ALU.add))
            norm(k, h[:], xx[:], T, 1e-6, mean=False, w=col("n2"))
            with nc.Fori(0, B) as b:
                copy_batch(k, hb[:], h, b)
                project(k, qb, hb, 2, wqc, 4, S)
                attention_start(k, st)
                with k.stage() as block:
                    @block.sync
                    def _(sp):
                        sp.dma_start(seg_i[:], d["seg_cols"][b]).then_inc(k.loaded, 16)

                    @block.vector
                    def _(v):
                        v.wait_ge(k.loaded, 16)
                        nc.vector.tensor_copy(seg[:], seg_i[:])
                        nc.vector.memset(offset[:], 0.0)
                with nc.Fori(0, SK // KB) as j:
                    window_mask(k, mask, seg, offset[:], work)
                    project(k, kt, ctx, 2, wkc, 4, KB, loads=[(ctx[:], rows(d["ctx_t"][b])[:, :, bass.ds(j * KB, KB)])])
                    project_tokens(k, val, ctx, 2, wvc, 2, D)
                    attend(k, hd, st, qb, kt, val, mask, mask_by_query=True)
                attention_end(k, hd, st, ot, b)
            project(k, xx, ot, 2, woc, 2, T, vec=(0.0, ALU.add, xx, ALU.add))
            norm(k, h[:], xx[:], T, 1e-6, mean=False, w=col("n3"))
            with ExitStack() as inner:
                wg = k.sb(inner, "wg", [P, 2, 1024])
                wu = k.sb(inner, "wu", [P, 2, 1024])
                wd = k.sb(inner, "wd", [P, 8, D])
                a = k.sb(inner, "a", [P, 8, T])
                project(k, a, h, 2, wg, 8, T, func=ACT.Silu, loads=[(wg[:], rows(d["L2_wg"][layer])), (wu[:], rows(d["L2_wu"][layer])),
                                                                    (wd[:], rows(d["L2_wd"][layer]))])
                project(k, a, h, 2, wu, 8, T, vec=(1.0, ALU.mult, a, ALU.mult))
                project(k, xx, a, 8, wd, 2, T, vec=(0.0, ALU.add, xx, ALU.add))
        norm(k, x[:], xx[:], T, 1e-6, mean=False, w=k.vec("L2_xattn_nf"), plus=x)


def l2_self(k, x):
    nc, d = k.nc, k.d
    nh, dim = 16, 16
    with ExitStack() as own:
        h = k.sb(own, "h", [P, 2, T])
        wq, wk, wv, wo = (k.sb(own, n, [P, 2, D]) for n in ("wq", "wk", "wv", "wo"))
        rb = k.sb(own, "rb", [P, 5, D])
        q, key, val = (k.sb(own, n, [P, 4, D]) for n in ("q", "key", "val"))
        rel = k.sb(own, "rel", [P, 6, nh])
        gw = k.sb(own, "gw", [P, dim, 8])
        gb = k.sb(own, "gb", [P, 8])
        ga = k.sb(own, "ga", [P, nh])
        gws = k.sb(own, "gws", [P, dim])
        gbs = k.sb(own, "gbs", [P, 1])
        gate = k.sb(own, "gate", [P, 4, nh])
        prod = k.sb(own, "prod", [P, D])
        sc = k.sb(own, "sc", [P, 4, 3, nh])
        mx = k.sb(own, "mx", [P, 4, nh])
        o = k.sb(own, "o", [P, 4, D])
        ot = k.sb(own, "ot", [P, 2, T])

        def all_rows(src, n):
            return src.unsqueeze(0).broadcast_to([P, n])

        bucket = {-1: 1, 0: 0, 1: 17, 2: 18}
        norm(k, h[:], x[:], T, 1e-5)
        load(k, [(wq[:], rows(d["L2_attn_q_w"])), (wk[:], rows(d["L2_attn_k_w"])), (wv[:], rows(d["L2_attn_v_w"])),
                 (wo[:], rows(d["L2_attn_out_w"]))]
             + [(rb[:, i, :], all_rows(d[n], D)) for i, n in enumerate(
                 ["L2_attn_q_b", "L2_attn_k_b", "L2_attn_v_b", "L2_attn_bias_k_row", "L2_attn_bias_v_row"])]
             + [(rel[:, 3 * t + s, :], all_rows(d["L2_attn_rel_emb"][bucket[s - t]], nh)) for t in range(2) for s in range(3)]
             + [(gw[:].rearrange("p a b -> p (a b)"), all_rows(d["L2_attn_grep_w_row"], 128)), (gb[:], all_rows(d["L2_attn_grep_b"], 8)),
                (ga[:], all_rows(d["L2_attn_grep_a_row"], nh))])
        project_tokens(k, q, h, 2, wq, 4, D, bias_rows=rb[:, 0, :])
        project_tokens(k, key, h, 2, wk, 4, D, bias_rows=rb[:, 1, :])
        project_tokens(k, val, h, 2, wv, 4, D, bias_rows=rb[:, 2, :])

        def heads(flat):
            return flat.rearrange("p (h x) -> p h x", h=nh)

        qq = k.sb(own, "qq", [P, 2, 2 * D])
        kk, vv = k.sb(own, "kk", [P, 2, 3 * D]), k.sb(own, "vv", [P, 2, 3 * D])

        def part(flat, n, i):
            return flat.rearrange("p (h n x) -> p h n x", h=nh, n=n)[:, :, i, :]

        with k.stage() as block:
            @block.vector
            def _(v):
                step = Steps(v, k.vec_step)
                step(nc.vector.reduce_sum(gws[:], gw[:], AX))
                step(nc.vector.reduce_sum(gbs[:], gb[:], AX))
                for t in range(4):
                    batch, tile = t // 2, t % 2
                    at = slice(batch * D, (batch + 1) * D)
                    for to, fr in ((qq, q), (kk, key), (vv, val)):
                        step(nc.vector.tensor_copy(to[:, tile, at], fr[:, t, :]))
                for tile in range(2):
                    for to, row in ((kk, 3), (vv, 4)):
                        step(nc.vector.tensor_copy(to[:, tile, 2 * D:3 * D], rb[:, row, :]))
                for t in range(4):
                    step(nc.vector.tensor_tensor(heads(prod[:]), part(qq[:, t % 2, :], 2, t // 2), gws[:].unsqueeze(1).broadcast_to([P, nh, dim]),
                                                 ALU.mult))
                    step(nc.vector.reduce_sum(gate[:, t, :], heads(prod[:]), AX))
                nc.vector.tensor_scalar(gate[:], gate[:], gbs[:], None, ALU.add).then_inc(k.vec_done, 1)
                v.wait_ge(k.act_done, 1)
                step(nc.vector.tensor_tensor(gate[:], gate[:], ga[:].unsqueeze(1).broadcast_to([P, 4, nh]), ALU.mult))
                for t in range(4):
                    for s in range(3):
                        step(nc.vector.tensor_tensor(heads(prod[:]), part(qq[:, t % 2, :], 2, t // 2), part(kk[:, t % 2, :], 3, s),
                                                     ALU.mult))
                        step(nc.vector.reduce_sum(mx[:, t, :], heads(prod[:]), AX))
                        step(nc.vector.tensor_tensor(sc[:, t, s, :], gate[:, t, :], rel[:, 3 * (t // 2) + s, :], ALU.mult))
                        step(nc.vector.scalar_tensor_tensor(out=sc[:, t, s, :], in0=mx[:, t, :], scalar=dim ** -0.5 / 32.0,
                                                            in1=sc[:, t, s, :], op0=ALU.mult, op1=ALU.add))
                step(nc.vector.tensor_tensor(mx[:], sc[:, :, 0, :], sc[:, :, 1, :], ALU.max))
                step(nc.vector.tensor_tensor(mx[:], mx[:], sc[:, :, 2, :], ALU.max))
                for s in range(3):
                    ins = nc.vector.tensor_tensor(sc[:, :, s, :], sc[:, :, s, :], mx[:], ALU.subtract)
                ins.then_inc(k.vec_done, 1)
                v.wait_ge(k.act_done, 2)
                step(nc.vector.tensor_tensor(mx[:], sc[:, :, 0, :], sc[:, :, 1, :], ALU.add))
                step(nc.vector.tensor_tensor(mx[:], mx[:], sc[:, :, 2, :], ALU.add))
                step(nc.vector.reciprocal(mx[:], mx[:]))
                for s in range(3):
                    step(nc.vector.tensor_tensor(sc[:, :, s, :], sc[:, :, s, :], mx[:], ALU.mult))
                for t in range(4):
                    for s in range(3):
                        to = o[:, t, :] if s == 0 else prod[:]
                        step(nc.vector.tensor_tensor(heads(to), part(vv[:, t % 2, :], 3, s), sc[:, t, s, :].unsqueeze(2).broadcast_to([P, nh, dim]),
                                                     ALU.mult))
                        if s:
                            step(nc.vector.tensor_tensor(o[:, t, :], o[:, t, :], prod[:], ALU.add))

            @block.scalar
            def _(act):
                act.wait_ge(k.vec_done, 1)
                nc.scalar.activation(gate[:], gate[:], ACT.Sigmoid).then_inc(k.act_done, 1)
                act.wait_ge(k.vec_done, 2)
                nc.scalar.activation(sc[:], sc[:], ACT.Exp).then_inc(k.act_done, 1)
        to_features(k, ot, o, 4, 2)
        project(k, x, ot, 2, wo, 2, T, vec=(k.vec("L2_attn_out_b"), ALU.add, x, ALU.add))


def to_features(k, dst, src, tiles, chunks):
    nc = k.nc
    with ExitStack() as own:
        ps = k.ps(own, "turn_ps", [P, chunks, 512])
        with k.stage() as block:
            @block.tensor
            def _(pe):
                for c in range(chunks):
                    for t in range(tiles):
                        mm = nc.tensor.transpose(ps[:, c, t * P:(t + 1) * P], src[:, t, c * P:(c + 1) * P], k.ident[:])
                mm.then_inc(k.products, 1)

            @block.scalar
            def _(act):
                act.wait_ge(k.products, 1)
                nc.scalar.activation(dst[:], ps[:, :, 0:tiles * P], ACT.Identity)


def l2_experts(k, x):
    nc, d = k.nc, k.d
    with ExitStack() as own:
        h = k.sb(own, "h", [P, 2, T])
        norm(k, h[:], x[:], T, 1e-5)
        s, bias = router(k, own, h, "L2_ffn_gate_w_t", "L2_ffn_gate_b")
        softmax8(k, s)
        top = k.sb(own, "top", [P, 4, 8])
        biased = k.sb(own, "biased", [P, 4, 8])
        w = k.sb(own, "w", [P, 4, 8])
        wt = k.sb(own, "wt", [8, T])
        with k.stage() as block:
            @block.vector
            def _(v):
                step = Steps(v, k.vec_step)
                step(nc.vector.tensor_tensor(biased[:], s[:], bias[:].unsqueeze(1).broadcast_to([P, 4, 8]), ALU.add))
                for t in range(4):
                    step(nc.vector.max(top[:, t, :], biased[:, t, :]))
                step(nc.vector.tensor_tensor(w[:], biased[:], top[:, :, 1:2].broadcast_to([P, 4, 8]), ALU.is_ge))
                nc.vector.tensor_tensor(w[:], w[:], s[:], ALU.mult)
        gates_by_expert(k, w, wt)
        store_gates(k, wt, 1.0)
        w1, w3 = k.sb(own, "w1", [P, 2, 512]), k.sb(own, "w3", [P, 2, 512])
        w2 = k.sb(own, "w2", [P, 2, D])
        bv = k.sb(own, "bv", [P, 10])
        gate = k.sb(own, "gate", [P, T])
        h1 = k.sb(own, "h1", [P, 4, T])
        sig = k.sb(own, "sig", [P, 2, T])
        a = k.sb(own, "a", [P, 2, T])
        y = k.sb(own, "y", [P, 2, T])
        ps = k.ps(own, "swi_ps", [P, 8, 512])
        with nc.Fori(0, 9) as e:
            with k.stage() as block:
                @block.sync
                def _(sp):
                    sp.dma_start(bv[:], d["L2_ffn_vecs"][e]).then_inc(k.loaded, 16)
                    sp.dma_start(w1[:], rows(d["L2_ffn_w1"][e])).then_inc(k.loaded, 16)
                    sp.dma_start(w3[:], rows(d["L2_ffn_w3"][e])).then_inc(k.loaded, 16)
                    sp.dma_start(w2[:], rows(d["L2_ffn_w2"][e])).then_inc(k.loaded, 16)
                    sp.dma_start(gate[:], d["gate_rows"][e].unsqueeze(0).broadcast_to([P, T])).then_inc(k.loaded, 16)

                @block.tensor
                def _(pe):
                    pe.wait_ge(k.loaded, 80)
                    for m in range(4):
                        for wi, w13 in enumerate((w1, w3)):
                            for c in range(2):
                                mm = nc.tensor.matmul(ps[:, 2 * m + wi, :], w13[:, c, m * P:(m + 1) * P], h[:, c, :],
                                                      start=(c == 0), stop=(c == 1))
                        mm.then_inc(k.products, 1)
                    pe.wait_ge(k.vec_done, 3)
                    for m in range(2):
                        for c in range(2):
                            mm = nc.tensor.matmul(ps[:, m, :], w2[:, c, m * P:(m + 1) * P], a[:, c, :],
                                                  start=(c == 0), stop=(c == 1))
                    mm.then_inc(k.products, 1)

                @block.scalar
                def _(act):
                    act.wait_ge(k.loaded, 80)
                    for m in range(4):
                        act.wait_ge(k.products, m + 1)
                        nc.scalar.activation(h1[:, m, :], ps[:, 2 * m, :], ACT.Identity, bias=bv[:, m:m + 1]).then_inc(k.act_done, 1)
                    act.wait_ge(k.vec_done, 2)
                    nc.scalar.activation(sig[:], h1[:, 0:2, :], ACT.Sigmoid, scale=1.702).then_inc(k.act_done, 1)

                @block.vector
                def _(v):
                    step = Steps(v, k.vec_step)
                    v.wait_ge(k.loaded, 80)
                    for m in range(4):
                        v.wait_ge(k.act_done, m + 1)
                        ins = nc.vector.scalar_tensor_tensor(out=h1[:, m, :], in0=ps[:, 2 * m + 1, :], scalar=bv[:, 4 + m:5 + m],
                                                             in1=h1[:, m, :], op0=ALU.add, op1=ALU.mult)
                        if m < 3:
                            step(ins)
                    ins.then_inc(k.vec_done, 1)
                    v.wait_ge(k.vec_done, 1)
                    nc.vector.tensor_scalar(h1[:, 0:2, :], h1[:, 0:2, :], 7.0, None, ALU.min).then_inc(k.vec_done, 1)
                    step(nc.vector.tensor_scalar(h1[:, 2:4, :], h1[:, 2:4, :], -7.0, 7.0, ALU.max, ALU.min))
                    v.wait_ge(k.vec_done, 2)
                    step(nc.vector.scalar_tensor_tensor(out=h1[:, 2:4, :], in0=h1[:, 2:4, :], scalar=1.0, in1=h1[:, 0:2, :],
                                                        op0=ALU.add, op1=ALU.mult))
                    v.wait_ge(k.act_done, 5)
                    nc.vector.tensor_tensor(a[:], h1[:, 2:4, :], sig[:], ALU.mult).then_inc(k.vec_done, 1)
                    v.wait_ge(k.products, 5)
                    for m in range(2):
                        step(nc.vector.scalar_tensor_tensor(out=y[:, m, :], in0=ps[:, m, :], scalar=bv[:, 8 + m:9 + m],
                                                            in1=gate[:], op0=ALU.add, op1=ALU.mult))
                    nc.vector.tensor_tensor(x[:], x[:], y[:], ALU.add)




def l3_cross(k, x):
    nc, d = k.nc, k.d
    hd = Heads(8, 64, 8.0)
    with ExitStack() as own:
        h = k.sb(own, "h", [P, 2, T])
        lat = k.sb(own, "lat", [P, 2, T])
        latb = k.sb(own, "latb", [P, 2, S])
        qb, kt = k.sb(own, "qb", [P, 4, S]), k.sb(own, "kt", [P, 4, KB])
        val = k.sb(own, "val", [P, 2, 512])
        ot = k.sb(own, "ot", [P, 4, T])
        wq, wkv, wo = k.sb(own, "wq", [P, 2, 512]), k.sb(own, "wkv", [P, 2, 1024]), k.sb(own, "wo", [P, 4, D])
        ctx, ctxn = k.sb(own, "ctx", [P, 2, KB]), k.sb(own, "ctxn", [P, 2, KB])
        raw = k.sb(own, "raw", [P, KB], mybir.dt.uint8)
        mask = k.sb(own, "mask", [P, 1, KB])
        st = attention_state(k, own, hd)
        wk, wv = wkv[:, :, 0:512], wkv[:, :, 512:1024]
        norm(k, h[:], x[:], T, 1e-5)
        norm(k, lat[:], h[:], T, 1e-5, w=k.vec("L3_xattn_ln_l_w"), b=k.vec("L3_xattn_ln_l_b"))
        load(k, [(wq[:], rows(d["L3_xattn_Wq"])), (wkv[:], rows(d["L3_xattn_Wkv"])), (wo[:], rows(d["L3_xattn_Wo"]))])
        with nc.Fori(0, B) as b:
            copy_batch(k, latb[:], lat, b)
            project(k, qb, latb, 2, wq, 4, S)
            unit_norm(k, qb[:], 4, S, k.vec("q_scale2"), k.head_ones[:])
            attention_start(k, st)
            with nc.Fori(0, SK // KB) as j:
                key_mask(k, mask[:, 0, :], d["mask_BxS2_bk0"][b, bass.ds(j * KB, KB)], raw[:])
                norm(k, ctxn[:], ctx[:], KB, 1e-5, w=k.vec("L3_xattn_ln_x_w"), b=k.vec("L3_xattn_ln_x_b"),
                     load_src=rows(d["ctx_t"][b])[:, :, bass.ds(j * KB, KB)])
                project(k, kt, ctxn, 2, wk, 4, KB)
                unit_norm(k, kt[:], 4, KB, k.vec("k_scale2"), k.head_ones[:])
                project_tokens(k, val, ctxn, 2, wv, 2, 512)
                attend(k, hd, st, qb, kt, val, mask)
            project(k, kt, latb, 2, wk, 4, KB)
            unit_norm(k, kt[:], 4, KB, k.vec("k_scale2"), k.head_ones[:])
            project_tokens(k, val, latb, 2, wv, 2, 512)
            attend(k, hd, st, qb, kt, val)
            attention_end(k, hd, st, ot, b)
        project(k, h, ot, 4, wo, 2, T)
        norm(k, x[:], h[:], T, 1e-5, w=k.vec("L3_xattn_ln_o_w"), b=k.vec("L3_xattn_ln_o_b"), plus=x)


def l3_self(k, x):
    nc, d = k.nc, k.d
    hd = Heads(16, 16, 0.25)
    with ExitStack() as own:
        h, hk, hv = (k.sb(own, n, [P, 2, T]) for n in ("h", "hk", "hv"))
        hb, hkb, hvb = (k.sb(own, n, [P, 2, S]) for n in ("hb", "hkb", "hvb"))
        qb, kt = k.sb(own, "qb", [P, 4, S]), k.sb(own, "kt", [P, 4, S])
        val = k.sb(own, "val", [P, 2, D])
        ot = k.sb(own, "ot", [P, 2, T])
        wk, wv, wl, wo = (k.sb(own, n, [P, 2, D]) for n in ("wk", "wv", "wl", "wo"))
        wq, wls = k.sb(own, "wq", [P, 2, 512]), k.sb(own, "wls", [P, 2, 512])
        st = attention_state(k, own, hd)
        norm(k, h[:], x[:], T, 1e-5)
        load(k, [(wk[:], rows(d["L3_attn_Wk"])), (wv[:], rows(d["L3_attn_Wv"])), (wl[:], rows(d["L3_attn_Wl"])),
                 (wo[:], rows(d["L3_attn_Wo"])), (wq[:], rows(d["L3_attn_Wq_strips"])), (wls[:], rows(d["L3_attn_Wl_strips"]))])
        project(k, hk, h, 2, wk, 2, T, bias=k.vec("L3_attn_bk"))
        project(k, hv, h, 2, wv, 2, T, bias=k.vec("L3_attn_bv"))
        with nc.Fori(0, B) as b:
            copy_batch(k, hb[:], h, b)
            copy_batch(k, hkb[:], hk, b)
            copy_batch(k, hvb[:], hv, b)
            project(k, qb, hb, 2, wq, 4, S, bias=k.vec("L3_attn_bq_strips"))
            project(k, kt, hkb, 2, wls, 4, S, bias=k.vec("L3_attn_bl_strips"))
            project_tokens(k, val, hvb, 2, wl, 2, D)
            attention_start(k, st)
            attend(k, hd, st, qb, kt, val)
            attention_end(k, hd, st, ot, b, bias=k.vec("L3_attn_bl"))
        project(k, x, ot, 2, wo, 2, T, vec=(k.vec("L3_attn_bo"), ALU.add, x, ALU.add))


def l3_experts(k, x):
    nc = k.nc
    capacity = int(S * 2.0 / 8) + 1
    with ExitStack() as own:
        h = k.sb(own, "h", [P, 2, T])
        norm(k, h[:], x[:], T, 1e-5)
        s, _ = router(k, own, h, "L3_ffn_router_w_t")
        softmax8(k, s)
        st = k.sb(own, "st", [8, T])
        gates_by_expert(k, s, st)
        work = k.sb(own, "work", [8, B, 2, S])
        top = k.sb(own, "top", [8, B, 8])
        wt = k.sb(own, "wt", [8, T])
        with k.stage() as block:
            @block.vector
            def _(v):
                step = Steps(v, k.vec_step)
                for b in range(B):
                    own_scores = st[:, b * S:(b + 1) * S]
                    src = own_scores
                    for r in range((capacity - 1) // 8):
                        step(nc.vector.max(top[:, b, :], src))
                        step(nc.vector.match_replace(work[:, b, r % 2, :], top[:, b, :], src, -1.0))
                        src = work[:, b, r % 2, :]
                    step(nc.vector.max(top[:, b, :], src))
                    last = (capacity - 1) % 8
                    step(nc.vector.tensor_scalar(wt[:, b * S:(b + 1) * S], own_scores, top[:, b, last:last + 1], None, ALU.is_ge))
                nc.vector.tensor_tensor(wt[:], wt[:], st[:], ALU.mult)
        store_gates(k, wt)
        experts_gelu(k, x, h, 8, "L3_ffn_w1", "L3_ffn_w2", "L3_ffn_vecs")


SUBLAYERS = [l0_cross, l0_scan, l0_experts, l1_cross, l1_self, l1_ffn, l2_cross, l2_self, l2_experts,
             l3_cross, l3_self, l3_experts]


def build(nc, d, out, sublayers=tuple(range(len(SUBLAYERS)))):
    with ExitStack() as ctx:
        k = Core(nc, d, ctx)
        x = k.sb(ctx, "x", [P, 2, T])
        k.vecs = k.sb(ctx, "vecs", [P, N_VECS])
        k.ident = k.sb(ctx, "ident", [P, P])
        k.mean_mat = k.sb(ctx, "mean_mat", [P, P])
        k.head_ones = k.sb(ctx, "head_ones", [P, P])
        k.cos, k.sin, k.iota = (k.sb(ctx, n, [P, S]) for n in ("cos", "sin", "iota"))
        k.causal = k.sb(ctx, "causal", [P, 2, S])
        load(k, [(x[:], rows(d["x_t"])), (k.vecs[:], d["vecs"]), (k.ident[:], d["const_ident"]),
                 (k.mean_mat[:], d["const_mean"]), (k.head_ones[:], d["const_head_ones"]), (k.cos[:], d["const_cos"]),
                 (k.sin[:], d["const_sin"]), (k.iota[:], d["const_iota"]), (k.causal[:], d["const_causal"])])
        for i in sublayers:
            SUBLAYERS[i](k, x)
        with nc.Block() as block:
            @block.sync
            def _(sp):
                sp.dma_start(rows(out), x[:]).then_inc(k.stored, 16)
                sp.wait_ge(k.stored, 16)




def strips(w):
    out = np.zeros(w.shape[:-1] + (16, 32), w.dtype)
    out[..., :16] = w.reshape(w.shape[:-1] + (16, 16))
    return out.reshape(w.shape[:-1] + (512,))


def turned(w):
    h = w.reshape(w.shape[:-1] + (16, 2, 8))
    return np.ascontiguousarray(h[..., ::-1, :]).reshape(w.shape)


def columns(v):
    return np.swapaxes(v.reshape(v.shape[:-1] + (-1, P)), -1, -2)


def constants():
    f = np.float32
    c = {"const_ident": np.eye(P, dtype=f), "const_mean": np.full((P, P), 1.0 / D, f),
         "const_head_ones": np.kron(np.eye(2), np.ones((64, 64))).astype(f),
         "const_iota": np.broadcast_to(np.arange(KB, dtype=f), (P, KB)).copy()}
    inv = 1.0 / 10000.0 ** (np.arange(0, 16, 2).astype(f) / f(16))
    ang = (np.arange(S, dtype=f)[:, None] * inv[None, :].astype(f)).astype(f)
    cos, sin = np.zeros((4, 32, S), f), np.zeros((4, 32, S), f)
    cos[:, 0:8], cos[:, 8:16] = np.cos(ang).T, np.cos(ang).T
    sin[:, 0:8], sin[:, 8:16] = -np.sin(ang).T, np.sin(ang).T
    c["const_cos"], c["const_sin"] = cos.reshape(P, S), sin.reshape(P, S)
    q = np.arange(S).reshape(2, P)
    c["const_causal"] = np.where(np.arange(S)[None, None, :] <= q.T[:, :, None], 0.0, NEG).astype(f)
    return c


def layouts(i):
    t = lambda a: np.swapaxes(a, -1, -2)
    cat = np.concatenate
    a = {"x_t": i["x"].transpose(2, 0, 1).reshape(D, T), "ctx_t": i["ctx_1024"].transpose(0, 2, 1),
         "mask_BxS2_ik1": i["mask_BxS2_ik1"], "mask_BxS2_bk0": i["mask_BxS2_bk0"],
         "seg_cols": i["itok_BxS_0_255"].reshape(B, 2, P).transpose(0, 2, 1)}
    for n in ("q", "k"):
        a[f"L0_xattn_W{n}_strips"] = strips(i[f"L0_xattn_W{n}"])
    for n in ("L0_xattn_Wv", "L0_xattn_Wo", "L0_ffn_gate_bias", "L1_attn_w_o", "L2_attn_q_w", "L2_attn_k_w", "L2_attn_v_w",
              "L2_attn_out_w", "L2_attn_q_b", "L2_attn_k_b", "L2_attn_v_b", "L2_attn_rel_emb", "L2_attn_grep_b", "L2_ffn_gate_b",
              "L3_xattn_Wq", "L3_xattn_Wkv", "L3_xattn_Wo", "L3_attn_Wk", "L3_attn_Wv", "L3_attn_Wl", "L3_attn_Wo",
              "L3_ffn_w1", "L3_ffn_w2"):
        a[n] = i[n]
    for n in ("L0_attn_w_in", "L0_attn_w_out", "L0_attn_w_dt", "L0_ffn_gate_w", "L1_xattn_Wk", "L1_xattn_Wv", "L1_xattn_Wq",
              "L1_xattn_Wo", "L2_ffn_gate_w", "L3_ffn_router_w"):
        a[n + "_t"] = t(i[n])
    a["L0_attn_w_xproj_t"] = cat([t(i["L0_attn_w_xproj"]), np.zeros((512, 32), np.float32)], 1)
    a["L0_ffn_up"] = t(cat([i["L0_ffn_Wu"], i["L0_ffn_sWu"][None]]))
    a["L0_ffn_down"] = t(cat([i["L0_ffn_Wd"], i["L0_ffn_sWd"][None]]))
    a["L0_ffn_vecs"] = columns(cat([cat([i["L0_ffn_bu"], i["L0_ffn_sbu"][None]]), cat([i["L0_ffn_bd"], i["L0_ffn_sbd"][None]])], 1))
    for n in "qkv":
        a[f"L1_attn_w_{n}_t"] = i[f"L1_attn_w_{n}"].transpose(1, 0, 2).reshape(D, 1024)
    for n in ("w1", "w2", "h1", "h2", "w3"):
        a[f"L1_ffn_{n}_t"] = t(i[f"L1_ffn_{n}_w"])
    wqkv, bqkv = t(i["L2_xattn_Wqkv"]), i["L2_xattn_bqkv"]
    a["L2_qk_strips"] = cat([strips(wqkv[..., 0:D]), strips(turned(wqkv[..., 0:D])),
                             strips(wqkv[..., D:2 * D]), strips(turned(wqkv[..., D:2 * D]))], -1)
    a["L2_wv"], a["L2_wo"] = wqkv[..., 2 * D:], t(i["L2_xattn_Wo"])
    a["L2_qc_strips"] = strips(t(i["L2_xattn_Wq_c"]))
    a["L2_kc_strips"] = strips(t(i["L2_xattn_Wkv_c"][:, 0:D]))
    a["L2_wvc"], a["L2_woc"] = t(i["L2_xattn_Wkv_c"][:, D:]), t(i["L2_xattn_Wo_c"])
    a["L2_wg"], a["L2_wu"], a["L2_wd"] = t(i["L2_xattn_Wg"]), t(i["L2_xattn_Wu"]), t(i["L2_xattn_Wd"])
    a["L2_vecs"] = columns(cat([strips(bqkv[:, 0:D]), strips(turned(bqkv[:, 0:D])), strips(bqkv[:, D:2 * D]),
                                strips(turned(bqkv[:, D:2 * D])), bqkv[:, 2 * D:], i["L2_xattn_bo"], i["L2_xattn_n1"],
                                i["L2_xattn_n2"], i["L2_xattn_n3"]], 1))
    a["L2_attn_bias_k_row"], a["L2_attn_bias_v_row"] = i["L2_attn_bias_k"].reshape(D), i["L2_attn_bias_v"].reshape(D)
    a["L2_attn_grep_w_row"], a["L2_attn_grep_a_row"] = i["L2_attn_grep_w"].reshape(128), i["L2_attn_grep_a"].reshape(16)
    halves = lambda w: cat([w[:, 0::2], w[:, 1::2]], 1)
    for n in ("1", "3"):
        a[f"L2_ffn_w{n}"] = t(halves(cat([i[f"L2_ffn_w{n}"], i[f"L2_ffn_sw{n}"][None]])))
    a["L2_ffn_w2"] = t(cat([i["L2_ffn_w2"], i["L2_ffn_sw2"][None]]))
    a["L2_ffn_vecs"] = columns(cat([halves(cat([i["L2_ffn_b1"], i["L2_ffn_sb1"][None]])),
                                    halves(cat([i["L2_ffn_b3"], i["L2_ffn_sb3"][None]])),
                                    cat([i["L2_ffn_b2"], i["L2_ffn_sb2"][None]])], 1))
    a["L3_attn_Wq_strips"], a["L3_attn_Wl_strips"] = strips(i["L3_attn_Wq"]), strips(i["L3_attn_Wl"])
    a["L3_ffn_vecs"] = columns(cat([i["L3_ffn_b1"], i["L3_ffn_b2"]], 1))
    conv = i["L0_attn_w_conv"].reshape(4, P, 4).transpose(1, 0, 2).reshape(P, 16)
    a_log = i["L0_attn_A_log"].reshape(4, P, 16).transpose(1, 2, 0).reshape(P, 64)
    own = {"q_scale2": np.tile(i["L3_xattn_q_scale"], 2)[:, None], "k_scale2": np.tile(i["L3_xattn_k_scale"], 2)[:, None],
           "conv": conv, "A_log": a_log, "L3_attn_bq_strips": columns(strips(i["L3_attn_bq"])),
           "L3_attn_bl_strips": columns(strips(i["L3_attn_bl"]))}
    a["vecs"] = cat([own[n] if n in own else columns(i[n]) for n, _ in VECS], 1)
    return {n: np.ascontiguousarray(v) for n, v in a.items()}


def kernel(**inputs):
    import concourse.bacc as bacc
    from concourse.bass_utils import run_bass_kernel_spmd

    arrays = {**layouts({n: np.asarray(v) for n, v in inputs.items()}), **constants()}
    nc = bacc.Bacc("TRN2", target_bir_lowering=False, num_devices=1)
    d = {n: nc.dram_tensor(n, v.shape, mybir.dt.from_np(v.dtype), kind="ExternalInput").ap() for n, v in arrays.items()}
    for name, shape in (("bc_rows", (32, T)), ("gate_rows", (9, T))):
        d[name] = nc.dram_tensor(name, shape, F32, kind="Internal").ap()
    out = nc.dram_tensor("out_t", (D, T), F32, kind="ExternalOutput").ap()
    build(nc, d, out)
    r = run_bass_kernel_spmd(nc, [arrays], core_ids=[0])
    return np.ascontiguousarray(r.results[0]["out_t"].reshape(D, B, S).transpose(1, 2, 0))
```

```python
from contextlib import ExitStack, contextmanager

import concourse.bass as bass
import numpy as np
from concourse import mybir

P = 128
D = 256
B = 2
S = 256
T = B * S
SK = 4096
KB = 256
F32 = mybir.dt.float32
BF16 = mybir.dt.bfloat16
ACT = mybir.ActivationFunctionType
ALU = mybir.AluOpType
AX = mybir.AxisListType.X
NEG = -1e30
START_MAX = -1e31

VECS = [("L0_attn_b_dt", 4), ("L0_attn_D", 4), ("L1_xattn_bv", 2), ("L1_xattn_bq", 2), ("L1_xattn_bo", 2),
        ("L1_ffn_w1_s", 8), ("L1_ffn_w2_s", 8), ("L1_ffn_h1_s", 8), ("L1_ffn_h2_s", 8), ("L1_ffn_w3_s", 2),
        ("L2_xattn_nf", 2), ("L2_attn_out_b", 2), ("L3_xattn_ln_x_w", 2), ("L3_xattn_ln_x_b", 2),
        ("L3_xattn_ln_l_w", 2), ("L3_xattn_ln_l_b", 2), ("q_scale2", 1), ("k_scale2", 1),
        ("L3_xattn_ln_o_w", 2), ("L3_xattn_ln_o_b", 2), ("L3_attn_bq_strips", 4), ("L3_attn_bk", 2),
        ("L3_attn_bv", 2), ("L3_attn_bl_strips", 4), ("L3_attn_bl", 2), ("L3_attn_bo", 2), ("conv", 16),
        ("A_log", 64)]
VEC_AT, _n = {}, 0
for _name, _c in VECS:
    VEC_AT[_name] = (_n, _n + _c)
    _n += _c
N_VECS = _n

LAYER_VECS = {"bq": (0, 4), "bq_turned": (4, 8), "bk": (8, 12), "bk_turned": (12, 16), "bv": (16, 18),
              "bo": (18, 20), "n1": (20, 22), "n2": (22, 24), "n3": (24, 26)}

SEMS = ["loaded", "stored", "products", "act_done", "vec_done", "vec_step", "evacuated", "pool_done",
        "scored", "shifted", "exps", "turned", "unturned", "weighted", "merged", "loaded_next", "ring_0", "ring_1", "ring_2",
        "ring_3", "values_0", "values_1"]


class Core:

    def __init__(self, nc, d, ctx):
        self.nc, self.d, self.ctx, self.count = nc, d, ctx, 0
        self.sems = [ctx.enter_context(nc.semaphore(n)) for n in SEMS]
        (self.loaded, self.stored, self.products, self.act_done, self.vec_done, self.vec_step, self.evacuated,
         self.pool_done, self.scored, self.shifted, self.exps, self.turned, self.unturned, self.weighted,
         self.merged, self.loaded_next, *others) = self.sems
        self.ring_in, self.values_in = others[0:4], others[4:6]
        nums = [s.num for s in self.sems]
        assert nums == list(range(nums[0], nums[0] + len(nums)))
        self.sem_range = range(nums[0], nums[0] + len(nums))

    def name(self, what):
        self.count += 1
        return f"{what}_{self.count}"

    def sb(self, stack, what, shape, dt=F32):
        return stack.enter_context(self.nc.sbuf_tensor(self.name(what), shape, dt))

    def ps(self, stack, what, shape, dt=F32):
        return stack.enter_context(self.nc.psum_tensor(self.name(what), shape, dt))

    @contextmanager
    def stage(self):
        with self.nc.Block() as block:
            yield block
        self.nc.sync.sem_clear(self.sem_range)
        self.nc.all_engine_barrier()

    def vec(self, name):
        a, b = VEC_AT[name]
        return self.vecs[:, a:b]


class Steps:

    def __init__(self, eng, sem):
        self.eng, self.sem, self.n = eng, sem, 0

    def __call__(self, instruction):
        instruction.then_inc(self.sem, 1)
        self.n += 1
        self.eng.wait_ge(self.sem, self.n)


def rows(w):
    return w.rearrange("(c p) m -> p c m", p=P)


def load(k, pairs):
    with k.stage() as block:
        @block.sync
        def _(sp):
            for dst, src in pairs:
                sp.dma_start(dst, src).then_inc(k.loaded, 16)
            sp.wait_ge(k.loaded, 16 * len(pairs))


def project(k, dst, src, kc, w, mc, n, loads=(), func=ACT.Identity, bias=None, scale=1.0, vec=None):
    nc = k.nc
    with ExitStack() as own:
        ps = k.ps(own, "proj_ps", [P, 4, 512])
        with k.stage() as block:
            @block.sync
            def _(sp):
                for to, fr in loads:
                    sp.dma_start(to, fr).then_inc(k.loaded, 16)

            @block.tensor
            def _(pe):
                if loads:
                    pe.wait_ge(k.loaded, 16 * len(loads))
                for m in range(mc):
                    if m >= 4:
                        pe.wait_ge(k.evacuated, m - 3)
                    for c in range(kc):
                        mm = nc.tensor.matmul(ps[:, m % 4, 0:n], w[:, c, m * P:(m + 1) * P], src[:, c, :],
                                              start=(c == 0), stop=(c == kc - 1))
                    mm.then_inc(k.products, 1)

            @block.scalar
            def _(act):
                if vec is None:
                    if loads:
                        act.wait_ge(k.loaded, 16 * len(loads))
                    for m in range(mc):
                        act.wait_ge(k.products, m + 1)
                        nc.scalar.activation(
                            dst[:, m, :], ps[:, m % 4, 0:n], func,
                            bias=0.0 if bias is None else bias[:, m:m + 1],
                            scale=scale if isinstance(scale, float) else scale[:, m:m + 1],
                        ).then_inc(k.evacuated, 1)

            @block.vector
            def _(v):
                if vec is not None:
                    col, op0, other, op1 = vec
                    if loads:
                        v.wait_ge(k.loaded, 16 * len(loads))
                    for m in range(mc):
                        v.wait_ge(k.products, m + 1)
                        nc.vector.scalar_tensor_tensor(
                            out=dst[:, m, :], in0=ps[:, m % 4, 0:n],
                            scalar=col if isinstance(col, float) else col[:, m:m + 1],
                            in1=other[:, m, :], op0=op0, op1=op1).then_inc(k.evacuated, 1)


def project_tokens(k, dst, src, kc, w, tiles, nf, loads=(), bias_rows=None):
    nc = k.nc
    nb = (nf + 511) // 512
    fb = nf // nb
    with ExitStack() as own:
        ps = k.ps(own, "tok_ps", [P, 4, 512])
        with k.stage() as block:
            @block.sync
            def _(sp):
                for to, fr in loads:
                    sp.dma_start(to, fr).then_inc(k.loaded, 16)

            @block.tensor
            def _(pe):
                if loads:
                    pe.wait_ge(k.loaded, 16 * len(loads))
                i = 0
                for t in range(tiles):
                    for f in range(nb):
                        if i >= 4:
                            pe.wait_ge(k.evacuated, i - 3)
                        for c in range(kc):
                            mm = nc.tensor.matmul(ps[:, i % 4, 0:fb], src[:, c, t * P:(t + 1) * P],
                                                  w[:, c, f * fb:(f + 1) * fb], start=(c == 0), stop=(c == kc - 1))
                        mm.then_inc(k.products, 1)
                        i += 1

            @block.scalar
            def _(act):
                if bias_rows is None:
                    for i in range(tiles * nb):
                        act.wait_ge(k.products, i + 1)
                        nc.scalar.activation(dst[:, i // nb, (i % nb) * fb:(i % nb + 1) * fb], ps[:, i % 4, 0:fb],
                                             ACT.Identity).then_inc(k.evacuated, 1)

            @block.vector
            def _(v):
                if bias_rows is not None:
                    if loads:
                        v.wait_ge(k.loaded, 16 * len(loads))
                    for i in range(tiles * nb):
                        v.wait_ge(k.products, i + 1)
                        nc.vector.tensor_tensor(dst[:, i // nb, (i % nb) * fb:(i % nb + 1) * fb], ps[:, i % 4, 0:fb],
                                                bias_rows[:, (i % nb) * fb:(i % nb + 1) * fb],
                                                ALU.add).then_inc(k.evacuated, 1)


def norm(k, dst, src, n, eps, mean=True, w=None, b=None, plus=None, load_src=None):
    nc = k.nc
    with ExitStack() as own:
        ps = k.ps(own, "norm_ps", [P, 2, 512])
        centred = k.sb(own, "centred", [P, 2, n])
        squares = k.sb(own, "squares", [P, 2, n])
        stat = k.sb(own, "stat", [P, 2, n])
        cen = centred if mean else src
        with k.stage() as block:
            @block.sync
            def _(sp):
                if load_src is not None:
                    sp.dma_start(src, load_src).then_inc(k.loaded, 16)

            @block.tensor
            def _(pe):
                if load_src is not None:
                    pe.wait_ge(k.loaded, 16)
                if mean:
                    for c in range(2):
                        mm = nc.tensor.matmul(ps[:, 0, 0:n], k.mean_mat[:], src[:, c, :], start=(c == 0), stop=(c == 1))
                    mm.then_inc(k.products, 1)
                pe.wait_ge(k.vec_done, 1)
                for c in range(2):
                    mm = nc.tensor.matmul(ps[:, 1, 0:n], k.mean_mat[:], squares[:, c, :], start=(c == 0), stop=(c == 1))
                mm.then_inc(k.products, 1)

            @block.scalar
            def _(act):
                act.wait_ge(k.vec_done, 2)
                nc.scalar.activation(stat[:, 1, :], stat[:, 0, :], ACT.Sqrt).then_inc(k.act_done, 1)

            @block.vector
            def _(v):
                step = Steps(v, k.vec_step)
                if load_src is not None:
                    v.wait_ge(k.loaded, 16)
                if mean:
                    v.wait_ge(k.products, 1)
                    step(nc.vector.tensor_tensor(centred[:], src, ps[:, 0, 0:n].unsqueeze(1).broadcast_to([P, 2, n]),
                                                 ALU.subtract))
                nc.vector.tensor_tensor(squares[:], cen[:, :, :], cen[:, :, :], ALU.mult).then_inc(k.vec_done, 1)
                v.wait_ge(k.products, 2 if mean else 1)
                nc.vector.tensor_scalar(stat[:, 0, :], ps[:, 1, 0:n], eps, None, ALU.add).then_inc(k.vec_done, 1)
                v.wait_ge(k.act_done, 1)
                step(nc.vector.reciprocal(stat[:, 0, :], stat[:, 1, :]))
                scaled = squares if plus is not None or w is not None else dst
                step(nc.vector.tensor_tensor(scaled[:, :, :], cen[:, :, :], stat[:, 0, :].unsqueeze(1).broadcast_to([P, 2, n]),
                                             ALU.mult))
                if w is not None:
                    for c in range(2):
                        if plus is not None:
                            step(nc.vector.scalar_tensor_tensor(out=dst[:, c, :], in0=squares[:, c, :], scalar=w[:, c:c + 1],
                                                                in1=plus[:, c, :], op0=ALU.mult, op1=ALU.add))
                            if b is not None:
                                step(nc.vector.tensor_scalar(dst[:, c, :], dst[:, c, :], b[:, c:c + 1], None, ALU.add))
                        elif b is not None:
                            step(nc.vector.tensor_scalar(dst[:, c, :], squares[:, c, :], w[:, c:c + 1], b[:, c:c + 1],
                                                         ALU.mult, ALU.add))
                        else:
                            step(nc.vector.tensor_scalar(dst[:, c, :], squares[:, c, :], w[:, c:c + 1], None, ALU.mult))


def copy_batch(k, dst, src, b):
    with k.stage() as block:
        @block.vector
        def _(v):
            k.nc.vector.tensor_copy(dst, src[:, :, bass.ds(b * S, S)])


def unit_norm(k, t, chunks, n, scale, ones_blocks):
    nc = k.nc
    with ExitStack() as own:
        ps = k.ps(own, "len_ps", [P, chunks, 512])
        sq = k.sb(own, "len_sq", [P, chunks, n])
        ln = k.sb(own, "len_root", [P, chunks, n])
        with k.stage() as block:
            @block.vector
            def _(v):
                step = Steps(v, k.vec_step)
                nc.vector.tensor_tensor(sq[:], t, t, ALU.mult).then_inc(k.vec_done, 1)
                v.wait_ge(k.act_done, 1)
                step(nc.vector.tensor_scalar(ln[:], ln[:], 1e-12, None, ALU.max))
                step(nc.vector.reciprocal(ln[:], ln[:]))
                step(nc.vector.tensor_tensor(ln[:], ln[:], t, ALU.mult))
                nc.vector.tensor_scalar(t, ln[:], scale, None, ALU.mult)

            @block.tensor
            def _(pe):
                pe.wait_ge(k.vec_done, 1)
                for c in range(chunks):
                    mm = nc.tensor.matmul(ps[:, c, 0:n], ones_blocks, sq[:, c, :], start=True, stop=True)
                mm.then_inc(k.products, 1)

            @block.scalar
            def _(act):
                act.wait_ge(k.products, 1)
                nc.scalar.activation(ln[:], ps[:, :, 0:n], ACT.Sqrt).then_inc(k.act_done, 1)


def rope(k, t, turned):
    nc = k.nc
    with k.stage() as block:
        @block.vector
        def _(v):
            step = Steps(v, k.vec_step)
            step(nc.vector.tensor_tensor(t[:], t[:], k.cos[:].unsqueeze(1).broadcast_to([P, 4, S]), ALU.mult))
            step(nc.vector.tensor_tensor(turned[:], turned[:], k.sin[:].unsqueeze(1).broadcast_to([P, 4, S]), ALU.mult))
            nc.vector.tensor_tensor(t[:], t[:], turned[:], ALU.add)


class Heads:

    def __init__(self, n, dim, scale):
        self.n, self.dim, self.scale = n, dim, scale
        self.wide = max(1, dim // P)
        self.rows = {16: 32, 64: 64, 256: P}[dim]
        self.places = P // self.rows
        self.chunks = n * self.wide // self.places
        self.per = min(4, n // self.places)
        self.groups = [(place, c0) for place in range(self.places)
                       for c0 in range(0, n // self.places, self.per)]

    def members(self, group):
        place, c0 = group
        return [(c, c * self.places + place) for c in range(c0, c0 + self.per)]

    def of_group(self, flat, group):
        place, c0 = group
        return flat.rearrange("p (c s x) -> p c s x", s=self.places, c=self.n // self.places)[:, c0:c0 + self.per, place, :]


def attention_state(k, own, hd):
    return {"o": k.sb(own, "att_o", [P, 2, hd.n * hd.dim]), "m": k.sb(own, "att_m", [P, 2, hd.n]),
            "l": k.sb(own, "att_l", [P, 2, hd.n])}


def attention_start(k, st):
    with k.stage() as block:
        @block.vector
        def _(v):
            k.nc.vector.memset(st["o"][:], 0.0)
            k.nc.vector.memset(st["m"][:], START_MAX)
            k.nc.vector.memset(st["l"][:], 0.0)


def attend(k, hd, st, q, kt, val, mask=None, mask_by_query=False):
    nc = k.nc
    units = [(qt, g) for qt in range(2) for g in hd.groups]
    per, dim = hd.per, hd.dim
    nu = len(units)
    with ExitStack() as own:
        score_ps = k.ps(own, "score_ps", [P, 2, 4, KB])
        turn_ps = k.ps(own, "turn_ps", [P, 8, P])
        out_ps = k.ps(own, "out_ps", [P, 2, 512])
        masked = k.sb(own, "masked", [P, per, KB]) if mask is not None else None
        prob = k.sb(own, "prob", [P, 2, per, KB])
        prob_t = k.sb(own, "prob_t", [P, 2, per * 2, P])
        top = k.sb(own, "top", [P, 2, per])
        new_max = k.sb(own, "new_max", [P, 2, per])
        drop = k.sb(own, "drop", [P, 2, per])
        fade = k.sb(own, "fade", [P, 2, per])
        part = k.sb(own, "part", [P, 2, per])
        with k.stage() as block:
            @block.tensor
            def _(pe):
                def scores(u):
                    qt, g = units[u]
                    if u >= 2:
                        pe.wait_ge(k.shifted, u - 1)
                    for i, (c, _) in enumerate(hd.members(g)):
                        p0 = g[0] * hd.rows
                        for w in range(hd.wide):
                            mm = nc.tensor.matmul(
                                score_ps[:, u % 2, i, :], q[p0:p0 + hd.rows, c * hd.wide + w, qt * P:(qt + 1) * P],
                                kt[p0:p0 + hd.rows, c * hd.wide + w, :], start=(w == 0), stop=(w == hd.wide - 1))
                    mm.then_inc(k.scored, 1)

                def values(u):
                    _, g = units[u]
                    pe.wait_ge(k.exps, u + 1)
                    if u >= 1:
                        pe.wait_ge(k.unturned, u)
                    for i in range(per):
                        for c in range(2):
                            mm = nc.tensor.transpose(turn_ps[:, 2 * i + c, :], prob[:, u % 2, i, c * P:(c + 1) * P], k.ident[:])
                    mm.then_inc(k.turned, 1)
                    pe.wait_ge(k.unturned, u + 1)
                    if u >= 2:
                        pe.wait_ge(k.merged, u - 1)
                    for i, (_, h) in enumerate(hd.members(g)):
                        for c in range(2):
                            mm = nc.tensor.matmul(out_ps[:, u % 2, i * dim:(i + 1) * dim], prob_t[:, u % 2, 2 * i + c, :],
                                                  val[:, c, h * dim:(h + 1) * dim], start=(c == 0), stop=(c == 1))
                    mm.then_inc(k.weighted, 1)

                for u in range(nu + 1):
                    if u < nu:
                        scores(u)
                    if u >= 1:
                        values(u - 1)

            @block.scalar
            def _(act):
                for u in range(nu + 1):
                    if u < nu:
                        act.wait_ge(k.shifted, u + 1)
                        nc.scalar.activation(fade[:, u % 2, :], drop[:, u % 2, :], ACT.Exp, scale=hd.scale)
                        nc.scalar.activation(prob[:, u % 2], prob[:, u % 2], ACT.Exp, scale=hd.scale).then_inc(k.exps, 1)
                    if u >= 1:
                        act.wait_ge(k.turned, u)
                        if u >= 3:
                            act.wait_ge(k.weighted, u - 2)
                        nc.scalar.activation(prob_t[:, (u - 1) % 2], turn_ps[:, 0:2 * per, :],
                                             ACT.Identity).then_inc(k.unturned, 1)

            @block.vector
            def _(v):
                step = Steps(v, k.vec_step)

                def maxima(u):
                    qt, g = units[u]
                    j = u % 2
                    m = hd.of_group(st["m"][:, qt, :], g)[:, :, 0]
                    v.wait_ge(k.scored, u + 1)
                    src = score_ps[:, j, 0:per, :]
                    if mask is not None:
                        rows_mask = mask[:, qt if mask_by_query else 0, :]
                        if u >= 1:
                            v.wait_ge(k.shifted, u)
                        step(nc.vector.tensor_tensor(masked[:], src, rows_mask.unsqueeze(1).broadcast_to([P, per, KB]), ALU.add))
                        src = masked[:]
                    step(nc.vector.tensor_reduce(top[:, j, :], src, AX, ALU.max))
                    step(nc.vector.tensor_tensor(new_max[:, j, :], m, top[:, j, :], ALU.max))
                    if u >= 2:
                        v.wait_ge(k.turned, u - 1)
                    step(nc.vector.tensor_tensor(drop[:, j, :], m, new_max[:, j, :], ALU.subtract))
                    step(nc.vector.tensor_copy(m, new_max[:, j, :]))
                    nc.vector.tensor_tensor(prob[:, j], src, new_max[:, j, :].unsqueeze(2).broadcast_to([P, per, KB]),
                                            ALU.subtract).then_inc(k.shifted, 1)

                def merge(u):
                    qt, g = units[u]
                    j = u % 2
                    l = hd.of_group(st["l"][:, qt, :], g)[:, :, 0]
                    o = hd.of_group(st["o"][:, qt, :], g)
                    v.wait_ge(k.exps, u + 1)
                    step(nc.vector.reduce_sum(part[:, j, :], prob[:, j], AX))
                    step(nc.vector.tensor_tensor(l, l, fade[:, j, :], ALU.mult))
                    step(nc.vector.tensor_tensor(l, l, part[:, j, :], ALU.add))
                    step(nc.vector.tensor_tensor(o, o, fade[:, j, :].unsqueeze(2).broadcast_to([P, per, dim]), ALU.mult))
                    v.wait_ge(k.weighted, u + 1)
                    nc.vector.tensor_tensor(o, o, out_ps[:, j, 0:per * dim].rearrange("p (a x) -> p a x", a=per),
                                            ALU.add).then_inc(k.merged, 1)
                    v.wait_ge(k.merged, u + 1)

                for u in range(nu + 1):
                    if u < nu:
                        maxima(u)
                    if u >= 1:
                        merge(u - 1)


def attention_end(k, hd, st, dst, b, bias=None):
    nc = k.nc
    nf = hd.n * hd.dim
    with ExitStack() as own:
        ps = k.ps(own, "end_ps", [P, 4, 512])
        with k.stage() as block:
            @block.vector
            def _(v):
                step = Steps(v, k.vec_step)
                step(nc.vector.reciprocal(st["l"][:], st["l"][:]))
                for qt in range(2):
                    o = st["o"][:, qt, :].rearrange("p (h x) -> p h x", h=hd.n)
                    nc.vector.tensor_tensor(o, o, st["l"][:, qt, :].unsqueeze(2).broadcast_to([P, hd.n, hd.dim]),
                                            ALU.mult).then_inc(k.vec_done, 1)

            @block.tensor
            def _(pe):
                pe.wait_ge(k.vec_done, 2)
                for c in range(nf // P):
                    if c >= 4:
                        pe.wait_ge(k.evacuated, c - 3)
                    for qt in range(2):
                        mm = nc.tensor.transpose(ps[:, c % 4, qt * P:(qt + 1) * P], st["o"][:, qt, c * P:(c + 1) * P], k.ident[:])
                    mm.then_inc(k.products, 1)

            @block.scalar
            def _(act):
                for c in range(nf // P):
                    act.wait_ge(k.products, c + 1)
                    nc.scalar.activation(dst[:, c, bass.ds(b * S, S)], ps[:, c % 4, 0:S], ACT.Identity,
                                         bias=0.0 if bias is None else bias[:, c:c + 1]).then_inc(k.evacuated, 1)


def key_mask(k, dst, src_row, raw):
    with k.stage() as block:
        @block.sync
        def _(sp):
            sp.dma_start(raw, src_row.unsqueeze(0).broadcast_to([P, KB])).then_inc(k.loaded, 16)

        @block.vector
        def _(v):
            v.wait_ge(k.loaded, 16)
            k.nc.vector.tensor_scalar(dst, raw, 0.0, NEG, ALU.is_equal, ALU.mult)


class Streamed:

    def __init__(self, n, dim, keys, scale, split, masked=True):
        self.n, self.dim, self.keys, self.scale, self.split = n, dim, keys, scale, split
        self.dt = BF16 if split else F32
        self.rows = 6 * dim if split else dim
        self.rows_a = self.rows + 1
        self.max_rows = 2 if split else 1
        self.blocks = [(qt, j, min(512, keys - j)) for qt in range(2) for j in range(0, keys, 512)]
        chunks = keys // P
        self.groups = [(c, min(4, chunks - c)) for c in range(0, chunks, 4)]
        self.chunks = chunks
        self.strips = dim < 32
        self.columns = 32 if self.strips else dim + 1
        self.out_rows = P if self.strips else dim + 1
        self.max_at = self.rows_a if split else 96
        self.depth_a = self.max_at
        self.depth_b = self.max_at + self.max_rows


RING = 4


def heads_turns(k, sa, bufs, i, first, last, b):
    nc, d = k.nc, k.d
    kst, qst, vh, val, prob, o, acc, fold, small = bufs
    part, top, parts, parts_t, inv = small
    turns = [] if first else list(range(RING))
    ahead = [0] if first else [t + 1 for t in turns if not (last and t == RING - 1)]
    loads = [0, 1] if first else [t + 2 for t in turns if not (last and t >= RING - 2)]
    load_done = 16 * n_loads(sa)
    nb, ng = len(sa.blocks), len(sa.groups)
    dim1 = sa.dim + 1
    base = 0 if first else i * RING
    with ExitStack() as own:
        ps_a = k.ps(own, "ps_a", [P, 2, 512])
        ps_b = k.ps(own, "ps_b", [P, 2, 4, S])
        ps_o = k.ps(own, "ps_o", [P, 512])
        ps_f = k.ps(own, "ps_f", [P, 512])
        with k.stage() as block:
            @block.sync
            def _(sp):
                def fetch(h):
                    if not first and h >= RING:
                        sp.wait_ge(k.products, (h - RING + 1) * ng)
                    load_head(k, sp, sa, kst, qst, h % RING, base + h, b)

                def max_rows(n, h):
                    sp.wait_ge(k.vec_done, n + 1)
                    for qt in range(2):
                        for j in range(sa.max_rows):
                            sp.dma_start(qst[sa.max_at + j:sa.max_at + j + 1, h % RING, qt * P:(qt + 1) * P],
                                         parts_t[2 * qt + j:2 * qt + j + 97:32, :]).then_inc(k.stored, 16)

                def fetch_values(h):
                    if h >= 2:
                        sp.wait_ge(k.weighted, (h - 1) * ng)
                    sp.dma_start(vh[:, h % 2, :, 0:sa.dim],
                                 d["v_full"].rearrange("(c p) f -> p c f", p=P)[:, :, bass.ds((base + h) * sa.dim, sa.dim)])\
                        .then_inc(k.values_in[h % 2], 16)

                if first:
                    for h in loads:
                        fetch(h)
                    if val is None:
                        fetch_values(0)
                    max_rows(0, 0)
                for t in turns:
                    if t + 2 in loads:
                        fetch(t + 2)
                    if t + 1 in ahead:
                        if val is None:
                            fetch_values(t + 1)
                        max_rows(t, t + 1)
                if ahead and val is None:
                    for h in ahead[-2:]:
                        sp.wait_ge(k.values_in[h % 2], 16 * len([a for a in ahead if a % 2 == h % 2]))
                if ahead:
                    sp.wait_ge(k.stored, 32 * sa.max_rows * len(ahead))
                for h in loads:
                    sp.wait_ge(k.ring_in[h % RING], load_done)

            @block.gpsimd
            def _(pool):
                for t in turns if val is not None else []:
                    if t >= 2:
                        pool.wait_ge(k.weighted, (t - 1) * ng)
                    nc.gpsimd.tensor_copy(vh[:, t % 2, :, 0:dim1], val[:, :, bass.ds((base + t) * dim1, dim1)])\
                        .then_inc(k.pool_done, 1)

            @block.tensor
            def _(pe):
                def pass_a(h, n, j):
                    qt, at, size = sa.blocks[j]
                    if j == 0 and h in loads:
                        pe.wait_ge(k.ring_in[h % RING], load_done)
                    e = n * nb + j
                    if e >= 2:
                        pe.wait_ge(k.shifted, e - 1)
                    nc.tensor.matmul(ps_a[:, e % 2, 0:size], qst[0:sa.depth_a, h % RING, qt * P:(qt + 1) * P],
                                     kst[0:sa.depth_a, h % RING, at:at + size], start=True, stop=True).then_inc(k.scored, 1)

                def pass_b(t, g, c):
                    c0, nch = sa.groups[g]
                    e = t * ng + g
                    if c == 0 and g == 0 and t >= 1:
                        pe.wait_ge(k.stored, 32 * sa.max_rows * t)
                    if c == 0 and e >= 2:
                        pe.wait_ge(k.exps, e - 1)
                    mm = nc.tensor.matmul(ps_b[:, e % 2, c, :], kst[0:sa.depth_b, t, (c0 + c) * P:(c0 + c + 1) * P],
                                          qst[0:sa.depth_b, t, :], start=True, stop=True)
                    if c == nch - 1:
                        mm.then_inc(k.products, 1)

                def weigh(t, g):
                    c0, nch = sa.groups[g]
                    e = t * ng + g
                    pe.wait_ge(k.exps, e + 1)
                    if g == 0:
                        if val is not None:
                            pe.wait_ge(k.pool_done, t + 1)
                        elif t >= 1:
                            pe.wait_ge(k.values_in[t % 2], 16 * ((t + 1) // 2))
                        if t >= 1:
                            pe.wait_ge(k.turned, t)
                    for c in range(nch):
                        at = 32 * c if sa.strips else 0
                        mm = nc.tensor.matmul(ps_o[at:at + sa.columns, 0:S], vh[:, t % 2, c0 + c, :], prob[:, e % 2, c, :],
                                              start=(g == 0 and (sa.strips or c == 0)),
                                              stop=(g == ng - 1 and (sa.strips or c == nch - 1)))
                    mm.then_inc(k.weighted, 1)

                def fold_sums(t):
                    pe.wait_ge(k.turned, t + 1)
                    if t >= 1:
                        pe.wait_ge(k.merged, t)
                    for qt in range(2):
                        mm = nc.tensor.matmul(ps_f[:, qt * 128:qt * 128 + dim1], acc[0:sa.out_rows, qt * P:(qt + 1) * P],
                                              fold[0:sa.out_rows, 0:dim1], start=True, stop=True)
                    mm.then_inc(k.unturned, 1)

                if first:
                    for j in range(nb):
                        pass_a(0, 0, j)
                for t in turns:
                    todo = list(range(nb)) if t + 1 in ahead else []

                    def next_a():
                        if todo:
                            pass_a(t + 1, t, todo.pop(0))

                    for g in range(ng + 1):
                        next_a()
                        if g < ng:
                            for c in range(sa.groups[g][1]):
                                pass_b(t, g, c)
                                if c % 2:
                                    next_a()
                        if g >= 1:
                            weigh(t, g - 1)
                        if g == 1 and t >= 1:
                            fold_sums(t - 1)
                if turns:
                    fold_sums(RING - 1)

            @block.scalar
            def _(act):
                def copy_sums(t):
                    act.wait_ge(k.weighted, (t + 1) * ng)
                    if t >= 1:
                        act.wait_ge(k.unturned, t)
                    nc.scalar.activation(acc[0:sa.out_rows, :], ps_o[0:sa.out_rows, 0:S], ACT.Identity).then_inc(k.turned, 1)

                for t in turns:
                    for g, (_, nch) in enumerate(sa.groups):
                        e = t * ng + g
                        act.wait_ge(k.products, e + 1)
                        if e >= 2:
                            act.wait_ge(k.weighted, e - 1)
                        nc.scalar.activation(prob[:, e % 2, 0:nch], ps_b[:, e % 2, 0:nch], ACT.Exp, scale=sa.scale)\
                            .then_inc(k.exps, 1)
                        if g == 0 and t >= 1:
                            copy_sums(t - 1)
                if turns:
                    copy_sums(RING - 1)

            @block.vector
            def _(v):
                step = Steps(v, k.vec_step)

                def maximum(n, j):
                    size = sa.blocks[j][2]
                    e = n * nb + j
                    v.wait_ge(k.scored, e + 1)
                    nc.vector.tensor_reduce(part[:, j:j + 1], ps_a[:, e % 2, 0:size], AX, ALU.max).then_inc(k.shifted, 1)

                def split_maxima(n):
                    v.wait_ge(k.shifted, (n + 1) * nb)
                    step(nc.vector.tensor_reduce(top[:], part[:].rearrange("p (a j) -> p a j", a=2), AX, ALU.max))
                    if n >= 1:
                        v.wait_ge(k.stored, 32 * sa.max_rows * n)
                    for qt in range(2):
                        step(nc.vector.tensor_scalar(parts[:, 2 * qt:2 * qt + 1], top[:, qt:qt + 1], -1.0, None, ALU.mult))
                        if sa.split:
                            step(nc.vector.scalar_tensor_tensor(out=parts[:, 2 * qt + 1:2 * qt + 2], in0=top[:, qt:qt + 1], scalar=-1.0,
                                                                in1=parts[:, 2 * qt:2 * qt + 1], op0=ALU.mult, op1=ALU.subtract))
                    nc.vector.transpose(parts_t[:], parts[:]).then_inc(k.vec_done, 1)

                def outputs(t):
                    v.wait_ge(k.unturned, t + 1)
                    for qt in range(2):
                        step(nc.vector.reciprocal(inv[:, qt:qt + 1], ps_f[:, qt * 128 + sa.dim:qt * 128 + dim1]))
                        ins = nc.vector.tensor_scalar(o[:, qt, bass.ds((base + t) * sa.dim, sa.dim)], ps_f[:, qt * 128:qt * 128 + sa.dim],
                                                      inv[:, qt:qt + 1], None, ALU.mult)
                        if qt == 0:
                            step(ins)
                    ins.then_inc(k.merged, 1)

                if first:
                    for j in range(nb):
                        maximum(0, j)
                    split_maxima(0)
                for t in turns:
                    for j in range(nb):
                        if t + 1 in ahead:
                            maximum(t, j)
                        if j == 7 and t >= 1:
                            outputs(t - 1)
                    if t + 1 in ahead:
                        split_maxima(t)
                if turns:
                    outputs(RING - 1)


def n_loads(sa):
    return 6 if sa.split else 2


def load_head(k, sp, sa, kst, qst, slot, h, b):
    d = k.d
    if sa.split:
        hr = bass.ds(h * sa.dim, sa.dim)
        at = 0
        for p, n in enumerate((3, 2, 1)):
            end = at + n * sa.dim
            sp.dma_start(kst[at:end, slot, :], d["k_parts"][p, hr, :].unsqueeze(0).broadcast_to([n, sa.dim, sa.keys]))\
                .then_inc(k.ring_in[slot], 16)
            sp.dma_start(qst[at:end, slot, :], d["q_parts"][0:n, hr, bass.ds(b * S, S)]).then_inc(k.ring_in[slot], 16)
            at = end
    else:
        hr = bass.ds(h * sa.dim, sa.dim)
        sp.dma_start(kst[0:sa.dim, slot, :], d["k_full"][hr, :]).then_inc(k.ring_in[slot], 16)
        sp.dma_start(qst[0:sa.dim, slot, :], d["q_full"][hr, bass.ds(b * S, S)]).then_inc(k.ring_in[slot], 16)


def mask_rows(k, sa, kst, qst, mask_name, mask_dt, b):
    nc, d = k.nc, k.d
    base = sa.rows
    piece, n = 1024, SK // 1024
    with ExitStack() as own:
        raw = k.sb(own, "raw", [1, n, piece], mask_dt)
        row = k.sb(own, "row", [1, piece], sa.dt)
        with k.stage() as block:
            @block.gpsimd
            def _(pool):
                nc.gpsimd.memset(kst[base:P], 1.0).then_inc(k.pool_done, 1)
                nc.gpsimd.memset(qst[base:base + 32], 1.0 if sa.split else 0.0).then_inc(k.pool_done, 1)
                pool.wait_ge(k.pool_done, 2)
                if not sa.split:
                    nc.gpsimd.memset(qst[base:base + 1], 1.0).then_inc(k.pool_done, 1)
                if sa.keys > SK:
                    nc.gpsimd.memset(kst[base:base + 1, :, SK:sa.keys], 0.0).then_inc(k.pool_done, 1)

            @block.sync
            def _(sp):
                sp.dma_start(raw[:].rearrange("o n x -> o (n x)"), d[mask_name][b].unsqueeze(0)).then_inc(k.loaded, 16)
                sp.wait_ge(k.pool_done, 2)
                for i in range(n):
                    sp.wait_ge(k.vec_done, i + 1)
                    for s in range(RING):
                        sp.dma_start(kst[base:base + 1, s, i * piece:(i + 1) * piece], row[:]).then_inc(k.stored, 16)
                    sp.wait_ge(k.stored, 16 * RING * (i + 1))

            @block.vector
            def _(v):
                v.wait_ge(k.loaded, 16)
                for i in range(n):
                    if i:
                        v.wait_ge(k.stored, 16 * RING * i)
                    nc.vector.tensor_scalar(row[:], raw[:, i, :], 0.0, NEG, ALU.is_equal, ALU.mult).then_inc(k.vec_done, 1)


def keys_split(k, src, w, dst):
    nc = k.nc
    with ExitStack() as own:
        ps = k.ps(own, "split_ps", [P, 2, 512])
        part = k.sb(own, "part3", [P, 3, 2, 512], BF16)
        rest = k.sb(own, "rest", [P, 2, 512])
        with k.stage() as block:
            @block.tensor
            def _(pe):
                for m in range(2):
                    for c in range(2):
                        mm = nc.tensor.matmul(ps[:, m, :], w[:, c, m * P:(m + 1) * P], src[:, c, :], start=(c == 0), stop=(c == 1))
                mm.then_inc(k.products, 1)

            @block.scalar
            def _(act):
                act.wait_ge(k.products, 1)
                nc.scalar.activation(part[:, 0], ps[:], ACT.Identity).then_inc(k.act_done, 1)
                act.wait_ge(k.vec_done, 1)
                nc.scalar.activation(part[:, 1], rest[:], ACT.Identity).then_inc(k.act_done, 1)

            @block.vector
            def _(v):
                v.wait_ge(k.act_done, 1)
                nc.vector.tensor_tensor(rest[:], ps[:], part[:, 0], ALU.subtract).then_inc(k.vec_done, 1)
                v.wait_ge(k.act_done, 2)
                nc.vector.tensor_tensor(part[:, 2], rest[:], part[:, 1], ALU.subtract).then_inc(k.vec_done, 1)

            @block.sync
            def _(sp):
                sp.wait_ge(k.vec_done, 2)
                for p in range(3):
                    sp.dma_start(rows(dst[p]), part[:, p]).then_inc(k.stored, 16)
                sp.wait_ge(k.stored, 48)


def keys_values(k, sa, ctx, wk, wv, val, b, j):
    nc, d = k.nc, k.d
    nf = sa.n * sa.dim
    with ExitStack() as own:
        ps_k = k.ps(own, "ps_k", [P, 2, 2, 512])
        ps_v = k.ps(own, "ps_v", [P, 4, 512])
        part = k.sb(own, "part3", [P, 2, 3, 2, 512], BF16)
        rest = k.sb(own, "rest", [P, 2, 2, 512])
        with k.stage() as block:
            @block.sync
            def _(sp):
                for u in range(2):
                    sp.dma_start(ctx[:, u], rows(d["ctx_t"][b])[:, :, bass.ds(j * 1024 + u * 512, 512)])\
                        .then_inc((k.loaded, k.loaded_next)[u], 16)
                for u in range(2):
                    sp.wait_ge(k.vec_done, 2 * u + 2)
                    for p in range(3):
                        sp.dma_start(rows(d["k_parts"][p])[:, :, bass.ds(j * 1024 + u * 512, 512)], part[:, u, p])\
                            .then_inc(k.stored, 16)
                sp.wait_ge(k.stored, 96)

            @block.tensor
            def _(pe):
                for u in range(2):
                    pe.wait_ge((k.loaded, k.loaded_next)[u], 16)
                    for m in range(2):
                        for c in range(2):
                            mm = nc.tensor.matmul(ps_k[:, u, m, :], wk[:, c, m * P:(m + 1) * P], ctx[:, u, c, :],
                                                  start=(c == 0), stop=(c == 1))
                    mm.then_inc(k.products, 1)
                    if u:
                        pe.wait_ge(k.evacuated, 1)
                    for t in range(4):
                        for c in range(2):
                            mm = nc.tensor.matmul(ps_v[:, t, 0:nf], ctx[:, u, c, t * P:(t + 1) * P], wv[:, c, :],
                                                  start=(c == 0), stop=(c == 1))
                    mm.then_inc(k.products, 1)

            @block.scalar
            def _(act):
                for u in range(2):
                    act.wait_ge(k.products, 2 * u + 1)
                    nc.scalar.activation(part[:, u, 0], ps_k[:, u], ACT.Identity).then_inc(k.act_done, 1)
                    act.wait_ge(k.products, 2 * u + 2)
                    chunks = val[:].rearrange("p c (h x) -> p c h x", h=sa.n)[:, bass.ds(j * 8 + u * 4, 4), :, 0:sa.dim]
                    nc.scalar.activation(chunks, ps_v[:, :, 0:nf].rearrange("p c (h x) -> p c h x", h=sa.n), ACT.Identity)\
                        .then_inc(k.evacuated, 1)
                    act.wait_ge(k.vec_done, 2 * u + 1)
                    nc.scalar.activation(part[:, u, 1], rest[:, u], ACT.Identity).then_inc(k.act_done, 1)

            @block.vector
            def _(v):
                for u in range(2):
                    v.wait_ge(k.act_done, 2 * u + 1)
                    nc.vector.tensor_tensor(rest[:, u], ps_k[:, u], part[:, u, 0], ALU.subtract).then_inc(k.vec_done, 1)
                    v.wait_ge(k.act_done, 2 * u + 2)
                    nc.vector.tensor_tensor(part[:, u, 2], rest[:, u], part[:, u, 1], ALU.subtract).then_inc(k.vec_done, 1)


def streamed_buffers(k, own, sa, val, o):
    kst = k.sb(own, "kst", [P, RING, sa.keys], sa.dt)
    qst = k.sb(own, "qst", [P, RING, S], sa.dt)
    vh = k.sb(own, "vh", [P, 2, sa.chunks, sa.columns])
    prob = k.sb(own, "prob", [P, 2, 4, S])
    acc = k.sb(own, "acc", [P, S])
    small = [k.sb(own, "part", [P, len(sa.blocks)]), k.sb(own, "top", [P, 2]), k.sb(own, "parts", [P, 32], sa.dt),
             k.sb(own, "parts_t", [P, 32], sa.dt), k.sb(own, "inv", [P, 2])]
    with k.stage() as block:
        @block.vector
        def _(v):
            k.nc.vector.memset(small[2][:], 0.0)
            k.nc.vector.memset(vh[:], 1.0 if val is None else 0.0)
    fold = k.fold if sa.strips else k.ident
    return kst, qst, vh, val, prob, o, acc, fold, small


def outputs_to_features(k, o, dst, chunks, b):
    nc = k.nc
    with ExitStack() as own:
        ps = k.ps(own, "turn_ps", [P, chunks, 512])
        with k.stage() as block:
            @block.tensor
            def _(pe):
                for c in range(chunks):
                    for qt in range(2):
                        mm = nc.tensor.transpose(ps[:, c, qt * P:(qt + 1) * P], o[:, qt, c * P:(c + 1) * P], k.ident[:])
                mm.then_inc(k.products, 1)

            @block.scalar
            def _(act):
                act.wait_ge(k.products, 1)
                nc.scalar.activation(dst[:, :, bass.ds(b * S, S)], ps[:, :, 0:S], ACT.Identity)




def l0_cross(k, x):
    nc, d = k.nc, k.d
    sa = Streamed(16, 16, SK, 0.25, split=True)
    dim1 = sa.dim + 1
    with ExitStack() as own:
        h = k.sb(own, "h", [P, 2, T])
        ot = k.sb(own, "ot", [P, 2, T])
        wq, wk, wv, wo = (k.sb(own, n, [P, 2, D]) for n in ("wq", "wk", "wv", "wo"))
        val = k.sb(own, "val", [P, sa.chunks, sa.n * dim1])
        o = k.sb(own, "att_o", [P, 2, sa.n * sa.dim])
        norm(k, h[:], x[:], T, 1e-5)
        load(k, [(wq[:], rows(d["L0_xattn_Wq"])), (wk[:], rows(d["L0_xattn_Wk"])), (wv[:], rows(d["L0_xattn_Wv"])),
                 (wo[:], rows(d["L0_xattn_Wo"]))])
        with k.stage() as block:
            @block.vector
            def _(v):
                nc.vector.memset(val[:], 1.0)
        keys_split(k, h, wq, d["q_parts"])
        with nc.Fori(0, B) as b:
            with ExitStack() as inner:
                ctx = k.sb(inner, "ctx", [P, 2, 2, 512])
                with nc.Fori(0, SK // 1024) as j:
                    keys_values(k, sa, ctx, wk, wv, val, b, j)
            with ExitStack() as inner:
                bufs = streamed_buffers(k, inner, sa, val, o)
                mask_rows(k, sa, bufs[0], bufs[1], "mask_BxS2_ik1", mybir.dt.int32, b)
                heads_turns(k, sa, bufs, 0, True, False, b)
                with nc.Fori(0, sa.n // RING - 1) as i:
                    heads_turns(k, sa, bufs, i, False, False, b)
                heads_turns(k, sa, bufs, sa.n // RING - 1, False, True, b)
            outputs_to_features(k, o, ot, sa.n * sa.dim // P, b)
        project(k, x, ot, 2, wo, 2, T, vec=(0.0, ALU.add, x, ALU.add))


def l0_scan(k, x):
    nc, d = k.nc, k.d
    NS = 16
    with ExitStack() as own:
        h = k.sb(own, "h", [P, 2, T])
        gate = k.sb(own, "gate", [P, 4, T])
        hs = k.sb(own, "hs", [P, 4, T])
        delta = k.sb(own, "delta", [P, 4, T])
        y = k.sb(own, "y", [P, 4, T])
        u = k.sb(own, "u", [P, 4, T])
        w_in = k.sb(own, "w_in", [P, 2, 1024])
        w_out = k.sb(own, "w_out", [P, 4, D])
        xp = k.sb(own, "xp", [P, 4, P])
        w_dt = k.sb(own, "w_dt", [64, 4 * P])
        dbl = k.sb(own, "dbl", [P, 1, T])
        a_neg = k.sb(own, "a_neg", [P, 64])
        conv = k.vec("conv")
        norm(k, h[:], x[:], T, 1e-5)
        project(k, hs, h, 2, w_in, 4, T, loads=[(w_in[:], rows(d["L0_attn_w_in_t"])), (w_out[:], rows(d["L0_attn_w_out_t"])),
                                                (xp[:], rows(d["L0_attn_w_xproj_t"])), (w_dt[:], d["L0_attn_w_dt_t"])])
        project(k, gate, h, 2, w_in[:, :, 512:1024], 4, T, func=ACT.Silu)
        with ExitStack() as inner:
            padded = k.sb(inner, "padded", [P, 4, B, S + 3])
            acc = k.sb(inner, "acc", [P, 4, B, S])
            with k.stage() as block:
                @block.vector
                def _(v):
                    step = Steps(v, k.vec_step)
                    step(nc.vector.memset(padded[:], 0.0))
                    for c in range(4):
                        step(nc.vector.tensor_copy(padded[:, c, :, 3:S + 3], hs[:, c, :].rearrange("p (b s) -> p b s", b=B)))
                        step(nc.vector.tensor_scalar(acc[:, c], padded[:, c, :, 0:S], conv[:, 4 * c:4 * c + 1], None, ALU.mult))
                        for i in range(1, 4):
                            ins = nc.vector.scalar_tensor_tensor(out=acc[:, c], in0=padded[:, c, :, i:S + i],
                                                                 scalar=conv[:, 4 * c + i:4 * c + i + 1], in1=acc[:, c],
                                                                 op0=ALU.mult, op1=ALU.add)
                            if i < 3:
                                step(ins)
                        ins.then_inc(k.vec_done, 1)

                @block.scalar
                def _(act):
                    for c in range(4):
                        act.wait_ge(k.vec_done, c + 1)
                        nc.scalar.activation(hs[:, c, :], acc[:, c].rearrange("p b s -> p (b s)"), ACT.Silu)
        project(k, dbl, hs, 4, xp, 1, T)
        with ExitStack() as inner:
            ps = k.ps(inner, "dt_ps", [P, 4, 512])
            z = k.sb(inner, "z", [P, 4, T])
            e = k.sb(inner, "e", [P, 4, T])
            with k.stage() as block:
                @block.sync
                def _(sp):
                    sp.dma_start(d["bc_rows"], dbl[64:96, 0, :]).then_inc(k.stored, 16)
                    sp.wait_ge(k.stored, 16)

                @block.tensor
                def _(pe):
                    for c in range(4):
                        mm = nc.tensor.matmul(ps[:, c, :], w_dt[:, c * P:(c + 1) * P], dbl[0:64, 0, :], start=True, stop=True)
                    mm.then_inc(k.products, 1)

                @block.scalar
                def _(act):
                    nc.scalar.activation(a_neg[:], k.vec("A_log"), ACT.Exp).then_inc(k.act_done, 1)
                    act.wait_ge(k.products, 1)
                    for c in range(4):
                        nc.scalar.activation(z[:, c, :], ps[:, c, :], ACT.Identity, bias=k.vec("L0_attn_b_dt")[:, c:c + 1])\
                            .then_inc(k.act_done, 1)
                    act.wait_ge(k.act_done, 5)
                    nc.scalar.activation(e[:], z[:], ACT.Abs).then_inc(k.act_done, 1)
                    act.wait_ge(k.act_done, 6)
                    nc.scalar.activation(e[:], e[:], ACT.Exp, scale=-1.0).then_inc(k.act_done, 1)
                    act.wait_ge(k.act_done, 7)
                    nc.scalar.activation(e[:], e[:], ACT.Ln, bias=1.0).then_inc(k.act_done, 1)

                @block.vector
                def _(v):
                    step = Steps(v, k.vec_step)
                    v.wait_ge(k.act_done, 8)
                    nc.vector.tensor_scalar(a_neg[:], a_neg[:], -1.0, None, ALU.mult)
                    step(nc.vector.scalar_tensor_tensor(out=delta[:], in0=z[:], scalar=0.0, in1=e[:], op0=ALU.max, op1=ALU.add))
                    nc.vector.tensor_tensor(u[:], delta[:], hs[:], ALU.mult)
                    for c in range(4):
                        nc.vector.tensor_scalar(y[:, c, :], hs[:, c, :], k.vec("L0_attn_D")[:, c:c + 1], None, ALU.mult)
        with ExitStack() as inner:
            bb = k.sb(inner, "bb", [P, T])
            cb = k.sb(inner, "cb", [P, T])
            decay = k.sb(inner, "decay", [P, 4, T])
            drive = k.sb(inner, "drive", [P, 4, T])
            state = k.sb(inner, "state", [P, 4, T])
            a_n = k.sb(inner, "a_n", [P, 4])
            with nc.Fori(0, NS) as n:
                with k.stage() as block:
                    @block.sync
                    def _(sp):
                        sp.dma_start(bb[:], d["bc_rows"][n].unsqueeze(0).broadcast_to([P, T])).then_inc(k.loaded, 16)
                        sp.dma_start(cb[:], d["bc_rows"][n + NS].unsqueeze(0).broadcast_to([P, T])).then_inc(k.loaded, 16)

                    @block.scalar
                    def _(act):
                        nc.scalar.activation(a_n[:], a_neg[:, bass.ds(n * 4, 4)], ACT.Identity).then_inc(k.act_done, 1)
                        act.wait_ge(k.act_done, 1)
                        for c in range(4):
                            nc.scalar.activation(decay[:, c, :], delta[:, c, :], ACT.Exp, scale=a_n[:, c:c + 1])\
                                .then_inc(k.act_done, 1)

                    @block.gpsimd
                    def _(pool):
                        pool.wait_ge(k.loaded, 32)
                        for c in range(4):
                            nc.gpsimd.tensor_tensor(drive[:, c, :], u[:, c, :], bb[:], ALU.mult).then_inc(k.pool_done, 1)

                    @block.vector
                    def _(v):
                        step = Steps(v, k.vec_step)
                        v.wait_ge(k.loaded, 32)
                        for c in range(4):
                            v.wait_ge(k.act_done, c + 2)
                            v.wait_ge(k.pool_done, c + 1)
                            for b in range(B):
                                s = slice(b * S, (b + 1) * S)
                                step(nc.vector.tensor_tensor_scan(state[:, c, s], decay[:, c, s], drive[:, c, s], 0.0,
                                                                  ALU.mult, ALU.add))
                            step(nc.vector.tensor_tensor(state[:, c, :], state[:, c, :], cb[:], ALU.mult))
                            nc.vector.tensor_tensor(y[:, c, :], y[:, c, :], state[:, c, :], ALU.add)
        with k.stage() as block:
            @block.vector
            def _(v):
                nc.vector.tensor_tensor(y[:], y[:], gate[:], ALU.mult)
        project(k, x, y, 4, w_out, 2, T, vec=(0.0, ALU.add, x, ALU.add))


def router(k, own, h, w_name, bias_name=None):
    d = k.d
    wg = k.sb(own, "wg", [P, 2, 8])
    logits = k.sb(own, "logits", [P, 4, 8])
    bias = k.sb(own, "gate_bias", [P, 8])
    loads = [(wg[:], rows(d[w_name]))]
    if bias_name is not None:
        loads.append((bias[:], d[bias_name].unsqueeze(0).broadcast_to([P, 8])))
    project_tokens(k, logits, h, 2, wg, 4, 8, loads=loads)
    return logits, bias


def softmax8(k, s):
    nc = k.nc
    with ExitStack() as own:
        r = k.sb(own, "row", [P, 4])
        with k.stage() as block:
            @block.vector
            def _(v):
                step = Steps(v, k.vec_step)
                step(nc.vector.tensor_reduce(r[:], s[:], AX, ALU.max))
                nc.vector.tensor_tensor(s[:], s[:], r[:].unsqueeze(2).broadcast_to([P, 4, 8]), ALU.subtract).then_inc(k.vec_done, 1)
                v.wait_ge(k.act_done, 1)
                step(nc.vector.reduce_sum(r[:], s[:], AX))
                step(nc.vector.reciprocal(r[:], r[:]))
                nc.vector.tensor_tensor(s[:], s[:], r[:].unsqueeze(2).broadcast_to([P, 4, 8]), ALU.mult)

            @block.scalar
            def _(act):
                act.wait_ge(k.vec_done, 1)
                nc.scalar.activation(s[:], s[:], ACT.Exp).then_inc(k.act_done, 1)


def gates_by_expert(k, w, wt):
    nc = k.nc
    with ExitStack() as own:
        ps = k.ps(own, "gate_ps", [P, 512])
        with k.stage() as block:
            @block.tensor
            def _(pe):
                for t in range(4):
                    mm = nc.tensor.transpose(ps[0:8, t * P:(t + 1) * P], w[:, t, :], k.ident[:])
                mm.then_inc(k.products, 1)

            @block.vector
            def _(v):
                v.wait_ge(k.products, 1)
                nc.vector.tensor_copy(wt[:], ps[0:8, :])


def store_gates(k, wt, shared=None):
    nc, d = k.nc, k.d
    with ExitStack() as own:
        row = k.sb(own, "shared_row", [1, T])
        with k.stage() as block:
            @block.vector
            def _(v):
                if shared is not None:
                    nc.vector.memset(row[:], shared).then_inc(k.vec_done, 1)

            @block.sync
            def _(sp):
                sp.dma_start(d["gate_rows"][0:8, :], wt[:]).then_inc(k.stored, 16)
                if shared is not None:
                    sp.wait_ge(k.vec_done, 1)
                    sp.dma_start(d["gate_rows"][8:9, :], row[:]).then_inc(k.stored, 16)
                sp.wait_ge(k.stored, 32 if shared is not None else 16)


def experts_gelu(k, x, h, n, up, down, vecs):
    nc, d = k.nc, k.d
    with ExitStack() as own:
        wu = k.sb(own, "wu", [P, 2, 1024])
        wd = k.sb(own, "wd", [P, 8, D])
        bv = k.sb(own, "bv", [P, 10])
        gate = k.sb(own, "gate", [P, T])
        a = k.sb(own, "a", [P, 8, T])
        y = k.sb(own, "y", [P, 2, T])
        ps = k.ps(own, "moe_ps", [P, 6, 512])
        with nc.Fori(0, n) as e:
            with k.stage() as block:
                @block.sync
                def _(sp):
                    sp.dma_start(bv[:], d[vecs][e]).then_inc(k.loaded, 16)
                    sp.dma_start(wu[:], rows(d[up][e])).then_inc(k.loaded, 16)
                    sp.wait_ge(k.loaded, 32)
                    sp.dma_start(gate[:], d["gate_rows"][e].unsqueeze(0).broadcast_to([P, T])).then_inc(k.loaded, 16)
                    sp.dma_start(wd[:], rows(d[down][e])).then_inc(k.loaded, 16)

                @block.tensor
                def _(pe):
                    pe.wait_ge(k.loaded, 32)
                    for m in range(8):
                        if m >= 4:
                            pe.wait_ge(k.act_done, m - 3)
                        for c in range(2):
                            mm = nc.tensor.matmul(ps[:, m % 4, :], wu[:, c, m * P:(m + 1) * P], h[:, c, :],
                                                  start=(c == 0), stop=(c == 1))
                        mm.then_inc(k.products, 1)
                    pe.wait_ge(k.loaded, 64)
                    for f in range(8):
                        pe.wait_ge(k.act_done, f + 1)
                        for m in range(2):
                            mm = nc.tensor.matmul(ps[:, 4 + m, :], wd[:, f, m * P:(m + 1) * P], a[:, f, :],
                                                  start=(f == 0), stop=(f == 7))
                    mm.then_inc(k.products, 1)

                @block.scalar
                def _(act):
                    act.wait_ge(k.loaded, 32)
                    for m in range(8):
                        act.wait_ge(k.products, m + 1)
                        nc.scalar.activation(a[:, m, :], ps[:, m % 4, :], ACT.Gelu, bias=bv[:, m:m + 1]).then_inc(k.act_done, 1)

                @block.vector
                def _(v):
                    step = Steps(v, k.vec_step)
                    v.wait_ge(k.loaded, 64)
                    v.wait_ge(k.products, 9)
                    for m in range(2):
                        step(nc.vector.scalar_tensor_tensor(out=y[:, m, :], in0=ps[:, 4 + m, :], scalar=bv[:, 8 + m:9 + m],
                                                            in1=gate[:], op0=ALU.add, op1=ALU.mult))
                    nc.vector.tensor_tensor(x[:], x[:], y[:], ALU.add)


def l0_experts(k, x):
    nc = k.nc
    with ExitStack() as own:
        h = k.sb(own, "h", [P, 2, T])
        norm(k, h[:], x[:], T, 1e-5)
        s, bias = router(k, own, h, "L0_ffn_gate_w_t", "L0_ffn_gate_bias")
        top = k.sb(own, "top", [P, 4, 8])
        den = k.sb(own, "den", [P, 4])
        w = k.sb(own, "w", [P, 4, 8])
        wt = k.sb(own, "wt", [8, T])
        with k.stage() as block:
            @block.vector
            def _(v):
                step = Steps(v, k.vec_step)
                nc.vector.tensor_tensor(s[:], s[:], bias[:].unsqueeze(1).broadcast_to([P, 4, 8]), ALU.add).then_inc(k.vec_done, 1)
                v.wait_ge(k.act_done, 1)
                for t in range(4):
                    step(nc.vector.max(top[:, t, :], s[:, t, :]))
                step(nc.vector.tensor_tensor(den[:], top[:, :, 0], top[:, :, 1], ALU.add))
                step(nc.vector.tensor_scalar(den[:], den[:], 1e-6, None, ALU.add))
                step(nc.vector.reciprocal(den[:], den[:]))
                step(nc.vector.tensor_tensor(w[:], s[:], top[:, :, 1:2].broadcast_to([P, 4, 8]), ALU.is_ge))
                step(nc.vector.tensor_tensor(w[:], w[:], s[:], ALU.mult))
                nc.vector.tensor_tensor(w[:], w[:], den[:].unsqueeze(2).broadcast_to([P, 4, 8]), ALU.mult)

            @block.scalar
            def _(act):
                act.wait_ge(k.vec_done, 1)
                nc.scalar.activation(s[:], s[:], ACT.Sigmoid).then_inc(k.act_done, 1)
        gates_by_expert(k, w, wt)
        store_gates(k, wt, 0.1)
        experts_gelu(k, x, h, 9, "L0_ffn_up", "L0_ffn_down", "L0_ffn_vecs")




def l1_cross(k, x):
    nc, d = k.nc, k.d
    hd = Heads(1, 256, 1.0 / 16)
    with ExitStack() as own:
        h = k.sb(own, "h", [P, 2, T])
        q = k.sb(own, "q", [P, 2, T])
        qb = k.sb(own, "qb", [P, 2, S])
        ot = k.sb(own, "ot", [P, 2, T])
        wq, wk, wv, wo = (k.sb(own, n, [P, 2, D]) for n in ("wq", "wk", "wv", "wo"))
        ctx = k.sb(own, "ctx", [P, 2, KB])
        kt = k.sb(own, "kt", [P, 2, KB])
        val = k.sb(own, "val", [P, 2, D])
        st = attention_state(k, own, hd)
        norm(k, h[:], x[:], T, 1e-5)
        project(k, q, h, 2, wq, 2, T, bias=k.vec("L1_xattn_bq"), loads=[
            (wq[:], rows(d["L1_xattn_Wq_t"])), (wk[:], rows(d["L1_xattn_Wk_t"])),
            (wv[:], rows(d["L1_xattn_Wv_t"])), (wo[:], rows(d["L1_xattn_Wo_t"]))])
        with nc.Fori(0, B) as b:
            copy_batch(k, qb[:], q, b)
            attention_start(k, st)
            with nc.Fori(0, SK // KB) as j:
                project(k, kt, ctx, 2, wk, 2, KB, loads=[(ctx[:], rows(d["ctx_t"][b])[:, :, bass.ds(j * KB, KB)])])
                project_tokens(k, val, ctx, 2, wv, 2, D)
                attend(k, hd, st, qb, kt, val)
            attention_end(k, hd, st, ot, b, bias=k.vec("L1_xattn_bv"))
        project(k, x, ot, 2, wo, 2, T, vec=(k.vec("L1_xattn_bo"), ALU.add, x, ALU.add))


def l1_self(k, x):
    nc, d = k.nc, k.d
    hd = Heads(16, 64, 0.125)
    with ExitStack() as own:
        h = k.sb(own, "h", [P, 2, T])
        hb = k.sb(own, "hb", [P, 2, S])
        qb, kt = k.sb(own, "qb", [P, 8, S]), k.sb(own, "kt", [P, 8, S])
        val = k.sb(own, "val", [P, 2, 1024])
        ot = k.sb(own, "ot", [P, 8, T])
        wq, wk, wv = (k.sb(own, n, [P, 2, 1024]) for n in ("wq", "wk", "wv"))
        wo = k.sb(own, "wo", [P, 8, D])
        st = attention_state(k, own, hd)
        norm(k, h[:], x[:], T, 1e-5)
        load(k, [(wq[:], rows(d["L1_attn_w_q_t"])), (wk[:], rows(d["L1_attn_w_k_t"])), (wv[:], rows(d["L1_attn_w_v_t"])),
                 (wo[:], rows(d["L1_attn_w_o"]))])
        with nc.Fori(0, B) as b:
            copy_batch(k, hb[:], h, b)
            project(k, qb, hb, 2, wq, 8, S)
            project(k, kt, hb, 2, wk, 8, S)
            project_tokens(k, val, hb, 2, wv, 2, 1024)
            attention_start(k, st)
            attend(k, hd, st, qb, kt, val)
            attention_end(k, hd, st, ot, b)
        project(k, h, ot, 8, wo, 2, T, vec=(0.0, ALU.add, h, ALU.add))
        with k.stage() as block:
            @block.vector
            def _(v):
                nc.vector.tensor_tensor(x[:], x[:], h[:], ALU.add)


def l1_ffn(k, x):
    d = k.d
    with ExitStack() as own:
        h = k.sb(own, "h", [P, 2, T])
        w = k.sb(own, "w", [P, 8, 1024])
        a1, a2 = k.sb(own, "a1", [P, 8, T]), k.sb(own, "a2", [P, 8, T])
        norm(k, h[:], x[:], T, 1e-5)
        project(k, a1, h, 2, w, 8, T, loads=[(w[:, 0:2, :], rows(d["L1_ffn_w1_t"]))], func=ACT.Silu, scale=k.vec("L1_ffn_w1_s"))
        project(k, a1, h, 2, w, 8, T, loads=[(w[:, 0:2, :], rows(d["L1_ffn_w2_t"]))],
                vec=(k.vec("L1_ffn_w2_s"), ALU.mult, a1, ALU.mult))
        project(k, a2, a1, 8, w, 8, T, loads=[(w[:], rows(d["L1_ffn_h1_t"]))], func=ACT.Gelu, scale=k.vec("L1_ffn_h1_s"))
        project(k, a1, a2, 8, w, 8, T, loads=[(w[:], rows(d["L1_ffn_h2_t"]))], func=ACT.Gelu, scale=k.vec("L1_ffn_h2_s"))
        project(k, x, a1, 8, w, 2, T, loads=[(w[:, :, 0:D], rows(d["L1_ffn_w3_t"]))],
                vec=(k.vec("L1_ffn_w3_s"), ALU.mult, x, ALU.add))




def window_mask(k, dst, seg, offset, work):
    nc = k.nc
    with k.stage() as block:
        @block.vector
        def _(v):
            step = Steps(v, k.vec_step)
            step(nc.vector.tensor_scalar(work[:, 0, :], k.iota[:], offset, None, ALU.add))
            for t in range(2):
                step(nc.vector.tensor_scalar(work[:, 1, :], work[:, 0, :], seg[:, t:t + 1], None, ALU.subtract))
                step(nc.vector.tensor_scalar(dst[:, t, :], work[:, 1, :], 0.0, NEG, ALU.is_gt, ALU.mult))
                step(nc.vector.tensor_scalar(work[:, 1, :], work[:, 1, :], -128.0, NEG, ALU.is_le, ALU.mult))
                step(nc.vector.tensor_tensor(dst[:, t, :], dst[:, t, :], work[:, 1, :], ALU.add))
            nc.vector.tensor_scalar(offset, offset, float(KB), None, ALU.add)


def blocks_with_segments(k, count, work, row):
    nc, d = k.nc, k.d
    top_i, low, top, bad = work
    with k.stage() as block:
        @block.sync
        def _(sp):
            sp.dma_start(row, d["seg_row"]).then_inc(k.loaded, 16)

        @block.vector
        def _(v):
            step = Steps(v, k.vec_step)
            v.wait_ge(k.loaded, 16)
            step(nc.vector.tensor_reduce(top_i, row, AX, ALU.max))
            step(nc.vector.tensor_reduce(top, row, AX, ALU.max))
            step(nc.vector.tensor_reduce(low, row, AX, ALU.min))
            step(nc.vector.tensor_scalar(top_i, top_i, KB.bit_length() - 1, None, ALU.arith_shift_right))
            step(nc.vector.tensor_scalar(low, low, 0.0, float(SK // KB), ALU.is_lt, ALU.mult))
            step(nc.vector.tensor_scalar(bad, top, float(SK - 1), float(SK // KB), ALU.is_gt, ALU.mult))
            step(nc.vector.tensor_tensor(bad, bad, low, ALU.add))
            step(nc.vector.tensor_copy(top, top_i))
            step(nc.vector.tensor_scalar(top, top, 1.0, 1.0, ALU.add, ALU.max))
            step(nc.vector.tensor_tensor(top, top, bad, ALU.add))
            step(nc.vector.tensor_scalar(top, top, float(SK // KB), None, ALU.min))
            nc.vector.tensor_copy(count, top)
    return nc.values_load(count, min_val=1, max_val=SK // KB)


def l2_cross(k, x):
    nc, d = k.nc, k.d
    hd = Heads(16, 16, 0.25)
    with ExitStack() as own:
        xx = k.sb(own, "xx", [P, 2, T])
        h = k.sb(own, "h", [P, 2, T])
        hb = k.sb(own, "hb", [P, 2, S])
        qb, qr, kt = (k.sb(own, n, [P, 4, S]) for n in ("qb", "qr", "kt"))
        val = k.sb(own, "val", [P, 2, D])
        ot = k.sb(own, "ot", [P, 2, T])
        wqk = k.sb(own, "wqk", [P, 2, 2048])
        wv, wo, wvc, woc = (k.sb(own, n, [P, 2, D]) for n in ("wv", "wo", "wvc", "woc"))
        wqc, wkc = k.sb(own, "wqc", [P, 2, 512]), k.sb(own, "wkc", [P, 2, 512])
        lv = k.sb(own, "lv", [P, 26])
        ctx = k.sb(own, "ctx", [P, 2, KB])
        mask = k.sb(own, "mask", [P, 2, KB])
        work = k.sb(own, "work", [P, 2, KB])
        seg_i = k.sb(own, "seg_i", [P, 2], mybir.dt.int32)
        seg = k.sb(own, "seg", [P, 2])
        offset = k.sb(own, "offset", [P, 1])
        st = attention_state(k, own, hd)

        def col(name):
            a, b = LAYER_VECS[name]
            return lv[:, a:b]

        row = k.sb(own, "seg_row", [1, T], mybir.dt.int32)
        top_i, count = (k.sb(own, n, [1, 1], mybir.dt.int32) for n in ("top_i", "count"))
        work3 = [k.sb(own, n, [1, 1]) for n in ("low", "top", "bad")]
        key_blocks = blocks_with_segments(k, count[:], [top_i[:]] + [t[:] for t in work3], row[:])
        norm(k, xx[:], x[:], T, 1e-5)
        with nc.Fori(0, 4) as layer:
            load(k, [(wqk[:], rows(d["L2_qk_strips"][layer])), (wv[:], rows(d["L2_wv"][layer])), (wo[:], rows(d["L2_wo"][layer])),
                     (wqc[:], rows(d["L2_qc_strips"][layer])), (wkc[:], rows(d["L2_kc_strips"][layer])),
                     (wvc[:], rows(d["L2_wvc"][layer])), (woc[:], rows(d["L2_woc"][layer])), (lv[:], d["L2_vecs"][layer])])
            norm(k, h[:], xx[:], T, 1e-6, mean=False, w=col("n1"))
            with nc.Fori(0, B) as b:
                copy_batch(k, hb[:], h, b)
                project(k, qb, hb, 2, wqk[:, :, 0:512], 4, S, bias=col("bq"))
                project(k, qr, hb, 2, wqk[:, :, 512:1024], 4, S, bias=col("bq_turned"))
                rope(k, qb, qr)
                project(k, kt, hb, 2, wqk[:, :, 1024:1536], 4, S, bias=col("bk"))
                project(k, qr, hb, 2, wqk[:, :, 1536:2048], 4, S, bias=col("bk_turned"))
                rope(k, kt, qr)
                project_tokens(k, val, hb, 2, wv, 2, D)
                attention_start(k, st)
                attend(k, hd, st, qb, kt, val, k.causal, mask_by_query=True)
                attention_end(k, hd, st, ot, b, bias=col("bv"))
            project(k, xx, ot, 2, wo, 2, T, vec=(col("bo"), ALU.add, xx, ALU.add))
            norm(k, h[:], xx[:], T, 1e-6, mean=False, w=col("n2"))
            with nc.Fori(0, B) as b:
                copy_batch(k, hb[:], h, b)
                project(k, qb, hb, 2, wqc, 4, S)
                attention_start(k, st)
                with k.stage() as block:
                    @block.sync
                    def _(sp):
                        sp.dma_start(seg_i[:], d["seg_cols"][b]).then_inc(k.loaded, 16)

                    @block.vector
                    def _(v):
                        v.wait_ge(k.loaded, 16)
                        nc.vector.tensor_copy(seg[:], seg_i[:])
                        nc.vector.memset(offset[:], 0.0)
                with nc.Fori(0, key_blocks) as j:
                    window_mask(k, mask, seg, offset[:], work)
                    project(k, kt, ctx, 2, wkc, 4, KB, loads=[(ctx[:], rows(d["ctx_t"][b])[:, :, bass.ds(j * KB, KB)])])
                    project_tokens(k, val, ctx, 2, wvc, 2, D)
                    attend(k, hd, st, qb, kt, val, mask, mask_by_query=True)
                attention_end(k, hd, st, ot, b)
            project(k, xx, ot, 2, woc, 2, T, vec=(0.0, ALU.add, xx, ALU.add))
            norm(k, h[:], xx[:], T, 1e-6, mean=False, w=col("n3"))
            with ExitStack() as inner:
                wg = k.sb(inner, "wg", [P, 2, 1024])
                wu = k.sb(inner, "wu", [P, 2, 1024])
                wd = k.sb(inner, "wd", [P, 8, D])
                a = k.sb(inner, "a", [P, 8, T])
                project(k, a, h, 2, wg, 8, T, func=ACT.Silu, loads=[(wg[:], rows(d["L2_wg"][layer])), (wu[:], rows(d["L2_wu"][layer])),
                                                                    (wd[:], rows(d["L2_wd"][layer]))])
                project(k, a, h, 2, wu, 8, T, vec=(1.0, ALU.mult, a, ALU.mult))
                project(k, xx, a, 8, wd, 2, T, vec=(0.0, ALU.add, xx, ALU.add))
        norm(k, x[:], xx[:], T, 1e-6, mean=False, w=k.vec("L2_xattn_nf"), plus=x)


def l2_self(k, x):
    nc, d = k.nc, k.d
    nh, dim = 16, 16
    with ExitStack() as own:
        h = k.sb(own, "h", [P, 2, T])
        wq, wk, wv, wo = (k.sb(own, n, [P, 2, D]) for n in ("wq", "wk", "wv", "wo"))
        rb = k.sb(own, "rb", [P, 5, D])
        q, key, val = (k.sb(own, n, [P, 4, D]) for n in ("q", "key", "val"))
        rel = k.sb(own, "rel", [P, 6, nh])
        gw = k.sb(own, "gw", [P, dim, 8])
        gb = k.sb(own, "gb", [P, 8])
        ga = k.sb(own, "ga", [P, nh])
        gws = k.sb(own, "gws", [P, dim])
        gbs = k.sb(own, "gbs", [P, 1])
        gate = k.sb(own, "gate", [P, 4, nh])
        prod = k.sb(own, "prod", [P, D])
        sc = k.sb(own, "sc", [P, 4, 3, nh])
        mx = k.sb(own, "mx", [P, 4, nh])
        o = k.sb(own, "o", [P, 4, D])
        ot = k.sb(own, "ot", [P, 2, T])

        def all_rows(src, n):
            return src.unsqueeze(0).broadcast_to([P, n])

        bucket = {-1: 1, 0: 0, 1: 17, 2: 18}
        norm(k, h[:], x[:], T, 1e-5)
        load(k, [(wq[:], rows(d["L2_attn_q_w"])), (wk[:], rows(d["L2_attn_k_w"])), (wv[:], rows(d["L2_attn_v_w"])),
                 (wo[:], rows(d["L2_attn_out_w"]))]
             + [(rb[:, i, :], all_rows(d[n], D)) for i, n in enumerate(
                 ["L2_attn_q_b", "L2_attn_k_b", "L2_attn_v_b", "L2_attn_bias_k_row", "L2_attn_bias_v_row"])]
             + [(rel[:, 3 * t + s, :], all_rows(d["L2_attn_rel_emb"][bucket[s - t]], nh)) for t in range(2) for s in range(3)]
             + [(gw[:].rearrange("p a b -> p (a b)"), all_rows(d["L2_attn_grep_w_row"], 128)), (gb[:], all_rows(d["L2_attn_grep_b"], 8)),
                (ga[:], all_rows(d["L2_attn_grep_a_row"], nh))])
        project_tokens(k, q, h, 2, wq, 4, D, bias_rows=rb[:, 0, :])
        project_tokens(k, key, h, 2, wk, 4, D, bias_rows=rb[:, 1, :])
        project_tokens(k, val, h, 2, wv, 4, D, bias_rows=rb[:, 2, :])

        def heads(flat):
            return flat.rearrange("p (h x) -> p h x", h=nh)

        qq = k.sb(own, "qq", [P, 2, 2 * D])
        kk, vv = k.sb(own, "kk", [P, 2, 3 * D]), k.sb(own, "vv", [P, 2, 3 * D])

        def part(flat, n, i):
            return flat.rearrange("p (h n x) -> p h n x", h=nh, n=n)[:, :, i, :]

        with k.stage() as block:
            @block.vector
            def _(v):
                step = Steps(v, k.vec_step)
                step(nc.vector.reduce_sum(gws[:], gw[:], AX))
                step(nc.vector.reduce_sum(gbs[:], gb[:], AX))
                for t in range(4):
                    batch, tile = t // 2, t % 2
                    at = slice(batch * D, (batch + 1) * D)
                    for to, fr in ((qq, q), (kk, key), (vv, val)):
                        step(nc.vector.tensor_copy(to[:, tile, at], fr[:, t, :]))
                for tile in range(2):
                    for to, row in ((kk, 3), (vv, 4)):
                        step(nc.vector.tensor_copy(to[:, tile, 2 * D:3 * D], rb[:, row, :]))
                for t in range(4):
                    step(nc.vector.tensor_tensor(heads(prod[:]), part(qq[:, t % 2, :], 2, t // 2), gws[:].unsqueeze(1).broadcast_to([P, nh, dim]),
                                                 ALU.mult))
                    step(nc.vector.reduce_sum(gate[:, t, :], heads(prod[:]), AX))
                nc.vector.tensor_scalar(gate[:], gate[:], gbs[:], None, ALU.add).then_inc(k.vec_done, 1)
                v.wait_ge(k.act_done, 1)
                step(nc.vector.tensor_tensor(gate[:], gate[:], ga[:].unsqueeze(1).broadcast_to([P, 4, nh]), ALU.mult))
                for t in range(4):
                    for s in range(3):
                        step(nc.vector.tensor_tensor(heads(prod[:]), part(qq[:, t % 2, :], 2, t // 2), part(kk[:, t % 2, :], 3, s),
                                                     ALU.mult))
                        step(nc.vector.reduce_sum(mx[:, t, :], heads(prod[:]), AX))
                        step(nc.vector.tensor_tensor(sc[:, t, s, :], gate[:, t, :], rel[:, 3 * (t // 2) + s, :], ALU.mult))
                        step(nc.vector.scalar_tensor_tensor(out=sc[:, t, s, :], in0=mx[:, t, :], scalar=dim ** -0.5 / 32.0,
                                                            in1=sc[:, t, s, :], op0=ALU.mult, op1=ALU.add))
                step(nc.vector.tensor_tensor(mx[:], sc[:, :, 0, :], sc[:, :, 1, :], ALU.max))
                step(nc.vector.tensor_tensor(mx[:], mx[:], sc[:, :, 2, :], ALU.max))
                for s in range(3):
                    ins = nc.vector.tensor_tensor(sc[:, :, s, :], sc[:, :, s, :], mx[:], ALU.subtract)
                ins.then_inc(k.vec_done, 1)
                v.wait_ge(k.act_done, 2)
                step(nc.vector.tensor_tensor(mx[:], sc[:, :, 0, :], sc[:, :, 1, :], ALU.add))
                step(nc.vector.tensor_tensor(mx[:], mx[:], sc[:, :, 2, :], ALU.add))
                step(nc.vector.reciprocal(mx[:], mx[:]))
                for s in range(3):
                    step(nc.vector.tensor_tensor(sc[:, :, s, :], sc[:, :, s, :], mx[:], ALU.mult))
                for t in range(4):
                    for s in range(3):
                        to = o[:, t, :] if s == 0 else prod[:]
                        step(nc.vector.tensor_tensor(heads(to), part(vv[:, t % 2, :], 3, s), sc[:, t, s, :].unsqueeze(2).broadcast_to([P, nh, dim]),
                                                     ALU.mult))
                        if s:
                            step(nc.vector.tensor_tensor(o[:, t, :], o[:, t, :], prod[:], ALU.add))

            @block.scalar
            def _(act):
                act.wait_ge(k.vec_done, 1)
                nc.scalar.activation(gate[:], gate[:], ACT.Sigmoid).then_inc(k.act_done, 1)
                act.wait_ge(k.vec_done, 2)
                nc.scalar.activation(sc[:], sc[:], ACT.Exp).then_inc(k.act_done, 1)
        to_features(k, ot, o, 4, 2)
        project(k, x, ot, 2, wo, 2, T, vec=(k.vec("L2_attn_out_b"), ALU.add, x, ALU.add))


def to_features(k, dst, src, tiles, chunks):
    nc = k.nc
    with ExitStack() as own:
        ps = k.ps(own, "turn_ps", [P, chunks, 512])
        with k.stage() as block:
            @block.tensor
            def _(pe):
                for c in range(chunks):
                    for t in range(tiles):
                        mm = nc.tensor.transpose(ps[:, c, t * P:(t + 1) * P], src[:, t, c * P:(c + 1) * P], k.ident[:])
                mm.then_inc(k.products, 1)

            @block.scalar
            def _(act):
                act.wait_ge(k.products, 1)
                nc.scalar.activation(dst[:], ps[:, :, 0:tiles * P], ACT.Identity)


def l2_experts(k, x):
    nc, d = k.nc, k.d
    with ExitStack() as own:
        h = k.sb(own, "h", [P, 2, T])
        norm(k, h[:], x[:], T, 1e-5)
        s, bias = router(k, own, h, "L2_ffn_gate_w_t", "L2_ffn_gate_b")
        softmax8(k, s)
        top = k.sb(own, "top", [P, 4, 8])
        biased = k.sb(own, "biased", [P, 4, 8])
        w = k.sb(own, "w", [P, 4, 8])
        wt = k.sb(own, "wt", [8, T])
        with k.stage() as block:
            @block.vector
            def _(v):
                step = Steps(v, k.vec_step)
                step(nc.vector.tensor_tensor(biased[:], s[:], bias[:].unsqueeze(1).broadcast_to([P, 4, 8]), ALU.add))
                for t in range(4):
                    step(nc.vector.max(top[:, t, :], biased[:, t, :]))
                step(nc.vector.tensor_tensor(w[:], biased[:], top[:, :, 1:2].broadcast_to([P, 4, 8]), ALU.is_ge))
                nc.vector.tensor_tensor(w[:], w[:], s[:], ALU.mult)
        gates_by_expert(k, w, wt)
        store_gates(k, wt, 1.0)
        w1, w3 = k.sb(own, "w1", [P, 2, 512]), k.sb(own, "w3", [P, 2, 512])
        w2 = k.sb(own, "w2", [P, 2, D])
        bv = k.sb(own, "bv", [P, 10])
        gate = k.sb(own, "gate", [P, T])
        h1 = k.sb(own, "h1", [P, 4, T])
        sig = k.sb(own, "sig", [P, 2, T])
        a = k.sb(own, "a", [P, 2, T])
        y = k.sb(own, "y", [P, 2, T])
        ps = k.ps(own, "swi_ps", [P, 8, 512])
        with nc.Fori(0, 9) as e:
            with k.stage() as block:
                @block.sync
                def _(sp):
                    sp.dma_start(bv[:], d["L2_ffn_vecs"][e]).then_inc(k.loaded, 16)
                    sp.dma_start(w1[:], rows(d["L2_ffn_w1"][e])).then_inc(k.loaded, 16)
                    sp.dma_start(w3[:], rows(d["L2_ffn_w3"][e])).then_inc(k.loaded, 16)
                    sp.dma_start(w2[:], rows(d["L2_ffn_w2"][e])).then_inc(k.loaded, 16)
                    sp.dma_start(gate[:], d["gate_rows"][e].unsqueeze(0).broadcast_to([P, T])).then_inc(k.loaded, 16)

                @block.tensor
                def _(pe):
                    pe.wait_ge(k.loaded, 80)
                    for m in range(4):
                        for wi, w13 in enumerate((w1, w3)):
                            for c in range(2):
                                mm = nc.tensor.matmul(ps[:, 2 * m + wi, :], w13[:, c, m * P:(m + 1) * P], h[:, c, :],
                                                      start=(c == 0), stop=(c == 1))
                        mm.then_inc(k.products, 1)
                    pe.wait_ge(k.vec_done, 3)
                    for m in range(2):
                        for c in range(2):
                            mm = nc.tensor.matmul(ps[:, m, :], w2[:, c, m * P:(m + 1) * P], a[:, c, :],
                                                  start=(c == 0), stop=(c == 1))
                    mm.then_inc(k.products, 1)

                @block.scalar
                def _(act):
                    act.wait_ge(k.loaded, 80)
                    for m in range(4):
                        act.wait_ge(k.products, m + 1)
                        nc.scalar.activation(h1[:, m, :], ps[:, 2 * m, :], ACT.Identity, bias=bv[:, m:m + 1]).then_inc(k.act_done, 1)
                    act.wait_ge(k.vec_done, 2)
                    nc.scalar.activation(sig[:], h1[:, 0:2, :], ACT.Sigmoid, scale=1.702).then_inc(k.act_done, 1)

                @block.vector
                def _(v):
                    step = Steps(v, k.vec_step)
                    v.wait_ge(k.loaded, 80)
                    for m in range(4):
                        v.wait_ge(k.act_done, m + 1)
                        ins = nc.vector.scalar_tensor_tensor(out=h1[:, m, :], in0=ps[:, 2 * m + 1, :], scalar=bv[:, 4 + m:5 + m],
                                                             in1=h1[:, m, :], op0=ALU.add, op1=ALU.mult)
                        if m < 3:
                            step(ins)
                    ins.then_inc(k.vec_done, 1)
                    v.wait_ge(k.vec_done, 1)
                    nc.vector.tensor_scalar(h1[:, 0:2, :], h1[:, 0:2, :], 7.0, None, ALU.min).then_inc(k.vec_done, 1)
                    step(nc.vector.tensor_scalar(h1[:, 2:4, :], h1[:, 2:4, :], -7.0, 7.0, ALU.max, ALU.min))
                    v.wait_ge(k.vec_done, 2)
                    step(nc.vector.scalar_tensor_tensor(out=h1[:, 2:4, :], in0=h1[:, 2:4, :], scalar=1.0, in1=h1[:, 0:2, :],
                                                        op0=ALU.add, op1=ALU.mult))
                    v.wait_ge(k.act_done, 5)
                    nc.vector.tensor_tensor(a[:], h1[:, 2:4, :], sig[:], ALU.mult).then_inc(k.vec_done, 1)
                    v.wait_ge(k.products, 5)
                    for m in range(2):
                        step(nc.vector.scalar_tensor_tensor(out=y[:, m, :], in0=ps[:, m, :], scalar=bv[:, 8 + m:9 + m],
                                                            in1=gate[:], op0=ALU.add, op1=ALU.mult))
                    nc.vector.tensor_tensor(x[:], x[:], y[:], ALU.add)




def values_and_keys_out(k, src, wv, tiles, kt, at):
    nc, d = k.nc, k.d
    n = tiles * P
    with ExitStack() as own:
        ps = k.ps(own, "val_ps", [P, 4, 512])
        out = k.sb(own, "val_out", [P, 4, 512])
        with k.stage() as block:
            @block.tensor
            def _(pe):
                for t in range(tiles):
                    for c in range(2):
                        mm = nc.tensor.matmul(ps[:, t, :], src[:, c, t * P:(t + 1) * P], wv[:, c, :], start=(c == 0), stop=(c == 1))
                    mm.then_inc(k.products, 1)

            @block.scalar
            def _(act):
                for t in range(tiles):
                    act.wait_ge(k.products, t + 1)
                    nc.scalar.activation(out[:, t, :], ps[:, t, :], ACT.Identity).then_inc(k.evacuated, 1)

            @block.sync
            def _(sp):
                sp.dma_start(rows(d["k_full"])[:, :, bass.ds(at, n)], kt[:, :, 0:n]).then_inc(k.stored, 16)
                sp.wait_ge(k.evacuated, tiles)
                sp.dma_start(d["v_full"][bass.ds(at, n), :].rearrange("(c p) f -> p c f", p=P), out[:, 0:tiles, :])\
                    .then_inc(k.stored, 16)
                sp.wait_ge(k.stored, 32)


def l3_cross(k, x):
    nc, d = k.nc, k.d
    sa = Streamed(8, 64, SK + S, 8.0, split=False)
    with ExitStack() as own:
        ot = k.sb(own, "ot", [P, 4, T])
        lat = k.sb(own, "lat", [P, 2, T])
        latb = k.sb(own, "latb", [P, 2, S])
        wq, wkv, wo = k.sb(own, "wq", [P, 2, 512]), k.sb(own, "wkv", [P, 2, 1024]), k.sb(own, "wo", [P, 4, D])
        o = k.sb(own, "att_o", [P, 2, 512])
        wk, wv = wkv[:, :, 0:512], wkv[:, :, 512:1024]
        norm(k, lat[:], x[:], T, 1e-5)
        norm(k, lat[:], lat[:], T, 1e-5, w=k.vec("L3_xattn_ln_l_w"), b=k.vec("L3_xattn_ln_l_b"))
        load(k, [(wq[:], rows(d["L3_xattn_Wq"])), (wkv[:], rows(d["L3_xattn_Wkv"])), (wo[:], rows(d["L3_xattn_Wo"]))])
        with nc.Fori(0, B) as b:
            with ExitStack() as inner:
                ctx, ctxn = k.sb(inner, "ctx", [P, 2, 512]), k.sb(inner, "ctxn", [P, 2, 512])
                kt = k.sb(inner, "kt", [P, 4, 512])
                copy_batch(k, latb[:], lat, b)
                project(k, kt[:, :, 0:S], latb, 2, wq, 4, S)
                unit_norm(k, kt[:, :, 0:S], 4, S, k.vec("q_scale2"), k.head_ones[:])
                with k.stage() as block:
                    @block.sync
                    def _(sp):
                        sp.dma_start(rows(d["q_full"])[:, :, bass.ds(b * S, S)], kt[:, :, 0:S]).then_inc(k.stored, 16)
                        sp.wait_ge(k.stored, 16)
                project(k, kt[:, :, 0:S], latb, 2, wk, 4, S)
                unit_norm(k, kt[:, :, 0:S], 4, S, k.vec("k_scale2"), k.head_ones[:])
                values_and_keys_out(k, latb, wv, 2, kt, SK)
                with nc.Fori(0, SK // 512) as j:
                    norm(k, ctxn[:], ctx[:], 512, 1e-5, w=k.vec("L3_xattn_ln_x_w"), b=k.vec("L3_xattn_ln_x_b"),
                         load_src=rows(d["ctx_t"][b])[:, :, bass.ds(j * 512, 512)])
                    project(k, kt, ctxn, 2, wk, 4, 512)
                    unit_norm(k, kt[:], 4, 512, k.vec("k_scale2"), k.head_ones[:])
                    values_and_keys_out(k, ctxn, wv, 4, kt, j * 512)
            with ExitStack() as inner:
                bufs = streamed_buffers(k, inner, sa, None, o)
                mask_rows(k, sa, bufs[0], bufs[1], "mask_BxS2_bk0", mybir.dt.uint8, b)
                heads_turns(k, sa, bufs, 0, True, False, b)
                heads_turns(k, sa, bufs, 0, False, False, b)
                heads_turns(k, sa, bufs, 1, False, True, b)
            outputs_to_features(k, o, ot, 4, b)
        with ExitStack() as inner:
            h = k.sb(inner, "h", [P, 2, T])
            project(k, h, ot, 4, wo, 2, T)
            norm(k, x[:], h[:], T, 1e-5, w=k.vec("L3_xattn_ln_o_w"), b=k.vec("L3_xattn_ln_o_b"), plus=x)


def l3_self(k, x):
    nc, d = k.nc, k.d
    hd = Heads(16, 16, 0.25)
    with ExitStack() as own:
        h, hk, hv = (k.sb(own, n, [P, 2, T]) for n in ("h", "hk", "hv"))
        hb, hkb, hvb = (k.sb(own, n, [P, 2, S]) for n in ("hb", "hkb", "hvb"))
        qb, kt = k.sb(own, "qb", [P, 4, S]), k.sb(own, "kt", [P, 4, S])
        val = k.sb(own, "val", [P, 2, D])
        ot = k.sb(own, "ot", [P, 2, T])
        wk, wv, wl, wo = (k.sb(own, n, [P, 2, D]) for n in ("wk", "wv", "wl", "wo"))
        wq, wls = k.sb(own, "wq", [P, 2, 512]), k.sb(own, "wls", [P, 2, 512])
        st = attention_state(k, own, hd)
        norm(k, h[:], x[:], T, 1e-5)
        load(k, [(wk[:], rows(d["L3_attn_Wk"])), (wv[:], rows(d["L3_attn_Wv"])), (wl[:], rows(d["L3_attn_Wl"])),
                 (wo[:], rows(d["L3_attn_Wo"])), (wq[:], rows(d["L3_attn_Wq_strips"])), (wls[:], rows(d["L3_attn_Wl_strips"]))])
        project(k, hk, h, 2, wk, 2, T, bias=k.vec("L3_attn_bk"))
        project(k, hv, h, 2, wv, 2, T, bias=k.vec("L3_attn_bv"))
        with nc.Fori(0, B) as b:
            copy_batch(k, hb[:], h, b)
            copy_batch(k, hkb[:], hk, b)
            copy_batch(k, hvb[:], hv, b)
            project(k, qb, hb, 2, wq, 4, S, bias=k.vec("L3_attn_bq_strips"))
            project(k, kt, hkb, 2, wls, 4, S, bias=k.vec("L3_attn_bl_strips"))
            project_tokens(k, val, hvb, 2, wl, 2, D)
            attention_start(k, st)
            attend(k, hd, st, qb, kt, val)
            attention_end(k, hd, st, ot, b, bias=k.vec("L3_attn_bl"))
        project(k, x, ot, 2, wo, 2, T, vec=(k.vec("L3_attn_bo"), ALU.add, x, ALU.add))


def l3_experts(k, x):
    nc = k.nc
    capacity = int(S * 2.0 / 8) + 1
    with ExitStack() as own:
        h = k.sb(own, "h", [P, 2, T])
        norm(k, h[:], x[:], T, 1e-5)
        s, _ = router(k, own, h, "L3_ffn_router_w_t")
        softmax8(k, s)
        st = k.sb(own, "st", [8, T])
        gates_by_expert(k, s, st)
        work = k.sb(own, "work", [8, B, 2, S])
        top = k.sb(own, "top", [8, B, 8])
        wt = k.sb(own, "wt", [8, T])
        with k.stage() as block:
            @block.vector
            def _(v):
                step = Steps(v, k.vec_step)
                for b in range(B):
                    own_scores = st[:, b * S:(b + 1) * S]
                    src = own_scores
                    for r in range((capacity - 1) // 8):
                        step(nc.vector.max(top[:, b, :], src))
                        step(nc.vector.match_replace(work[:, b, r % 2, :], top[:, b, :], src, -1.0))
                        src = work[:, b, r % 2, :]
                    step(nc.vector.max(top[:, b, :], src))
                    last = (capacity - 1) % 8
                    step(nc.vector.tensor_scalar(wt[:, b * S:(b + 1) * S], own_scores, top[:, b, last:last + 1], None, ALU.is_ge))
                nc.vector.tensor_tensor(wt[:], wt[:], st[:], ALU.mult)
        store_gates(k, wt)
        experts_gelu(k, x, h, 8, "L3_ffn_w1", "L3_ffn_w2", "L3_ffn_vecs")


SUBLAYERS = [l0_cross, l0_scan, l0_experts, l1_cross, l1_self, l1_ffn, l2_cross, l2_self, l2_experts,
             l3_cross, l3_self, l3_experts]


def build(nc, d, out, sublayers=tuple(range(len(SUBLAYERS)))):
    with ExitStack() as ctx:
        k = Core(nc, d, ctx)
        x = k.sb(ctx, "x", [P, 2, T])
        k.vecs = k.sb(ctx, "vecs", [P, N_VECS])
        k.ident = k.sb(ctx, "ident", [P, P])
        k.mean_mat = k.sb(ctx, "mean_mat", [P, P])
        k.fold = k.sb(ctx, "fold", [P, 17])
        k.head_ones = k.sb(ctx, "head_ones", [P, P])
        k.cos, k.sin, k.iota = (k.sb(ctx, n, [P, S]) for n in ("cos", "sin", "iota"))
        k.causal = k.sb(ctx, "causal", [P, 2, S])
        load(k, [(x[:], rows(d["x_t"])), (k.vecs[:], d["vecs"]), (k.ident[:], d["const_ident"]),
                 (k.mean_mat[:], d["const_mean"]), (k.head_ones[:], d["const_head_ones"]), (k.cos[:], d["const_cos"]),
                 (k.sin[:], d["const_sin"]), (k.iota[:], d["const_iota"]), (k.fold[:], d["const_fold"]), (k.causal[:], d["const_causal"])])
        for i in sublayers:
            SUBLAYERS[i](k, x)
        with nc.Block() as block:
            @block.sync
            def _(sp):
                sp.dma_start(rows(out), x[:]).then_inc(k.stored, 16)
                sp.wait_ge(k.stored, 16)




def strips(w):
    out = np.zeros(w.shape[:-1] + (16, 32), w.dtype)
    out[..., :16] = w.reshape(w.shape[:-1] + (16, 16))
    return out.reshape(w.shape[:-1] + (512,))


def turned(w):
    h = w.reshape(w.shape[:-1] + (16, 2, 8))
    return np.ascontiguousarray(h[..., ::-1, :]).reshape(w.shape)


def columns(v):
    return np.swapaxes(v.reshape(v.shape[:-1] + (-1, P)), -1, -2)


def constants():
    f = np.float32
    c = {"const_ident": np.eye(P, dtype=f), "const_mean": np.full((P, P), 1.0 / D, f),
         "const_head_ones": np.kron(np.eye(2), np.ones((64, 64))).astype(f),
         "const_fold": np.tile(np.eye(32, 17, dtype=f), (4, 1)),
         "const_iota": np.broadcast_to(np.arange(KB, dtype=f), (P, KB)).copy()}
    inv = 1.0 / 10000.0 ** (np.arange(0, 16, 2).astype(f) / f(16))
    ang = (np.arange(S, dtype=f)[:, None] * inv[None, :].astype(f)).astype(f)
    cos, sin = np.zeros((4, 32, S), f), np.zeros((4, 32, S), f)
    cos[:, 0:8], cos[:, 8:16] = np.cos(ang).T, np.cos(ang).T
    sin[:, 0:8], sin[:, 8:16] = -np.sin(ang).T, np.sin(ang).T
    c["const_cos"], c["const_sin"] = cos.reshape(P, S), sin.reshape(P, S)
    q = np.arange(S).reshape(2, P)
    c["const_causal"] = np.where(np.arange(S)[None, None, :] <= q.T[:, :, None], 0.0, NEG).astype(f)
    return c


def layouts(i):
    t = lambda a: np.swapaxes(a, -1, -2)
    cat = np.concatenate
    a = {"x_t": i["x"].transpose(2, 0, 1).reshape(D, T), "ctx_t": i["ctx_1024"].transpose(0, 2, 1),
         "mask_BxS2_ik1": i["mask_BxS2_ik1"], "mask_BxS2_bk0": i["mask_BxS2_bk0"],
         "seg_row": i["itok_BxS_0_255"].reshape(1, T), "seg_cols": i["itok_BxS_0_255"].reshape(B, 2, P).transpose(0, 2, 1)}
    for n in ("L0_xattn_Wq", "L0_xattn_Wk", "L0_xattn_Wv", "L0_xattn_Wo", "L0_ffn_gate_bias", "L1_attn_w_o", "L2_attn_q_w", "L2_attn_k_w", "L2_attn_v_w",
              "L2_attn_out_w", "L2_attn_q_b", "L2_attn_k_b", "L2_attn_v_b", "L2_attn_rel_emb", "L2_attn_grep_b", "L2_ffn_gate_b",
              "L3_xattn_Wq", "L3_xattn_Wkv", "L3_xattn_Wo", "L3_attn_Wk", "L3_attn_Wv", "L3_attn_Wl", "L3_attn_Wo",
              "L3_ffn_w1", "L3_ffn_w2"):
        a[n] = i[n]
    for n in ("L0_attn_w_in", "L0_attn_w_out", "L0_attn_w_dt", "L0_ffn_gate_w", "L1_xattn_Wk", "L1_xattn_Wv", "L1_xattn_Wq",
              "L1_xattn_Wo", "L2_ffn_gate_w", "L3_ffn_router_w"):
        a[n + "_t"] = t(i[n])
    a["L0_attn_w_xproj_t"] = cat([t(i["L0_attn_w_xproj"]), np.zeros((512, 32), np.float32)], 1)
    a["L0_ffn_up"] = t(cat([i["L0_ffn_Wu"], i["L0_ffn_sWu"][None]]))
    a["L0_ffn_down"] = t(cat([i["L0_ffn_Wd"], i["L0_ffn_sWd"][None]]))
    a["L0_ffn_vecs"] = columns(cat([cat([i["L0_ffn_bu"], i["L0_ffn_sbu"][None]]), cat([i["L0_ffn_bd"], i["L0_ffn_sbd"][None]])], 1))
    for n in "qkv":
        a[f"L1_attn_w_{n}_t"] = i[f"L1_attn_w_{n}"].transpose(1, 0, 2).reshape(D, 1024)
    for n in ("w1", "w2", "h1", "h2", "w3"):
        a[f"L1_ffn_{n}_t"] = t(i[f"L1_ffn_{n}_w"])
    wqkv, bqkv = t(i["L2_xattn_Wqkv"]), i["L2_xattn_bqkv"]
    a["L2_qk_strips"] = cat([strips(wqkv[..., 0:D]), strips(turned(wqkv[..., 0:D])),
                             strips(wqkv[..., D:2 * D]), strips(turned(wqkv[..., D:2 * D]))], -1)
    a["L2_wv"], a["L2_wo"] = wqkv[..., 2 * D:], t(i["L2_xattn_Wo"])
    a["L2_qc_strips"] = strips(t(i["L2_xattn_Wq_c"]))
    a["L2_kc_strips"] = strips(t(i["L2_xattn_Wkv_c"][:, 0:D]))
    a["L2_wvc"], a["L2_woc"] = t(i["L2_xattn_Wkv_c"][:, D:]), t(i["L2_xattn_Wo_c"])
    a["L2_wg"], a["L2_wu"], a["L2_wd"] = t(i["L2_xattn_Wg"]), t(i["L2_xattn_Wu"]), t(i["L2_xattn_Wd"])
    a["L2_vecs"] = columns(cat([strips(bqkv[:, 0:D]), strips(turned(bqkv[:, 0:D])), strips(bqkv[:, D:2 * D]),
                                strips(turned(bqkv[:, D:2 * D])), bqkv[:, 2 * D:], i["L2_xattn_bo"], i["L2_xattn_n1"],
                                i["L2_xattn_n2"], i["L2_xattn_n3"]], 1))
    a["L2_attn_bias_k_row"], a["L2_attn_bias_v_row"] = i["L2_attn_bias_k"].reshape(D), i["L2_attn_bias_v"].reshape(D)
    a["L2_attn_grep_w_row"], a["L2_attn_grep_a_row"] = i["L2_attn_grep_w"].reshape(128), i["L2_attn_grep_a"].reshape(16)
    halves = lambda w: cat([w[:, 0::2], w[:, 1::2]], 1)
    for n in ("1", "3"):
        a[f"L2_ffn_w{n}"] = t(halves(cat([i[f"L2_ffn_w{n}"], i[f"L2_ffn_sw{n}"][None]])))
    a["L2_ffn_w2"] = t(cat([i["L2_ffn_w2"], i["L2_ffn_sw2"][None]]))
    a["L2_ffn_vecs"] = columns(cat([halves(cat([i["L2_ffn_b1"], i["L2_ffn_sb1"][None]])),
                                    halves(cat([i["L2_ffn_b3"], i["L2_ffn_sb3"][None]])),
                                    cat([i["L2_ffn_b2"], i["L2_ffn_sb2"][None]])], 1))
    a["L3_attn_Wq_strips"], a["L3_attn_Wl_strips"] = strips(i["L3_attn_Wq"]), strips(i["L3_attn_Wl"])
    a["L3_ffn_vecs"] = columns(cat([i["L3_ffn_b1"], i["L3_ffn_b2"]], 1))
    conv = i["L0_attn_w_conv"].reshape(4, P, 4).transpose(1, 0, 2).reshape(P, 16)
    a_log = i["L0_attn_A_log"].reshape(4, P, 16).transpose(1, 2, 0).reshape(P, 64)
    own = {"q_scale2": np.tile(i["L3_xattn_q_scale"], 2)[:, None], "k_scale2": np.tile(i["L3_xattn_k_scale"], 2)[:, None],
           "conv": conv, "A_log": a_log, "L3_attn_bq_strips": columns(strips(i["L3_attn_bq"])),
           "L3_attn_bl_strips": columns(strips(i["L3_attn_bl"]))}
    a["vecs"] = cat([own[n] if n in own else columns(i[n]) for n, _ in VECS], 1)
    return {n: np.ascontiguousarray(v) for n, v in a.items()}


SCRATCH = (("bc_rows", (32, T), F32), ("gate_rows", (9, T), F32), ("k_parts", (3, D, SK), BF16), ("q_parts", (3, D, T), BF16),
           ("k_full", (512, SK + S), F32), ("q_full", (512, T), F32), ("v_full", (SK + S, 512), F32))


def kernel(**inputs):
    import concourse.bacc as bacc
    from concourse.bass_utils import run_bass_kernel_spmd

    arrays = {**layouts({n: np.asarray(v) for n, v in inputs.items()}), **constants()}
    nc = bacc.Bacc("TRN2", target_bir_lowering=False, num_devices=1)
    d = {n: nc.dram_tensor(n, v.shape, mybir.dt.from_np(v.dtype), kind="ExternalInput").ap() for n, v in arrays.items()}
    for name, shape, dt in SCRATCH:
        d[name] = nc.dram_tensor(name, shape, dt, kind="Internal").ap()
    out = nc.dram_tensor("out_t", (D, T), F32, kind="ExternalOutput").ap()
    build(nc, d, out)
    r = run_bass_kernel_spmd(nc, [arrays], core_ids=[0])
    return np.ascontiguousarray(r.results[0]["out_t"].reshape(D, B, S).transpose(1, 2, 0))
```

```python
from contextlib import ExitStack, contextmanager

import concourse.bass as bass
import numpy as np
from concourse import mybir

P = 128
D = 256
B = 2
S = 256
T = B * S
SK = 4096
KB = 256
F32 = mybir.dt.float32
BF16 = mybir.dt.bfloat16
ACT = mybir.ActivationFunctionType
ALU = mybir.AluOpType
AX = mybir.AxisListType.X
NEG = -1e30
START_MAX = -1e31

VECS = [("L0_attn_b_dt", 4), ("L0_attn_D", 4), ("L1_xattn_bv", 2), ("L1_xattn_bq", 2), ("L1_xattn_bo", 2),
        ("L1_ffn_w1_s", 8), ("L1_ffn_w2_s", 8), ("L1_ffn_h1_s", 8), ("L1_ffn_h2_s", 8), ("L1_ffn_w3_s", 2),
        ("L2_xattn_nf", 2), ("L2_attn_out_b", 2), ("L3_xattn_ln_x_w", 2), ("L3_xattn_ln_x_b", 2),
        ("L3_xattn_ln_l_w", 2), ("L3_xattn_ln_l_b", 2), ("q_scale2", 1), ("k_scale2", 1),
        ("L3_xattn_ln_o_w", 2), ("L3_xattn_ln_o_b", 2), ("L3_attn_bq", 2), ("L3_attn_bk", 2),
        ("L3_attn_bv", 2), ("L3_attn_bl", 2), ("L3_attn_bo", 2), ("conv", 16),
        ("A_log", 64), ("eps_5", 1), ("eps_6", 1)]
VEC_AT, _n = {}, 0
for _name, _c in VECS:
    VEC_AT[_name] = (_n, _n + _c)
    _n += _c
N_VECS = _n

LAYER_VECS = {"bqk": (0, 8), "bv": (8, 10), "bo": (10, 12), "n1": (12, 14), "n2": (14, 16), "n3": (16, 18)}

SEMS = ["loaded", "stored", "products", "act_done", "vec_done", "vec_step", "evacuated", "pool_done",
        "scored", "shifted", "exps", "turned", "unturned", "weighted", "merged", "loaded_next", "ring_0", "ring_1", "ring_2",
        "ring_3", "values_0", "values_1", "means", "squared", "mean_squares", "roots", "normed"]


class Core:

    def __init__(self, nc, d, ctx):
        self.nc, self.d, self.ctx, self.count = nc, d, ctx, 0
        self.sems = [ctx.enter_context(nc.semaphore(n)) for n in SEMS]
        (self.loaded, self.stored, self.products, self.act_done, self.vec_done, self.vec_step, self.evacuated,
         self.pool_done, self.scored, self.shifted, self.exps, self.turned, self.unturned, self.weighted,
         self.merged, self.loaded_next, *others) = self.sems
        self.ring_in, self.values_in = others[0:4], others[4:6]
        self.means, self.squared, self.mean_squares, self.roots, self.normed = others[6:11]
        nums = [s.num for s in self.sems]
        assert nums == list(range(nums[0], nums[0] + len(nums)))
        self.sem_range = range(nums[0], nums[0] + len(nums))

    def name(self, what):
        self.count += 1
        return f"{what}_{self.count}"

    def sb(self, stack, what, shape, dt=F32):
        return stack.enter_context(self.nc.sbuf_tensor(self.name(what), shape, dt))

    def ps(self, stack, what, shape, dt=F32):
        return stack.enter_context(self.nc.psum_tensor(self.name(what), shape, dt))

    @contextmanager
    def stage(self):
        with self.nc.Block() as block:
            yield block
        self.nc.sync.sem_clear(self.sem_range)
        self.nc.all_engine_barrier()

    def vec(self, name):
        a, b = VEC_AT[name]
        return self.vecs[:, a:b]


class Steps:

    def __init__(self, eng, sem):
        self.eng, self.sem, self.n = eng, sem, 0

    def __call__(self, instruction):
        instruction.then_inc(self.sem, 1)
        self.n += 1
        self.eng.wait_ge(self.sem, self.n)


def rows(w):
    return w.rearrange("(c p) m -> p c m", p=P)


def load(k, pairs):
    with k.stage() as block:
        @block.sync
        def _(sp):
            for dst, src in pairs:
                sp.dma_start(dst, src).then_inc(k.loaded, 16)
            sp.wait_ge(k.loaded, 16 * len(pairs))


def project(k, dst, src, kc, w, mc, n, loads=(), func=ACT.Identity, bias=None, scale=1.0, vec=None, ahead=(),
            meanwhile=None):
    nc = k.nc
    with ExitStack() as own:
        ps = k.ps(own, "proj_ps", [P, 4, 512])
        with k.stage() as block:
            @block.sync
            def _(sp):
                for to, fr in loads:
                    sp.dma_start(to, fr).then_inc(k.loaded, 16)
                for to, fr in ahead:
                    sp.dma_start(to, fr).then_inc(k.loaded_next, 16)
                if ahead:
                    sp.wait_ge(k.loaded_next, 16 * len(ahead))

            @block.tensor
            def _(pe):
                if loads:
                    pe.wait_ge(k.loaded, 16 * len(loads))
                for m in range(mc):
                    if m >= 4:
                        pe.wait_ge(k.evacuated, m - 3)
                    for c in range(kc):
                        mm = nc.tensor.matmul(ps[:, m % 4, 0:n], w[:, c, m * P:(m + 1) * P], src[:, c, :],
                                              start=(c == 0), stop=(c == kc - 1))
                    mm.then_inc(k.products, 1)

            @block.scalar
            def _(act):
                if vec is None:
                    if loads:
                        act.wait_ge(k.loaded, 16 * len(loads))
                    for m in range(mc):
                        act.wait_ge(k.products, m + 1)
                        nc.scalar.activation(
                            dst[:, m, :], ps[:, m % 4, 0:n], func,
                            bias=0.0 if bias is None else bias[:, m:m + 1],
                            scale=scale if isinstance(scale, float) else scale[:, m:m + 1],
                        ).then_inc(k.evacuated, 1)

            @block.vector
            def _(v):
                if vec is not None:
                    col, op0, other, op1 = vec
                    if loads:
                        v.wait_ge(k.loaded, 16 * len(loads))
                    for m in range(mc):
                        v.wait_ge(k.products, m + 1)
                        nc.vector.scalar_tensor_tensor(
                            out=dst[:, m, :], in0=ps[:, m % 4, 0:n],
                            scalar=col if isinstance(col, float) else col[:, m:m + 1],
                            in1=other[:, m, :], op0=op0, op1=op1).then_inc(k.evacuated, 1)
                if meanwhile is not None:
                    meanwhile(v)


def project_tokens(k, dst, src, kc, w, tiles, nf, loads=(), bias_rows=None, strips_of=None, meanwhile=None):
    nc = k.nc
    nb = (nf + 511) // 512
    fb = nf // nb
    with ExitStack() as own:
        ps = k.ps(own, "tok_ps", [P, 4, 512])
        with k.stage() as block:
            @block.sync
            def _(sp):
                for to, fr in loads:
                    sp.dma_start(to, fr).then_inc(k.loaded, 16)

            @block.tensor
            def _(pe):
                if loads:
                    pe.wait_ge(k.loaded, 16 * len(loads))
                i = 0
                for t in range(tiles):
                    for f in range(nb):
                        if i >= 4:
                            pe.wait_ge(k.evacuated, i - 3)
                        for c in range(kc):
                            mm = nc.tensor.matmul(ps[:, i % 4, 0:fb], src[:, c, t * P:(t + 1) * P],
                                                  w[:, c, f * fb:(f + 1) * fb], start=(c == 0), stop=(c == kc - 1))
                        mm.then_inc(k.products, 1)
                        i += 1

            @block.scalar
            def _(act):
                if bias_rows is None:
                    for i in range(tiles * nb):
                        act.wait_ge(k.products, i + 1)
                        if strips_of is None:
                            to, fr = dst[:, i // nb, (i % nb) * fb:(i % nb + 1) * fb], ps[:, i % 4, 0:fb]
                        else:
                            to = dst[:, i, :, 0:nf // strips_of]
                            fr = ps[:, i % 4, 0:fb].rearrange("p (h x) -> p h x", h=strips_of)
                        nc.scalar.activation(to, fr, ACT.Identity).then_inc(k.evacuated, 1)

            @block.vector
            def _(v):
                if bias_rows is not None:
                    if loads:
                        v.wait_ge(k.loaded, 16 * len(loads))
                    for i in range(tiles * nb):
                        v.wait_ge(k.products, i + 1)
                        nc.vector.tensor_tensor(dst[:, i // nb, (i % nb) * fb:(i % nb + 1) * fb], ps[:, i % 4, 0:fb],
                                                bias_rows[:, (i % nb) * fb:(i % nb + 1) * fb],
                                                ALU.add).then_inc(k.evacuated, 1)
                if meanwhile is not None:
                    meanwhile(v)


def norm(k, dst, src, eps, mean=True, w=None, b=None, plus=None, ahead=()):
    nc = k.nc
    halves = [slice(i * S, (i + 1) * S) for i in range(B)]
    eps_col = k.vec({1e-5: "eps_5", 1e-6: "eps_6"}[eps])
    with ExitStack() as own:
        mean_ps, square_ps = k.ps(own, "mean_ps", [P, B, 512]), k.ps(own, "square_ps", [P, B, 512])
        centred = k.sb(own, "centred", [P, 2, T]) if mean else src
        squares = k.sb(own, "squares", [P, 2, T])
        root = k.sb(own, "root", [P, T])
        with k.stage() as block:
            @block.sync
            def _(sp):
                for to, fr in ahead:
                    sp.dma_start(to, fr).then_inc(k.loaded, 16)
                if ahead:
                    sp.wait_ge(k.loaded, 16 * len(ahead))

            @block.tensor
            def _(pe):
                if mean:
                    for i, half in enumerate(halves):
                        for c in range(2):
                            mm = nc.tensor.matmul(mean_ps[:, i, 0:S], k.mean_mat[:], src[:, c, half], start=(c == 0), stop=(c == 1))
                        mm.then_inc(k.means, 1)
                for i, half in enumerate(halves):
                    pe.wait_ge(k.squared, i + 1)
                    for c in range(2):
                        mm = nc.tensor.matmul(square_ps[:, i, 0:S], k.mean_mat[:], squares[:, c, half], start=(c == 0), stop=(c == 1))
                    mm.then_inc(k.mean_squares, 1)

            @block.scalar
            def _(act):
                for i, half in enumerate(halves):
                    if mean:
                        act.wait_ge(k.normed, i + 1)
                    nc.scalar.activation(squares[:, :, half], centred[:, :, half], ACT.Square).then_inc(k.squared, 1)
                for i, half in enumerate(halves):
                    act.wait_ge(k.mean_squares, i + 1)
                    nc.scalar.activation(root[:, half], square_ps[:, i, 0:S], ACT.Sqrt, bias=eps_col).then_inc(k.roots, 1)

            @block.vector
            def _(v):
                step = Steps(v, k.vec_step)
                if mean:
                    for i, half in enumerate(halves):
                        v.wait_ge(k.means, i + 1)
                        nc.vector.tensor_tensor(centred[:, :, half], src[:, :, half], mean_ps[:, i, 0:S].unsqueeze(1).broadcast_to([P, 2, S]),
                                                ALU.subtract).then_inc(k.normed, 1)
                for i, half in enumerate(halves):
                    v.wait_ge(k.roots, i + 1)
                    step(nc.vector.reciprocal(root[:, half], root[:, half]))
                    if w is None:
                        nc.vector.tensor_tensor(dst[:, :, half], centred[:, :, half], root[:, half].unsqueeze(1).broadcast_to([P, 2, S]), ALU.mult)
                        continue
                    for c in range(2):
                        to = dst[:, c, half] if b is None and plus is None else squares[:, c, half]
                        scaled = nc.vector.scalar_tensor_tensor(out=to, in0=centred[:, c, half], scalar=w[:, c:c + 1], in1=root[:, half],
                                                                op0=ALU.mult, op1=ALU.mult)
                        if plus is not None and b is not None:
                            step(scaled)
                            nc.vector.scalar_tensor_tensor(out=dst[:, c, half], in0=squares[:, c, half], scalar=b[:, c:c + 1],
                                                           in1=plus[:, c, half], op0=ALU.add, op1=ALU.add)
                        elif plus is not None:
                            step(scaled)
                            nc.vector.tensor_tensor(dst[:, c, half], squares[:, c, half], plus[:, c, half], ALU.add)
                        elif b is not None:
                            step(scaled)
                            nc.vector.tensor_scalar(dst[:, c, half], squares[:, c, half], b[:, c:c + 1], None, ALU.add)


def copy_batch(k, dst, src, b):
    with k.stage() as block:
        @block.vector
        def _(v):
            k.nc.vector.tensor_copy(dst, src[:, :, bass.ds(b * S, S)])


class Heads:

    def __init__(self, n, dim, scale):
        self.n, self.dim, self.scale = n, dim, scale
        self.wide = max(1, dim // P)
        self.rows = {16: 32, 64: 64, 256: P}[dim]
        self.places = P // self.rows
        self.chunks = n * self.wide // self.places
        self.per = min(4, n // self.places)
        self.groups = [(place, c0) for place in range(self.places)
                       for c0 in range(0, n // self.places, self.per)]

    def members(self, group):
        place, c0 = group
        return [(c, c * self.places + place) for c in range(c0, c0 + self.per)]

    def of_group(self, flat, group):
        place, c0 = group
        return flat.rearrange("p (c s x) -> p c s x", s=self.places, c=self.n // self.places)[:, c0:c0 + self.per, place, :]


def attention_state(k, own, hd):
    return {"o": k.sb(own, "att_o", [P, 2, hd.n * hd.dim]), "m": k.sb(own, "att_m", [P, 2, hd.n]),
            "l": k.sb(own, "att_l", [P, 2, hd.n])}


def attention_start(k, st):
    with k.stage() as block:
        @block.vector
        def _(v):
            k.nc.vector.memset(st["o"][:], 0.0)
            k.nc.vector.memset(st["m"][:], START_MAX)
            k.nc.vector.memset(st["l"][:], 0.0)


def attend(k, hd, st, q, kt, val):
    nc = k.nc
    units = [(qt, g) for qt in range(2) for g in hd.groups]
    per, dim = hd.per, hd.dim
    nu = len(units)
    with ExitStack() as own:
        score_ps = k.ps(own, "score_ps", [P, 2, 4, KB])
        turn_ps = k.ps(own, "turn_ps", [P, 8, P])
        out_ps = k.ps(own, "out_ps", [P, 2, 512])
        prob = k.sb(own, "prob", [P, 2, per, KB])
        prob_t = k.sb(own, "prob_t", [P, 2, per * 2, P])
        top = k.sb(own, "top", [P, 2, per])
        new_max = k.sb(own, "new_max", [P, 2, per])
        drop = k.sb(own, "drop", [P, 2, per])
        fade = k.sb(own, "fade", [P, 2, per])
        part = k.sb(own, "part", [P, 2, per])
        with k.stage() as block:
            @block.tensor
            def _(pe):
                def scores(u):
                    qt, g = units[u]
                    if u >= 2:
                        pe.wait_ge(k.shifted, u - 1)
                    for i, (c, _) in enumerate(hd.members(g)):
                        p0 = g[0] * hd.rows
                        for w in range(hd.wide):
                            mm = nc.tensor.matmul(
                                score_ps[:, u % 2, i, :], q[p0:p0 + hd.rows, c * hd.wide + w, qt * P:(qt + 1) * P],
                                kt[p0:p0 + hd.rows, c * hd.wide + w, :], start=(w == 0), stop=(w == hd.wide - 1))
                    mm.then_inc(k.scored, 1)

                def turn(u):
                    pe.wait_ge(k.exps, u + 1)
                    if u >= 1:
                        pe.wait_ge(k.unturned, u)
                    for i in range(per):
                        for c in range(2):
                            mm = nc.tensor.transpose(turn_ps[:, 2 * i + c, :], prob[:, u % 2, i, c * P:(c + 1) * P], k.ident[:])
                    mm.then_inc(k.turned, 1)

                def weigh(u):
                    _, g = units[u]
                    pe.wait_ge(k.unturned, u + 1)
                    if u >= 2:
                        pe.wait_ge(k.merged, u - 1)
                    for i, (_, h) in enumerate(hd.members(g)):
                        for c in range(2):
                            mm = nc.tensor.matmul(out_ps[:, u % 2, i * dim:(i + 1) * dim], prob_t[:, u % 2, 2 * i + c, :],
                                                  val[:, c, h * dim:(h + 1) * dim], start=(c == 0), stop=(c == 1))
                    mm.then_inc(k.weighted, 1)

                for u in range(nu + 2):
                    if u < nu:
                        scores(u)
                    if 1 <= u <= nu:
                        turn(u - 1)
                    if u >= 2:
                        weigh(u - 2)

            @block.scalar
            def _(act):
                for u in range(nu + 1):
                    if u < nu:
                        act.wait_ge(k.shifted, u + 1)
                        nc.scalar.activation(fade[:, u % 2, :], drop[:, u % 2, :], ACT.Exp, scale=hd.scale)
                        nc.scalar.activation(prob[:, u % 2], prob[:, u % 2], ACT.Exp, scale=hd.scale).then_inc(k.exps, 1)
                    if u >= 1:
                        act.wait_ge(k.turned, u)
                        if u >= 3:
                            act.wait_ge(k.weighted, u - 2)
                        nc.scalar.activation(prob_t[:, (u - 1) % 2], turn_ps[:, 0:2 * per, :],
                                             ACT.Identity).then_inc(k.unturned, 1)

            @block.vector
            def _(v):
                step = Steps(v, k.vec_step)

                def maxima(u):
                    qt, g = units[u]
                    j = u % 2
                    m = hd.of_group(st["m"][:, qt, :], g)[:, :, 0]
                    v.wait_ge(k.scored, u + 1)
                    src = score_ps[:, j, 0:per, :]
                    step(nc.vector.tensor_reduce(top[:, j, :], src, AX, ALU.max))
                    step(nc.vector.tensor_tensor(new_max[:, j, :], m, top[:, j, :], ALU.max))
                    if u >= 2:
                        v.wait_ge(k.turned, u - 1)
                    step(nc.vector.tensor_tensor(drop[:, j, :], m, new_max[:, j, :], ALU.subtract))
                    step(nc.vector.tensor_copy(m, new_max[:, j, :]))
                    nc.vector.tensor_tensor(prob[:, j], src, new_max[:, j, :].unsqueeze(2).broadcast_to([P, per, KB]),
                                            ALU.subtract).then_inc(k.shifted, 1)

                def sums(u):
                    qt, g = units[u]
                    j = u % 2
                    l = hd.of_group(st["l"][:, qt, :], g)[:, :, 0]
                    o = hd.of_group(st["o"][:, qt, :], g)
                    v.wait_ge(k.exps, u + 1)
                    step(nc.vector.reduce_sum(part[:, j, :], prob[:, j], AX))
                    step(nc.vector.tensor_tensor(l, l, fade[:, j, :], ALU.mult))
                    step(nc.vector.tensor_tensor(l, l, part[:, j, :], ALU.add))
                    step(nc.vector.tensor_tensor(o, o, fade[:, j, :].unsqueeze(2).broadcast_to([P, per, dim]), ALU.mult))

                def merge(u):
                    qt, g = units[u]
                    o = hd.of_group(st["o"][:, qt, :], g)
                    v.wait_ge(k.weighted, u + 1)
                    nc.vector.tensor_tensor(o, o, out_ps[:, u % 2, 0:per * dim].rearrange("p (a x) -> p a x", a=per),
                                            ALU.add).then_inc(k.merged, 1)
                    v.wait_ge(k.merged, u + 1)

                for u in range(nu + 2):
                    if u < nu:
                        maxima(u)
                    if 1 <= u <= nu:
                        sums(u - 1)
                    if u >= 2:
                        merge(u - 2)


def attention_end(k, hd, st, dst, b, bias=None):
    nc = k.nc
    nf = hd.n * hd.dim
    with ExitStack() as own:
        ps = k.ps(own, "end_ps", [P, 4, 512])
        with k.stage() as block:
            @block.vector
            def _(v):
                step = Steps(v, k.vec_step)
                step(nc.vector.reciprocal(st["l"][:], st["l"][:]))
                for qt in range(2):
                    o = st["o"][:, qt, :].rearrange("p (h x) -> p h x", h=hd.n)
                    nc.vector.tensor_tensor(o, o, st["l"][:, qt, :].unsqueeze(2).broadcast_to([P, hd.n, hd.dim]),
                                            ALU.mult).then_inc(k.vec_done, 1)

            @block.tensor
            def _(pe):
                pe.wait_ge(k.vec_done, 2)
                for c in range(nf // P):
                    if c >= 4:
                        pe.wait_ge(k.evacuated, c - 3)
                    for qt in range(2):
                        mm = nc.tensor.transpose(ps[:, c % 4, qt * P:(qt + 1) * P], st["o"][:, qt, c * P:(c + 1) * P], k.ident[:])
                    mm.then_inc(k.products, 1)

            @block.scalar
            def _(act):
                for c in range(nf // P):
                    act.wait_ge(k.products, c + 1)
                    nc.scalar.activation(dst[:, c, bass.ds(b * S, S)], ps[:, c % 4, 0:S], ACT.Identity,
                                         bias=0.0 if bias is None else bias[:, c:c + 1]).then_inc(k.evacuated, 1)


class Narrow:

    heads, dim, scale = 16, 16, 0.25

    def __init__(self, k, own):
        self.qz = k.sb(own, "qz", [P, B, 16, S])
        self.val = k.sb(own, "val_strips", [P, 2 * B, 16, 32])
        self.top = k.sb(own, "top", [P, 2 * B, 16])
        self.top_t = k.sb(own, "top_t", [32, 2 * B, P], BF16)
        self.o = k.sb(own, "att_o", [P, 2 * B, D])
        self.l = k.sb(own, "att_l", [P, 2 * B, 16])
        self.prob = k.sb(own, "prob", [P, 2, 4, S])
        self.acc = k.sb(own, "acc", [P, 2, S])
        self.block_top = k.sb(own, "block_top", [P, 2, 4])
        self.hi, self.hi_f = k.sb(own, "hi", [P, 2 * B, 16], BF16), k.sb(own, "hi_f", [P, 2 * B, 2, 16])
        nc = k.nc
        with k.stage() as block:
            @block.gpsimd
            def _(pool):
                nc.gpsimd.memset(self.val[:], 0.0).then_inc(k.pool_done, 1)
                pool.wait_ge(k.pool_done, 1)
                nc.gpsimd.memset(self.val[:, :, :, 16:17], 1.0)

    def spread(self, k, v, q, c, b):
        return k.nc.vector.tensor_tensor(self.qz[:, b, 8 * c:8 * c + 8, :], q.unsqueeze(1).broadcast_to([P, 8, S]),
                                         k.head_rows[:].unsqueeze(2).broadcast_to([P, 8, S]), ALU.mult)


    def start(self, k):
        k.nc.vector.memset(self.top[:], START_MAX)
        k.nc.vector.memset(self.o[:], 0.0)
        k.nc.vector.memset(self.l[:], 0.0)

    def spread_and_start(self, k, q):
        def work(v):
            self.start(k)
            for c in range(2):
                v.wait_ge(k.evacuated, c + 1)
                for b in range(B):
                    self.spread(k, v, q[:, c, b * S:(b + 1) * S], c, b)
        return work


def narrow_maxima(k, at, keys, mask=None, causal=False):
    nc = k.nc
    units = [(b, qt, g) for b in range(B) for qt in range(2) for g in range(4)]
    with ExitStack() as own:
        ps = k.ps(own, "ps_a", [P, 3, 4, KB])
        with k.stage() as block:
            @block.tensor
            def _(pe):
                for u, (b, qt, g) in enumerate(units):
                    if u >= 3:
                        pe.wait_ge(k.shifted, u - 2)
                    n = P if causal and qt == 0 else KB
                    for i in range(4):
                        h = 4 * g + i
                        mm = nc.tensor.matmul(ps[:, u % 3, i, 0:n], at.qz[:, b, h, qt * P:(qt + 1) * P], keys(h // 8, b)[:, 0:n],
                                              start=True, stop=mask is None)
                        if mask is not None:
                            mm = nc.tensor.matmul(ps[:, u % 3, i, 0:n], k.ident_b[:], mask(b, qt)[:, 0:n], start=False, stop=True)
                    mm.then_inc(k.scored, 1)

            @block.vector
            def _(v):
                for u, (b, qt, g) in enumerate(units):
                    v.wait_ge(k.scored, u + 1)
                    if u >= 2:
                        v.wait_ge(k.merged, u - 1)
                    n = P if causal and qt == 0 else KB
                    nc.vector.tensor_reduce(at.block_top[:, u % 2, :], ps[:, u % 3, :, 0:n], AX, ALU.max).then_inc(k.shifted, 1)
                    v.wait_ge(k.shifted, u + 1)
                    top = at.top[:, 2 * b + qt, 4 * g:4 * g + 4]
                    nc.vector.tensor_tensor(top, top, at.block_top[:, u % 2, :], ALU.max).then_inc(k.merged, 1)


def narrow_turn(k, at):
    nc = k.nc
    with ExitStack() as own:
        ps = k.ps(own, "top_ps", [P, 2 * B, P])
        with k.stage() as block:
            @block.vector
            def _(v):
                step = Steps(v, k.vec_step)
                step(nc.vector.tensor_scalar(at.hi[:], at.top[:], -1.0, None, ALU.mult))
                step(nc.vector.tensor_copy(at.hi_f[:, :, 0, :], at.hi[:]))
                nc.vector.scalar_tensor_tensor(out=at.hi_f[:, :, 1, :], in0=at.top[:], scalar=-1.0, in1=at.hi[:],
                                               op0=ALU.mult, op1=ALU.subtract).then_inc(k.vec_done, 1)

            @block.tensor
            def _(pe):
                pe.wait_ge(k.vec_done, 1)
                for t in range(2 * B):
                    mm = nc.tensor.transpose(ps[0:32, t, :], at.hi_f[:, t].rearrange("p a h -> p (a h)"), k.ident[:])
                mm.then_inc(k.products, 1)

            @block.scalar
            def _(act):
                act.wait_ge(k.products, 1)
                nc.scalar.activation(at.top_t[:], ps[0:32], ACT.Identity)


def narrow_sums(k, at, keys, mask=None, causal=False, loads=()):
    nc = k.nc
    first = lambda kc: P if causal and kc == 1 else 0
    units = [(b, g, kc) for b in range(B) for g in range(4) for kc in range(2)]
    nu = len(units)
    with ExitStack() as own:
        ps = k.ps(own, "ps_b", [P, 2, 4, S])
        ps_o = k.ps(own, "ps_o", [P, 2, 512])
        ps_f = k.ps(own, "ps_f", [P, 2, 2, S])
        with k.stage() as block:
            @block.sync
            def _(sp):
                for to, fr in loads:
                    sp.dma_start(to, fr).then_inc(k.loaded, 16)
                if loads:
                    sp.wait_ge(k.loaded, 16 * len(loads))

            @block.tensor
            def _(pe):
                def scores(u):
                    b, g, kc = units[u]
                    if u >= 2:
                        pe.wait_ge(k.exps, u - 1)
                    for i in range(4):
                        h = 4 * g + i
                        q0 = first(kc)
                        out = ps[:, u % 2, i, q0:S]
                        nc.tensor.matmul(out, keys(h // 8, b, kc), at.qz[:, b, h, q0:S], start=True, stop=False)
                        if mask is not None:
                            nc.tensor.matmul(out, k.ident_b[:], mask(b, kc)[:, q0:S], start=False, stop=False)
                        mm = nc.tensor.matmul(out, k.pick_head[:, h, :],
                                              at.top_t[:, 2 * b:2 * b + 2, :].rearrange("p a q -> p (a q)")[:, q0:S],
                                              start=False, stop=True)
                    mm.then_inc(k.scored, 1)

                def weigh(u):
                    b, g, kc = units[u]
                    n = u // 2
                    if kc == 0 and n >= 2:
                        pe.wait_ge(k.turned, n - 1)
                    pe.wait_ge(k.exps, u + 1)
                    for i in range(4):
                        q0 = first(kc)
                        mm = nc.tensor.matmul(ps_o[32 * i:32 * i + 32, n % 2, q0:S], at.val[:, 2 * b + kc, 4 * g + i, :],
                                              at.prob[:, u % 2, i, q0:S], start=(kc == 0), stop=(kc == 1))
                    mm.then_inc(k.weighted, 1)

                def turn(n):
                    pe.wait_ge(k.turned, n + 1)
                    if n >= 2:
                        pe.wait_ge(k.merged, n - 1)
                    for qt in range(2):
                        mm = nc.tensor.transpose(ps_f[:, n % 2, qt, 0:P], at.acc[:, n % 2, qt * P:(qt + 1) * P], k.ident[:])
                    mm.then_inc(k.unturned, 1)

                for u in range(nu + 1):
                    if u < nu:
                        scores(u)
                    if u >= 1:
                        weigh(u - 1)
                    if u >= 3 and u % 2:
                        turn((u - 3) // 2)
                turn(nu // 2 - 1)

            @block.scalar
            def _(act):
                def copy(n):
                    act.wait_ge(k.weighted, 2 * n + 2)
                    if n >= 2:
                        act.wait_ge(k.unturned, n - 1)
                    nc.scalar.activation(at.acc[:, n % 2, :], ps_o[:, n % 2, 0:S], ACT.Identity).then_inc(k.turned, 1)

                for u in range(nu):
                    act.wait_ge(k.scored, u + 1)
                    if u >= 2:
                        act.wait_ge(k.weighted, u - 1)
                    q0 = first(units[u][2])
                    nc.scalar.activation(at.prob[:, u % 2, :, q0:S], ps[:, u % 2, :, q0:S], ACT.Exp, scale=at.scale).then_inc(k.exps, 1)
                    if u >= 2 and u % 2 == 0:
                        copy(u // 2 - 1)
                copy(nu // 2 - 1)

            @block.vector
            def _(v):
                for n in range(nu // 2):
                    b, g = n // 4, n % 4
                    v.wait_ge(k.unturned, n + 1)
                    sums = ps_f[:, n % 2, :, 0:P].rearrange("p a (i x) -> p a i x", i=4)
                    o = at.o[:, 2 * b:2 * b + 2, 64 * g:64 * g + 64].rearrange("p a (i x) -> p a i x", i=4)
                    l = at.l[:, 2 * b:2 * b + 2, 4 * g:4 * g + 4]
                    nc.vector.tensor_tensor(l, l, sums[:, :, :, 16], ALU.add)
                    nc.vector.tensor_tensor(o, o, sums[:, :, :, 0:16], ALU.add).then_inc(k.merged, 1)


def narrow_end(k, at, dst, bias=None):
    nc = k.nc
    with ExitStack() as own:
        ps = k.ps(own, "end_ps", [P, 2, 512])
        with k.stage() as block:
            @block.vector
            def _(v):
                step = Steps(v, k.vec_step)
                step(nc.vector.reciprocal(at.l[:], at.l[:]))
                for t in range(2 * B):
                    o = at.o[:, t, :].rearrange("p (h x) -> p h x", h=16)
                    nc.vector.tensor_tensor(o, o, at.l[:, t, :].unsqueeze(2).broadcast_to([P, 16, 16]), ALU.mult).then_inc(k.vec_done, 1)

            @block.tensor
            def _(pe):
                for t in range(2 * B):
                    pe.wait_ge(k.vec_done, t + 1)
                    for c in range(2):
                        mm = nc.tensor.transpose(ps[:, c, t * P:(t + 1) * P], at.o[:, t, c * P:(c + 1) * P], k.ident[:])
                mm.then_inc(k.products, 1)

            @block.scalar
            def _(act):
                act.wait_ge(k.products, 1)
                for c in range(2):
                    nc.scalar.activation(dst[:, c, :], ps[:, c, :], ACT.Identity, bias=0.0 if bias is None else bias[:, c:c + 1])


def rotated_projections(k, at, kt, h, w, bias):
    nc = k.nc
    with ExitStack() as own:
        ps = k.ps(own, "rot_ps", [P, 8, T])
        t = k.sb(own, "rot", [P, 2, 2, T])
        qt = k.sb(own, "rot_q", [P, 2, T])
        order = [(side, m) for side in range(2) for m in range(2)]
        with k.stage() as block:
            @block.tensor
            def _(pe):
                for n, (side, m) in enumerate(order):
                    for turned in range(2):
                        col = 512 * side + 256 * turned + m * P
                        for c in range(2):
                            mm = nc.tensor.matmul(ps[:, 2 * n + turned, :], w[:, c, col:col + P], h[:, c, :], start=(c == 0), stop=(c == 1))
                    mm.then_inc(k.products, 1)

            @block.vector
            def _(v):
                step = Steps(v, k.vec_step)
                for n, (side, m) in enumerate(order):
                    v.wait_ge(k.products, n + 1)
                    for turned, table in ((0, k.cos), (1, k.sin)):
                        col = 4 * side + 2 * turned + m
                        step(nc.vector.scalar_tensor_tensor(
                            out=t[:, n % 2, turned, :].rearrange("p (b s) -> p b s", b=B),
                            in0=ps[:, 2 * n + turned, :].rearrange("p (b s) -> p b s", b=B), scalar=bias[:, col:col + 1],
                            in1=table[:].unsqueeze(1).broadcast_to([P, B, S]), op0=ALU.add, op1=ALU.mult))
                    to = (qt, kt)[side][:, m, :]
                    step(nc.vector.tensor_tensor(to, t[:, n % 2, 0, :], t[:, n % 2, 1, :], ALU.add))
                    if side == 0:
                        for b in range(B):
                            step(at.spread(k, v, qt[:, m, b * S:(b + 1) * S], m, b))


def window_by_query(k, mask, seg, first_key, work):
    nc = k.nc

    def compute(v):
        step = Steps(v, k.vec_step)
        step(nc.vector.tensor_scalar(work[:, 0, :], k.iota[:], first_key, None, ALU.add))
        for t in range(2 * B):
            step(nc.vector.tensor_scalar(work[:, 1, :], work[:, 0, :], seg[:, t:t + 1], None, ALU.subtract))
            step(nc.vector.tensor_scalar(work[:, 2, :], work[:, 1, :], 0.0, NEG, ALU.is_gt, ALU.mult))
            step(nc.vector.tensor_scalar(work[:, 1, :], work[:, 1, :], -128.0, NEG, ALU.is_le, ALU.mult))
            step(nc.vector.tensor_tensor(mask[:, t, :], work[:, 2, :], work[:, 1, :], ALU.add))
        nc.vector.tensor_scalar(first_key, first_key, float(KB), None, ALU.add)
    return compute


def window_by_key(k, mask, seg, key, work, kt, keys):
    nc = k.nc

    def compute(v):
        step = Steps(v, k.vec_step)
        nc.vector.tensor_copy(kt, keys)
        for t in range(2 * B):
            b, kc = t // 2, t % 2
            step(nc.vector.tensor_scalar(work[:, 1, :], seg[:, b * S:(b + 1) * S], key[:, kc:kc + 1], None, ALU.subtract))
            step(nc.vector.tensor_scalar(work[:, 2, :], work[:, 1, :], 0.0, NEG, ALU.is_lt, ALU.mult))
            step(nc.vector.tensor_scalar(work[:, 1, :], work[:, 1, :], 128.0, NEG, ALU.is_ge, ALU.mult))
            step(nc.vector.tensor_tensor(mask[:, t, :], work[:, 2, :], work[:, 1, :], ALU.add))
        nc.vector.tensor_scalar(key, key, float(KB), None, ALU.add)
    return compute


class Streamed:

    def __init__(self, n, dim, keys, scale, split, masked=True):
        self.n, self.dim, self.keys, self.scale, self.split = n, dim, keys, scale, split
        self.dt = BF16 if split else F32
        self.rows = 6 * dim if split else dim
        self.rows_a = self.rows + 1
        self.max_rows = 2 if split else 1
        self.blocks = [(qt, j, min(512, keys - j)) for qt in range(2) for j in range(0, keys, 512)]
        chunks = keys // P
        self.groups = [(c, min(4, chunks - c)) for c in range(0, chunks, 4)]
        self.chunks = chunks
        self.strips = dim < 32
        self.columns = 32 if self.strips else dim + 1
        self.out_rows = P if self.strips else dim + 1
        self.max_at = self.rows_a if split else 96
        self.depth_a = self.max_at
        self.depth_b = self.max_at + self.max_rows


RING = 4


def heads_turns(k, sa, bufs, i, first, last, b):
    nc, d = k.nc, k.d
    kst, qst, vh, val, prob, o, acc, fold, small = bufs
    part, top, parts, parts_t, inv = small
    turns = [] if first else list(range(RING))
    ahead = [0] if first else [t + 1 for t in turns if not (last and t == RING - 1)]
    loads = [0, 1] if first else [t + 2 for t in turns if not (last and t >= RING - 2)]
    load_done = 16 * n_loads(sa)
    nb, ng = len(sa.blocks), len(sa.groups)
    dim1 = sa.dim + 1
    base = 0 if first else i * RING
    with ExitStack() as own:
        ps_a = k.ps(own, "ps_a", [P, 2, 512])
        ps_b = k.ps(own, "ps_b", [P, 2, 4, S])
        ps_o = k.ps(own, "ps_o", [P, 512])
        ps_f = k.ps(own, "ps_f", [P, 512])
        with k.stage() as block:
            @block.sync
            def _(sp):
                def fetch(h):
                    if not first and h >= RING:
                        sp.wait_ge(k.products, (h - RING + 1) * ng)
                    load_head(k, sp, sa, kst, qst, h % RING, base + h, b)

                def max_rows(n, h):
                    sp.wait_ge(k.vec_done, n + 1)
                    for qt in range(2):
                        for j in range(sa.max_rows):
                            sp.dma_start(qst[sa.max_at + j:sa.max_at + j + 1, h % RING, qt * P:(qt + 1) * P],
                                         parts_t[2 * qt + j:2 * qt + j + 97:32, :]).then_inc(k.stored, 16)

                def fetch_values(h):
                    if h >= 2:
                        sp.wait_ge(k.weighted, (h - 1) * ng)
                    sp.dma_start(vh[:, h % 2, :, 0:sa.dim],
                                 d["v_full"][b].rearrange("(c p) f -> p c f", p=P)[:, :, bass.ds((base + h) * sa.dim, sa.dim)])\
                        .then_inc(k.values_in[h % 2], 16)

                if first:
                    for h in loads:
                        fetch(h)
                    if val is None:
                        fetch_values(0)
                    max_rows(0, 0)
                for t in turns:
                    if t + 2 in loads:
                        fetch(t + 2)
                    if t + 1 in ahead:
                        if val is None:
                            fetch_values(t + 1)
                        max_rows(t, t + 1)
                if ahead and val is None:
                    for h in ahead[-2:]:
                        sp.wait_ge(k.values_in[h % 2], 16 * len([a for a in ahead if a % 2 == h % 2]))
                if ahead:
                    sp.wait_ge(k.stored, 32 * sa.max_rows * len(ahead))
                for h in loads:
                    sp.wait_ge(k.ring_in[h % RING], load_done)

            @block.gpsimd
            def _(pool):
                for t in turns if val is not None else []:
                    if t >= 2:
                        pool.wait_ge(k.weighted, (t - 1) * ng)
                    nc.gpsimd.tensor_copy(vh[:, t % 2, :, 0:dim1], val[:, :, bass.ds((base + t) * dim1, dim1)])\
                        .then_inc(k.pool_done, 1)

            @block.tensor
            def _(pe):
                def pass_a(h, n, j):
                    qt, at, size = sa.blocks[j]
                    if j == 0 and h in loads:
                        pe.wait_ge(k.ring_in[h % RING], load_done)
                    e = n * nb + j
                    if e >= 2:
                        pe.wait_ge(k.shifted, e - 1)
                    nc.tensor.matmul(ps_a[:, e % 2, 0:size], qst[0:sa.depth_a, h % RING, qt * P:(qt + 1) * P],
                                     kst[0:sa.depth_a, h % RING, at:at + size], start=True, stop=True).then_inc(k.scored, 1)

                def pass_b(t, g, c):
                    c0, nch = sa.groups[g]
                    e = t * ng + g
                    if c == 0 and g == 0 and t >= 1:
                        pe.wait_ge(k.stored, 32 * sa.max_rows * t)
                    if c == 0 and e >= 2:
                        pe.wait_ge(k.exps, e - 1)
                    mm = nc.tensor.matmul(ps_b[:, e % 2, c, :], kst[0:sa.depth_b, t, (c0 + c) * P:(c0 + c + 1) * P],
                                          qst[0:sa.depth_b, t, :], start=True, stop=True)
                    if c == nch - 1:
                        mm.then_inc(k.products, 1)

                def weigh(t, g):
                    c0, nch = sa.groups[g]
                    e = t * ng + g
                    pe.wait_ge(k.exps, e + 1)
                    if g == 0:
                        if val is not None:
                            pe.wait_ge(k.pool_done, t + 1)
                        elif t >= 1:
                            pe.wait_ge(k.values_in[t % 2], 16 * ((t + 1) // 2))
                        if t >= 1:
                            pe.wait_ge(k.turned, t)
                    for c in range(nch):
                        at = 32 * c if sa.strips else 0
                        mm = nc.tensor.matmul(ps_o[at:at + sa.columns, 0:S], vh[:, t % 2, c0 + c, :], prob[:, e % 2, c, :],
                                              start=(g == 0 and (sa.strips or c == 0)),
                                              stop=(g == ng - 1 and (sa.strips or c == nch - 1)))
                    mm.then_inc(k.weighted, 1)

                def fold_sums(t):
                    pe.wait_ge(k.turned, t + 1)
                    if t >= 1:
                        pe.wait_ge(k.merged, t)
                    for qt in range(2):
                        mm = nc.tensor.matmul(ps_f[:, qt * 128:qt * 128 + dim1], acc[0:sa.out_rows, qt * P:(qt + 1) * P],
                                              fold[0:sa.out_rows, 0:dim1], start=True, stop=True)
                    mm.then_inc(k.unturned, 1)

                if first:
                    for j in range(nb):
                        pass_a(0, 0, j)
                for t in turns:
                    todo = list(range(nb)) if t + 1 in ahead else []

                    def next_a():
                        if todo:
                            pass_a(t + 1, t, todo.pop(0))

                    for g in range(ng + 1):
                        next_a()
                        if g < ng:
                            for c in range(sa.groups[g][1]):
                                pass_b(t, g, c)
                                if c % 2:
                                    next_a()
                        if g >= 1:
                            weigh(t, g - 1)
                        if g == 1 and t >= 1:
                            fold_sums(t - 1)
                if turns:
                    fold_sums(RING - 1)

            @block.scalar
            def _(act):
                def copy_sums(t):
                    act.wait_ge(k.weighted, (t + 1) * ng)
                    if t >= 1:
                        act.wait_ge(k.unturned, t)
                    nc.scalar.activation(acc[0:sa.out_rows, :], ps_o[0:sa.out_rows, 0:S], ACT.Identity).then_inc(k.turned, 1)

                for t in turns:
                    for g, (_, nch) in enumerate(sa.groups):
                        e = t * ng + g
                        act.wait_ge(k.products, e + 1)
                        if e >= 2:
                            act.wait_ge(k.weighted, e - 1)
                        nc.scalar.activation(prob[:, e % 2, 0:nch], ps_b[:, e % 2, 0:nch], ACT.Exp, scale=sa.scale)\
                            .then_inc(k.exps, 1)
                        if g == 0 and t >= 1:
                            copy_sums(t - 1)
                if turns:
                    copy_sums(RING - 1)

            @block.vector
            def _(v):
                step = Steps(v, k.vec_step)

                def maximum(n, j):
                    size = sa.blocks[j][2]
                    e = n * nb + j
                    v.wait_ge(k.scored, e + 1)
                    nc.vector.tensor_reduce(part[:, j:j + 1], ps_a[:, e % 2, 0:size], AX, ALU.max).then_inc(k.shifted, 1)

                def split_maxima(n):
                    v.wait_ge(k.shifted, (n + 1) * nb)
                    step(nc.vector.tensor_reduce(top[:], part[:].rearrange("p (a j) -> p a j", a=2), AX, ALU.max))
                    if n >= 1:
                        v.wait_ge(k.stored, 32 * sa.max_rows * n)
                    for qt in range(2):
                        step(nc.vector.tensor_scalar(parts[:, 2 * qt:2 * qt + 1], top[:, qt:qt + 1], -1.0, None, ALU.mult))
                        if sa.split:
                            step(nc.vector.scalar_tensor_tensor(out=parts[:, 2 * qt + 1:2 * qt + 2], in0=top[:, qt:qt + 1], scalar=-1.0,
                                                                in1=parts[:, 2 * qt:2 * qt + 1], op0=ALU.mult, op1=ALU.subtract))
                    nc.vector.transpose(parts_t[:], parts[:]).then_inc(k.vec_done, 1)

                def outputs(t):
                    v.wait_ge(k.unturned, t + 1)
                    for qt in range(2):
                        step(nc.vector.reciprocal(inv[:, qt:qt + 1], ps_f[:, qt * 128 + sa.dim:qt * 128 + dim1]))
                        ins = nc.vector.tensor_scalar(o[:, qt, bass.ds((base + t) * sa.dim, sa.dim)], ps_f[:, qt * 128:qt * 128 + sa.dim],
                                                      inv[:, qt:qt + 1], None, ALU.mult)
                        if qt == 0:
                            step(ins)
                    ins.then_inc(k.merged, 1)

                if first:
                    for j in range(nb):
                        maximum(0, j)
                    split_maxima(0)
                for t in turns:
                    for j in range(nb):
                        if t + 1 in ahead:
                            maximum(t, j)
                        if j == 7 and t >= 1:
                            outputs(t - 1)
                    if t + 1 in ahead:
                        split_maxima(t)
                if turns:
                    outputs(RING - 1)


def n_loads(sa):
    return 6 if sa.split else 2


def load_head(k, sp, sa, kst, qst, slot, h, b):
    d = k.d
    if sa.split:
        hr = bass.ds(h * sa.dim, sa.dim)
        at = 0
        for p, n in enumerate((3, 2, 1)):
            end = at + n * sa.dim
            sp.dma_start(kst[at:end, slot, :], d["k_parts"][p, hr, :].unsqueeze(0).broadcast_to([n, sa.dim, sa.keys]))\
                .then_inc(k.ring_in[slot], 16)
            sp.dma_start(qst[at:end, slot, :], d["q_parts"][0:n, hr, bass.ds(b * S, S)]).then_inc(k.ring_in[slot], 16)
            at = end
    else:
        hr = bass.ds(h * sa.dim, sa.dim)
        sp.dma_start(kst[0:sa.dim, slot, :], d["k_full"][b][hr, :]).then_inc(k.ring_in[slot], 16)
        sp.dma_start(qst[0:sa.dim, slot, :], d["q_full"][hr, bass.ds(b * S, S)]).then_inc(k.ring_in[slot], 16)


def mask_row(k, sa, kst, mask_name, mask_dt, b):
    nc, d = k.nc, k.d
    base, pieces = sa.rows, 16
    with ExitStack() as own:
        raw = k.sb(own, "raw", [pieces, SK // pieces], mask_dt)
        row = k.sb(own, "row", [pieces, SK // pieces], sa.dt)
        with k.stage() as block:
            @block.sync
            def _(sp):
                sp.dma_start(raw[:], d[mask_name][b].rearrange("(a x) -> a x", a=pieces)).then_inc(k.loaded, 16)
                sp.wait_ge(k.vec_done, 1)
                for s in range(RING):
                    sp.dma_start(kst[base:base + 1, s, 0:SK].rearrange("o (a x) -> o a x", a=pieces), row[:]).then_inc(k.stored, 16)
                sp.wait_ge(k.stored, 16 * RING)

            @block.vector
            def _(v):
                v.wait_ge(k.loaded, 16)
                nc.vector.tensor_scalar(row[:], raw[:], 0.0, NEG, ALU.is_equal, ALU.mult).then_inc(k.vec_done, 1)


def keys_split(k, src, w, dst):
    nc = k.nc
    with ExitStack() as own:
        ps = k.ps(own, "split_ps", [P, 2, 512])
        part = k.sb(own, "part3", [P, 3, 2, 512], BF16)
        rest = k.sb(own, "rest", [P, 2, 512])
        with k.stage() as block:
            @block.tensor
            def _(pe):
                for m in range(2):
                    for c in range(2):
                        mm = nc.tensor.matmul(ps[:, m, :], w[:, c, m * P:(m + 1) * P], src[:, c, :], start=(c == 0), stop=(c == 1))
                mm.then_inc(k.products, 1)

            @block.scalar
            def _(act):
                act.wait_ge(k.products, 1)
                nc.scalar.activation(part[:, 0], ps[:], ACT.Identity).then_inc(k.act_done, 1)
                act.wait_ge(k.vec_done, 1)
                nc.scalar.activation(part[:, 1], rest[:], ACT.Identity).then_inc(k.act_done, 1)

            @block.vector
            def _(v):
                v.wait_ge(k.act_done, 1)
                nc.vector.tensor_tensor(rest[:], ps[:], part[:, 0], ALU.subtract).then_inc(k.vec_done, 1)
                v.wait_ge(k.act_done, 2)
                nc.vector.tensor_tensor(part[:, 2], rest[:], part[:, 1], ALU.subtract).then_inc(k.vec_done, 1)

            @block.sync
            def _(sp):
                sp.wait_ge(k.vec_done, 2)
                for p in range(3):
                    sp.dma_start(rows(dst[p]), part[:, p]).then_inc(k.stored, 16)
                sp.wait_ge(k.stored, 48)


def keys_values(k, sa, ctx, wk, wv, val, b, j):
    nc, d = k.nc, k.d
    nf = sa.n * sa.dim
    with ExitStack() as own:
        ps_k = k.ps(own, "ps_k", [P, 2, 2, 512])
        ps_v = k.ps(own, "ps_v", [P, 4, 512])
        part = k.sb(own, "part3", [P, 2, 3, 2, 512], BF16)
        rest = k.sb(own, "rest", [P, 2, 2, 512])
        with k.stage() as block:
            @block.sync
            def _(sp):
                for u in range(4):
                    sp.dma_start(ctx[:, u], rows(d["ctx_t"][b])[:, :, bass.ds(j * 2048 + u * 512, 512)]).then_inc(k.ring_in[u], 16)
                for u in range(4):
                    sp.wait_ge(k.vec_done, 2 * u + 2)
                    for p in range(3):
                        sp.dma_start(rows(d["k_parts"][p])[:, :, bass.ds(j * 2048 + u * 512, 512)], part[:, u % 2, p])\
                            .then_inc(k.values_in[u % 2], 16)
                for sem in k.values_in:
                    sp.wait_ge(sem, 96)

            @block.tensor
            def _(pe):
                for u in range(4):
                    pe.wait_ge(k.ring_in[u], 16)
                    if u >= 2:
                        pe.wait_ge(k.vec_done, 2 * u - 3)
                    for m in range(2):
                        for c in range(2):
                            mm = nc.tensor.matmul(ps_k[:, u % 2, m, :], wk[:, c, m * P:(m + 1) * P], ctx[:, u, c, :],
                                                  start=(c == 0), stop=(c == 1))
                    mm.then_inc(k.products, 1)
                    if u:
                        pe.wait_ge(k.evacuated, u)
                    for t in range(4):
                        for c in range(2):
                            mm = nc.tensor.matmul(ps_v[:, t, 0:nf], ctx[:, u, c, t * P:(t + 1) * P], wv[:, c, :],
                                                  start=(c == 0), stop=(c == 1))
                    mm.then_inc(k.products, 1)

            @block.scalar
            def _(act):
                for u in range(4):
                    act.wait_ge(k.products, 2 * u + 1)
                    if u >= 2:
                        act.wait_ge(k.values_in[u % 2], 48)
                        act.wait_ge(k.vec_done, 2 * u - 2)
                    nc.scalar.activation(part[:, u % 2, 0], ps_k[:, u % 2], ACT.Identity).then_inc(k.act_done, 1)
                    act.wait_ge(k.products, 2 * u + 2)
                    chunks = val[:].rearrange("p c (h x) -> p c h x", h=sa.n)[:, bass.ds(j * 16 + u * 4, 4), :, 0:sa.dim]
                    nc.scalar.activation(chunks, ps_v[:, :, 0:nf].rearrange("p c (h x) -> p c h x", h=sa.n), ACT.Identity)\
                        .then_inc(k.evacuated, 1)
                    act.wait_ge(k.vec_done, 2 * u + 1)
                    nc.scalar.activation(part[:, u % 2, 1], rest[:, u % 2], ACT.Identity).then_inc(k.act_done, 1)

            @block.vector
            def _(v):
                for u in range(4):
                    v.wait_ge(k.act_done, 2 * u + 1)
                    nc.vector.tensor_tensor(rest[:, u % 2], ps_k[:, u % 2], part[:, u % 2, 0], ALU.subtract).then_inc(k.vec_done, 1)
                    v.wait_ge(k.act_done, 2 * u + 2)
                    nc.vector.tensor_tensor(part[:, u % 2, 2], rest[:, u % 2], part[:, u % 2, 1], ALU.subtract).then_inc(k.vec_done, 1)


def streamed_buffers(k, own, sa, val, o):
    kst = k.sb(own, "kst", [P, RING, sa.keys], sa.dt)
    qst = k.sb(own, "qst", [P, RING, S], sa.dt)
    vh = k.sb(own, "vh", [P, 2, sa.chunks, sa.columns])
    prob = k.sb(own, "prob", [P, 2, 4, S])
    acc = k.sb(own, "acc", [P, S])
    small = [k.sb(own, "part", [P, len(sa.blocks)]), k.sb(own, "top", [P, 2]), k.sb(own, "parts", [P, 32], sa.dt),
             k.sb(own, "parts_t", [P, 32], sa.dt), k.sb(own, "inv", [P, 2])]
    nc, base = k.nc, sa.rows
    with k.stage() as block:
        @block.gpsimd
        def _(pool):
            nc.gpsimd.memset(kst[base:P], 1.0).then_inc(k.pool_done, 1)
            if sa.keys > SK:
                pool.wait_ge(k.pool_done, 1)
                nc.gpsimd.memset(kst[base:base + 1, :, SK:sa.keys], 0.0)

        @block.vector
        def _(v):
            nc.vector.memset(qst[base:base + 32], 1.0 if sa.split else 0.0).then_inc(k.vec_done, 1)
            v.wait_ge(k.vec_done, 1)
            if not sa.split:
                nc.vector.memset(qst[base:base + 1], 1.0)
            if val is not None:
                nc.vector.memset(val[:], 1.0)
            k.nc.vector.memset(small[2][:], 0.0)
            k.nc.vector.memset(vh[:], 1.0 if val is None else 0.0)
    fold = k.fold if sa.strips else k.ident
    return kst, qst, vh, val, prob, o, acc, fold, small


def outputs_to_features(k, o, dst, chunks, b):
    nc = k.nc
    with ExitStack() as own:
        ps = k.ps(own, "turn_ps", [P, chunks, 512])
        with k.stage() as block:
            @block.tensor
            def _(pe):
                for c in range(chunks):
                    for qt in range(2):
                        mm = nc.tensor.transpose(ps[:, c, qt * P:(qt + 1) * P], o[:, qt, c * P:(c + 1) * P], k.ident[:])
                mm.then_inc(k.products, 1)

            @block.scalar
            def _(act):
                act.wait_ge(k.products, 1)
                nc.scalar.activation(dst[:, :, bass.ds(b * S, S)], ps[:, :, 0:S], ACT.Identity)




def l0_cross(k, x):
    nc, d = k.nc, k.d
    sa = Streamed(16, 16, SK, 0.25, split=True)
    dim1 = sa.dim + 1
    with ExitStack() as own:
        h = k.sb(own, "h", [P, 2, T])
        ot = k.sb(own, "ot", [P, 2, T])
        wq, wk, wv, wo = (k.sb(own, n, [P, 2, D]) for n in ("wq", "wk", "wv", "wo"))
        val = k.sb(own, "val", [P, sa.chunks, sa.n * dim1])
        o = k.sb(own, "att_o", [P, 2, sa.n * sa.dim])
        norm(k, h[:], x[:], 1e-5, ahead=[(wq[:], rows(d["L0_xattn_Wq"])), (wk[:], rows(d["L0_xattn_Wk"])), (wv[:], rows(d["L0_xattn_Wv"])),
                 (wo[:], rows(d["L0_xattn_Wo"]))])
        bufs = streamed_buffers(k, own, sa, val, o)
        keys_split(k, h, wq, d["q_parts"])
        with nc.Fori(0, B) as b:
            with ExitStack() as inner:
                ctx = k.sb(inner, "ctx", [P, 4, 2, 512])
                with nc.Fori(0, SK // 2048) as j:
                    keys_values(k, sa, ctx, wk, wv, val, b, j)
            mask_row(k, sa, bufs[0], "mask_BxS2_ik1", mybir.dt.int32, b)
            heads_turns(k, sa, bufs, 0, True, False, b)
            with nc.Fori(0, sa.n // RING - 1) as i:
                heads_turns(k, sa, bufs, i, False, False, b)
            heads_turns(k, sa, bufs, sa.n // RING - 1, False, True, b)
            outputs_to_features(k, o, ot, sa.n * sa.dim // P, b)
        project(k, x, ot, 2, wo, 2, T, vec=(0.0, ALU.add, x, ALU.add))


def l0_scan(k, x):
    nc, d = k.nc, k.d
    NS = 16
    with ExitStack() as own:
        h = k.sb(own, "h", [P, 2, T])
        gate = k.sb(own, "gate", [P, 4, T])
        hs = k.sb(own, "hs", [P, 4, T])
        delta = k.sb(own, "delta", [P, 4, T])
        y = k.sb(own, "y", [P, 4, T])
        u = k.sb(own, "u", [P, 4, T])
        w_in = k.sb(own, "w_in", [P, 2, 1024])
        w_out = k.sb(own, "w_out", [P, 4, D])
        xp = k.sb(own, "xp", [P, 4, P])
        w_dt = k.sb(own, "w_dt", [64, 4 * P])
        dbl = k.sb(own, "dbl", [P, 1, T])
        a_neg = k.sb(own, "a_neg", [P, 64])
        conv = k.vec("conv")
        norm(k, h[:], x[:], 1e-5)
        project(k, hs, h, 2, w_in, 4, T, loads=[(w_in[:], rows(d["L0_attn_w_in_t"])), (w_out[:], rows(d["L0_attn_w_out_t"])),
                                                (xp[:], rows(d["L0_attn_w_xproj_t"])), (w_dt[:], d["L0_attn_w_dt_t"])])
        project(k, gate, h, 2, w_in[:, :, 512:1024], 4, T, func=ACT.Silu)
        with ExitStack() as inner:
            padded = k.sb(inner, "padded", [P, 4, B, S + 3])
            acc = k.sb(inner, "acc", [P, 4, B, S])
            with k.stage() as block:
                @block.vector
                def _(v):
                    step = Steps(v, k.vec_step)
                    step(nc.vector.memset(padded[:], 0.0))
                    for c in range(4):
                        step(nc.vector.tensor_copy(padded[:, c, :, 3:S + 3], hs[:, c, :].rearrange("p (b s) -> p b s", b=B)))
                        step(nc.vector.tensor_scalar(acc[:, c], padded[:, c, :, 0:S], conv[:, 4 * c:4 * c + 1], None, ALU.mult))
                        for i in range(1, 4):
                            ins = nc.vector.scalar_tensor_tensor(out=acc[:, c], in0=padded[:, c, :, i:S + i],
                                                                 scalar=conv[:, 4 * c + i:4 * c + i + 1], in1=acc[:, c],
                                                                 op0=ALU.mult, op1=ALU.add)
                            if i < 3:
                                step(ins)
                        ins.then_inc(k.vec_done, 1)

                @block.scalar
                def _(act):
                    for c in range(4):
                        act.wait_ge(k.vec_done, c + 1)
                        nc.scalar.activation(hs[:, c, :], acc[:, c].rearrange("p b s -> p (b s)"), ACT.Silu)
        project(k, dbl, hs, 4, xp, 1, T)
        with ExitStack() as inner:
            ps = k.ps(inner, "dt_ps", [P, 4, 512])
            z = k.sb(inner, "z", [P, 4, T])
            e = k.sb(inner, "e", [P, 4, T])
            with k.stage() as block:
                @block.sync
                def _(sp):
                    sp.dma_start(d["bc_rows"], dbl[64:96, 0, :]).then_inc(k.stored, 16)
                    sp.wait_ge(k.stored, 16)

                @block.tensor
                def _(pe):
                    for c in range(4):
                        mm = nc.tensor.matmul(ps[:, c, :], w_dt[:, c * P:(c + 1) * P], dbl[0:64, 0, :], start=True, stop=True)
                    mm.then_inc(k.products, 1)

                @block.scalar
                def _(act):
                    nc.scalar.activation(a_neg[:], k.vec("A_log"), ACT.Exp).then_inc(k.act_done, 1)
                    act.wait_ge(k.products, 1)
                    for c in range(4):
                        nc.scalar.activation(z[:, c, :], ps[:, c, :], ACT.Identity, bias=k.vec("L0_attn_b_dt")[:, c:c + 1])\
                            .then_inc(k.act_done, 1)
                    act.wait_ge(k.act_done, 5)
                    nc.scalar.activation(e[:], z[:], ACT.Abs).then_inc(k.act_done, 1)
                    act.wait_ge(k.act_done, 6)
                    nc.scalar.activation(e[:], e[:], ACT.Exp, scale=-1.0).then_inc(k.act_done, 1)
                    act.wait_ge(k.act_done, 7)
                    nc.scalar.activation(e[:], e[:], ACT.Ln, bias=1.0).then_inc(k.act_done, 1)

                @block.vector
                def _(v):
                    step = Steps(v, k.vec_step)
                    v.wait_ge(k.act_done, 8)
                    nc.vector.tensor_scalar(a_neg[:], a_neg[:], -1.0, None, ALU.mult)
                    step(nc.vector.scalar_tensor_tensor(out=delta[:], in0=z[:], scalar=0.0, in1=e[:], op0=ALU.max, op1=ALU.add))
                    nc.vector.tensor_tensor(u[:], delta[:], hs[:], ALU.mult)
                    for c in range(4):
                        nc.vector.tensor_scalar(y[:, c, :], hs[:, c, :], k.vec("L0_attn_D")[:, c:c + 1], None, ALU.mult)
        per = 4
        with ExitStack() as inner:
            bb, cb = k.sb(inner, "bb", [P, per, T]), k.sb(inner, "cb", [P, per, T])
            decay, drive, state = (k.sb(inner, n, [P, 2, 4, T]) for n in ("decay", "drive", "state"))
            a_n = k.sb(inner, "a_n", [P, per * 4])
            ps = k.ps(inner, "y_ps", [P, 4, T])
            with nc.Fori(0, NS // per) as turn:
                with k.stage() as block:
                    @block.sync
                    def _(sp):
                        for i in range(per):
                            for to, first in ((bb, 0), (cb, NS)):
                                sp.dma_start(to[:, i, :], d["bc_rows"][turn * per + (first + i)].unsqueeze(0).broadcast_to([P, T]))\
                                    .then_inc(k.ring_in[i], 16)

                    @block.scalar
                    def _(act):
                        nc.scalar.activation(a_n[:], a_neg[:, bass.ds(turn * (4 * per), 4 * per)], ACT.Identity).then_inc(k.unturned, 1)
                        act.wait_ge(k.unturned, 1)
                        for i in range(per):
                            for c in range(4):
                                if i >= 2:
                                    act.wait_ge(k.shifted, 2 * (4 * (i - 2) + c) + 2)
                                nc.scalar.activation(decay[:, i % 2, c, :], delta[:, c, :], ACT.Exp, scale=a_n[:, 4 * i + c:4 * i + c + 1])\
                                    .then_inc(k.act_done, 1)

                    @block.gpsimd
                    def _(pool):
                        for i in range(per):
                            pool.wait_ge(k.ring_in[i], 32)
                            for c in range(4):
                                if i >= 2:
                                    pool.wait_ge(k.shifted, 2 * (4 * (i - 2) + c) + 2)
                                nc.gpsimd.tensor_tensor(drive[:, i % 2, c, :], u[:, c, :], bb[:, i, :], ALU.mult).then_inc(k.pool_done, 1)

                    @block.tensor
                    def _(pe):
                        for i in range(per):
                            for c in range(4):
                                pe.wait_ge(k.merged, 4 * i + c + 1)
                                nc.tensor.matmul(ps[:, c, :], k.ident[:], state[:, i % 2, c, :], start=(i == 0), stop=(i == per - 1))\
                                    .then_inc(k.turned, 1)

                    @block.vector
                    def _(v):
                        for i in range(per):
                            v.wait_ge(k.ring_in[i], 32)
                            for c in range(4):
                                at = 4 * i + c
                                v.wait_ge(k.act_done, at + 1)
                                v.wait_ge(k.pool_done, at + 1)
                                if i >= 2:
                                    v.wait_ge(k.turned, at - 7)
                                for b in range(B):
                                    s = slice(b * S, (b + 1) * S)
                                    nc.vector.tensor_tensor_scan(state[:, i % 2, c, s], decay[:, i % 2, c, s], drive[:, i % 2, c, s],
                                                                 0.0, ALU.mult, ALU.add).then_inc(k.shifted, 1)
                                v.wait_ge(k.shifted, 2 * at + 2)
                                nc.vector.tensor_tensor(state[:, i % 2, c, :], state[:, i % 2, c, :], cb[:, i, :], ALU.mult)\
                                    .then_inc(k.merged, 1)
                        for c in range(4):
                            v.wait_ge(k.turned, 4 * (per - 1) + c + 1)
                            nc.vector.tensor_tensor(y[:, c, :], y[:, c, :], ps[:, c, :], ALU.add)
        with k.stage() as block:
            @block.vector
            def _(v):
                nc.vector.tensor_tensor(y[:], y[:], gate[:], ALU.mult)
        project(k, x, y, 4, w_out, 2, T, vec=(0.0, ALU.add, x, ALU.add))


def router(k, own, h, w_name, bias_name=None):
    d = k.d
    wg = k.sb(own, "wg", [P, 2, 8])
    logits = k.sb(own, "logits", [P, 4, 8])
    bias = k.sb(own, "gate_bias", [P, 8])
    loads = [(wg[:], rows(d[w_name]))]
    if bias_name is not None:
        loads.append((bias[:], d[bias_name].unsqueeze(0).broadcast_to([P, 8])))
    project_tokens(k, logits, h, 2, wg, 4, 8, loads=loads)
    return logits, bias


def softmax8(k, s):
    nc = k.nc
    with ExitStack() as own:
        r = k.sb(own, "row", [P, 4])
        with k.stage() as block:
            @block.vector
            def _(v):
                step = Steps(v, k.vec_step)
                step(nc.vector.tensor_reduce(r[:], s[:], AX, ALU.max))
                nc.vector.tensor_tensor(s[:], s[:], r[:].unsqueeze(2).broadcast_to([P, 4, 8]), ALU.subtract).then_inc(k.vec_done, 1)
                v.wait_ge(k.act_done, 1)
                step(nc.vector.reduce_sum(r[:], s[:], AX))
                step(nc.vector.reciprocal(r[:], r[:]))
                nc.vector.tensor_tensor(s[:], s[:], r[:].unsqueeze(2).broadcast_to([P, 4, 8]), ALU.mult)

            @block.scalar
            def _(act):
                act.wait_ge(k.vec_done, 1)
                nc.scalar.activation(s[:], s[:], ACT.Exp).then_inc(k.act_done, 1)


def gates_by_expert(k, w, wt):
    nc = k.nc
    with ExitStack() as own:
        ps = k.ps(own, "gate_ps", [P, 512])
        with k.stage() as block:
            @block.tensor
            def _(pe):
                for t in range(4):
                    mm = nc.tensor.transpose(ps[0:8, t * P:(t + 1) * P], w[:, t, :], k.ident[:])
                mm.then_inc(k.products, 1)

            @block.vector
            def _(v):
                v.wait_ge(k.products, 1)
                nc.vector.tensor_copy(wt[:], ps[0:8, :])


def store_gates(k, wt, shared=None):
    nc, d = k.nc, k.d
    with ExitStack() as own:
        row = k.sb(own, "shared_row", [1, T])
        with k.stage() as block:
            @block.vector
            def _(v):
                if shared is not None:
                    nc.vector.memset(row[:], shared).then_inc(k.vec_done, 1)

            @block.sync
            def _(sp):
                sp.dma_start(d["gate_rows"][0:8, :], wt[:]).then_inc(k.stored, 16)
                if shared is not None:
                    sp.wait_ge(k.vec_done, 1)
                    sp.dma_start(d["gate_rows"][8:9, :], row[:]).then_inc(k.stored, 16)
                sp.wait_ge(k.stored, 32 if shared is not None else 16)


def gelu_turn(k, x, h, bufs, names, e, n, ahead):
    nc, d = k.nc, k.d
    up, down, vecs = names
    wu, wd, bv, gate, a, y, ps = bufs
    late = [t for t in range(2, n + ahead)]
    with k.stage() as block:
        @block.sync
        def _(sp):
            def fetch(t, sem):
                i = t % 2
                sp.dma_start(bv[:, i], d[vecs][e + t]).then_inc(sem, 16)
                sp.dma_start(wu[:, i], rows(d[up][e + t])).then_inc(sem, 16)
                sp.dma_start(gate[:, i], d["gate_rows"][e + t].unsqueeze(0).broadcast_to([P, T])).then_inc(sem, 16)
                sp.dma_start(wd[:, i], rows(d[down][e + t])).then_inc(sem, 16)

            if n == 0:
                fetch(0, k.loaded)
                sp.wait_ge(k.loaded, 64)
            if n + ahead > 1 and n:
                fetch(1, k.loaded)
            for t in late:
                sp.wait_ge(k.merged, t - 1)
                fetch(t, k.loaded_next)
            if n:
                if n + ahead > 1:
                    sp.wait_ge(k.loaded, 64)
                if late:
                    sp.wait_ge(k.loaded_next, 64 * len(late))

        @block.tensor
        def _(pe):
            for t in range(n):
                if t == 1:
                    pe.wait_ge(k.loaded, 64)
                for m in range(8):
                    u = 8 * t + m
                    if u >= 4:
                        pe.wait_ge(k.act_done, u - 3)
                    for c in range(2):
                        mm = nc.tensor.matmul(ps[:, m % 4, :], wu[:, t, c, m * P:(m + 1) * P], h[:, c, :],
                                              start=(c == 0), stop=(c == 1))
                    mm.then_inc(k.products, 1)
                for f in range(8):
                    pe.wait_ge(k.act_done, 8 * t + f + 1)
                    for m in range(2):
                        mm = nc.tensor.matmul(ps[:, 4 + 2 * t + m, :], wd[:, t, f, m * P:(m + 1) * P], a[:, t, f, :],
                                              start=(f == 0), stop=(f == 7))
                mm.then_inc(k.weighted, 1)

        @block.scalar
        def _(act):
            for t in range(n):
                if t == 1:
                    act.wait_ge(k.loaded, 64)
                for m in range(8):
                    act.wait_ge(k.products, 8 * t + m + 1)
                    nc.scalar.activation(a[:, t, m, :], ps[:, m % 4, :], ACT.Gelu, bias=bv[:, t, m:m + 1]).then_inc(k.act_done, 1)

        @block.vector
        def _(v):
            step = Steps(v, k.vec_step)
            for t in range(n):
                if t == 1:
                    v.wait_ge(k.loaded, 64)
                v.wait_ge(k.weighted, t + 1)
                for m in range(2):
                    step(nc.vector.scalar_tensor_tensor(out=y[:, m, :], in0=ps[:, 4 + 2 * t + m, :], scalar=bv[:, t, 8 + m:9 + m],
                                                        in1=gate[:, t], op0=ALU.add, op1=ALU.mult))
                nc.vector.tensor_tensor(x[:], x[:], y[:], ALU.add).then_inc(k.merged, 1)
                v.wait_ge(k.merged, t + 1)


def experts_gelu(k, x, h, n, up, down, vecs):
    with ExitStack() as own:
        bufs = (k.sb(own, "wu", [P, 2, 2, 1024]), k.sb(own, "wd", [P, 2, 8, D]), k.sb(own, "bv", [P, 2, 10]),
                k.sb(own, "gate", [P, 2, T]), k.sb(own, "a", [P, 2, 8, T]), k.sb(own, "y", [P, 2, T]),
                k.ps(own, "moe_ps", [P, 8, 512]))
        names = (up, down, vecs)
        gelu_turn(k, x, h, bufs, names, 0, 0, 1)
        pairs = (n - 1) // 2
        with k.nc.Fori(0, pairs) as i:
            gelu_turn(k, x, h, bufs, names, i * 2, 2, 1)
        gelu_turn(k, x, h, bufs, names, 2 * pairs, n - 2 * pairs, 0)


def l0_experts(k, x):
    nc = k.nc
    with ExitStack() as own:
        h = k.sb(own, "h", [P, 2, T])
        norm(k, h[:], x[:], 1e-5)
        s, bias = router(k, own, h, "L0_ffn_gate_w_t", "L0_ffn_gate_bias")
        top = k.sb(own, "top", [P, 4, 8])
        den = k.sb(own, "den", [P, 4])
        w = k.sb(own, "w", [P, 4, 8])
        wt = k.sb(own, "wt", [8, T])
        with k.stage() as block:
            @block.vector
            def _(v):
                step = Steps(v, k.vec_step)
                nc.vector.tensor_tensor(s[:], s[:], bias[:].unsqueeze(1).broadcast_to([P, 4, 8]), ALU.add).then_inc(k.vec_done, 1)
                v.wait_ge(k.act_done, 1)
                for t in range(4):
                    step(nc.vector.max(top[:, t, :], s[:, t, :]))
                step(nc.vector.tensor_tensor(den[:], top[:, :, 0], top[:, :, 1], ALU.add))
                step(nc.vector.tensor_scalar(den[:], den[:], 1e-6, None, ALU.add))
                step(nc.vector.reciprocal(den[:], den[:]))
                step(nc.vector.tensor_tensor(w[:], s[:], top[:, :, 1:2].broadcast_to([P, 4, 8]), ALU.is_ge))
                step(nc.vector.tensor_tensor(w[:], w[:], s[:], ALU.mult))
                nc.vector.tensor_tensor(w[:], w[:], den[:].unsqueeze(2).broadcast_to([P, 4, 8]), ALU.mult)

            @block.scalar
            def _(act):
                act.wait_ge(k.vec_done, 1)
                nc.scalar.activation(s[:], s[:], ACT.Sigmoid).then_inc(k.act_done, 1)
        gates_by_expert(k, w, wt)
        store_gates(k, wt, 0.1)
        experts_gelu(k, x, h, 9, "L0_ffn_up", "L0_ffn_down", "L0_ffn_vecs")




def context_attention(k, q, dst, b, scale):
    nc, d = k.nc, k.d
    chunks, groups, blocks = SK // P, SK // 512, SK // 512
    piece = SK // 4
    with ExitStack() as own:
        feat = k.sb(own, "ctx_feat", [P, 2, SK])
        tok = k.sb(own, "ctx_tok", [P, chunks, D + 1])
        prob = k.sb(own, "prob", [P, 2, 4, S])
        part, top = k.sb(own, "part", [P, 2, blocks]), k.sb(own, "top", [P, 2])
        hi, split = k.sb(own, "hi", [P, 2], BF16), k.sb(own, "split", [P, 2, 2])
        top_t, ones = k.sb(own, "top_t", [2, S], BF16), k.sb(own, "ones", [2, P], BF16)
        o, inv = k.sb(own, "o", [P, 2, D]), k.sb(own, "inv", [P, 2])
        ps_a = k.ps(own, "ps_a", [P, 2, 512])
        ps_b = k.ps(own, "ps_b", [P, 2, 4, S])
        ps_o = k.ps(own, "ps_o", [P, 2, 512])
        with k.stage() as block:
            @block.sync
            def _(sp):
                for i in range(4):
                    sp.dma_start(feat[:, :, i * piece:(i + 1) * piece], rows(d["ctx_t"][b])[:, :, i * piece:(i + 1) * piece])\
                        .then_inc(k.ring_in[i], 16)
                for i, sem in enumerate(k.values_in):
                    at = i * SK // 2
                    sp.dma_start(tok[:, i * chunks // 2:(i + 1) * chunks // 2, 0:D],
                                 d["ctx_1024"][b][at:at + SK // 2].rearrange("(c p) f -> p c f", p=P)).then_inc(sem, 16)

            @block.gpsimd
            def _(pool):
                nc.gpsimd.memset(tok[:, :, D:D + 1], 1.0)
                nc.gpsimd.memset(ones[:], 1.0).then_inc(k.pool_done, 1)

            @block.tensor
            def _(pe):
                for n in range(2 * blocks):
                    j, qt = n // 2, n % 2
                    if qt == 0 and j * 512 % piece == 0:
                        pe.wait_ge(k.ring_in[j * 512 // piece], 16)
                    if n >= 2:
                        pe.wait_ge(k.shifted, n - 1)
                    for c in range(2):
                        mm = nc.tensor.matmul(ps_a[:, n % 2, :], q[:, c, qt * P:(qt + 1) * P], feat[:, c, j * 512:(j + 1) * 512],
                                              start=(c == 0), stop=(c == 1))
                    mm.then_inc(k.scored, 1)
                pe.wait_ge(k.vec_done, 1)
                for qt in range(2):
                    mm = nc.tensor.transpose(ps_a[0:2, 0, qt * P:(qt + 1) * P], split[:, qt, :], k.ident[:])
                mm.then_inc(k.turned, 1)

                def scores(g):
                    if g >= 2:
                        pe.wait_ge(k.exps, g - 1)
                    for i in range(4):
                        at = (4 * g + i) * P
                        for c in range(2):
                            nc.tensor.matmul(ps_b[:, g % 2, i, :], feat[:, c, at:at + P], q[:, c, :], start=(c == 0), stop=False)
                        mm = nc.tensor.matmul(ps_b[:, g % 2, i, :], ones[:], top_t[:], start=False, stop=True)
                    mm.then_inc(k.products, 1)

                def weigh(g):
                    pe.wait_ge(k.exps, g + 1)
                    if g in (0, groups // 2):
                        pe.wait_ge(k.values_in[g * 2 // groups], 16)
                    for i in range(4):
                        for qt in range(2):
                            mm = nc.tensor.matmul(ps_o[:, qt, 0:D + 1], prob[:, g % 2, i, qt * P:(qt + 1) * P], tok[:, 4 * g + i, :],
                                                  start=(g == 0 and i == 0), stop=(g == groups - 1 and i == 3))
                    mm.then_inc(k.weighted, 1)

                pe.wait_ge(k.unturned, 1)
                pe.wait_ge(k.pool_done, 1)
                for g in range(groups + 1):
                    if g < groups:
                        scores(g)
                    if g >= 1:
                        weigh(g - 1)
                pe.wait_ge(k.merged, 1)
                for c in range(2):
                    for qt in range(2):
                        mm = nc.tensor.transpose(ps_a[:, c, qt * P:(qt + 1) * P], o[:, qt, c * P:(c + 1) * P], k.ident[:])
                mm.then_inc(k.turned, 1)

            @block.scalar
            def _(act):
                act.wait_ge(k.turned, 1)
                nc.scalar.activation(top_t[:], ps_a[0:2, 0, 0:S], ACT.Identity).then_inc(k.unturned, 1)
                for g in range(groups):
                    act.wait_ge(k.products, g + 1)
                    if g >= 2:
                        act.wait_ge(k.weighted, g - 1)
                    nc.scalar.activation(prob[:, g % 2], ps_b[:, g % 2], ACT.Exp, scale=scale).then_inc(k.exps, 1)
                act.wait_ge(k.turned, 2)
                nc.scalar.activation(dst[:, :, bass.ds(b * S, S)], ps_a[:, :, 0:S], ACT.Identity)

            @block.vector
            def _(v):
                step = Steps(v, k.vec_step)
                for n in range(2 * blocks):
                    j, qt = n // 2, n % 2
                    v.wait_ge(k.scored, n + 1)
                    nc.vector.tensor_reduce(part[:, qt, j:j + 1], ps_a[:, n % 2, :], AX, ALU.max).then_inc(k.shifted, 1)
                v.wait_ge(k.shifted, 2 * blocks)
                step(nc.vector.tensor_reduce(top[:], part[:], AX, ALU.max))
                step(nc.vector.tensor_scalar(hi[:], top[:], -1.0, None, ALU.mult))
                step(nc.vector.tensor_copy(split[:, :, 0], hi[:]))
                nc.vector.scalar_tensor_tensor(out=split[:, :, 1], in0=top[:], scalar=-1.0, in1=hi[:],
                                               op0=ALU.mult, op1=ALU.subtract).then_inc(k.vec_done, 1)
                v.wait_ge(k.weighted, groups)
                step(nc.vector.reciprocal(inv[:], ps_o[:, :, D]))
                nc.vector.tensor_tensor(o[:], ps_o[:, :, 0:D], inv[:].unsqueeze(2).broadcast_to([P, 2, D]), ALU.mult).then_inc(k.merged, 1)


def l1_cross(k, x):
    nc, d = k.nc, k.d
    with ExitStack() as own:
        h, q, qk, oc, ot = (k.sb(own, n, [P, 2, T]) for n in ("h", "q", "qk", "oc", "ot"))
        qb = k.sb(own, "qb", [P, 2, S])
        wq, wk, wv, wo = (k.sb(own, n, [P, 2, D]) for n in ("wq", "wk", "wv", "wo"))
        norm(k, h[:], x[:], 1e-5)
        project(k, q, h, 2, wq, 2, T, bias=k.vec("L1_xattn_bq"), loads=[
            (wq[:], rows(d["L1_xattn_Wq_t"])), (wk[:], rows(d["L1_xattn_Wk"])),
            (wv[:], rows(d["L1_xattn_Wv_t"])), (wo[:], rows(d["L1_xattn_Wo_t"]))])
        project(k, qk, q, 2, wk, 2, T)
        with nc.Fori(0, B) as b:
            copy_batch(k, qb[:], qk, b)
            context_attention(k, qb, oc, b, 1.0 / 16)
        project(k, ot, oc, 2, wv, 2, T, bias=k.vec("L1_xattn_bv"))
        project(k, x, ot, 2, wo, 2, T, vec=(k.vec("L1_xattn_bo"), ALU.add, x, ALU.add))


def l1_self(k, x):
    nc, d = k.nc, k.d
    hd = Heads(16, 64, 0.125)
    with ExitStack() as own:
        h = k.sb(own, "h", [P, 2, T])
        hb = k.sb(own, "hb", [P, 2, S])
        qb, kt = k.sb(own, "qb", [P, 8, S]), k.sb(own, "kt", [P, 8, S])
        val = k.sb(own, "val", [P, 2, 1024])
        ot = k.sb(own, "ot", [P, 8, T])
        wq, wk, wv = (k.sb(own, n, [P, 2, 1024]) for n in ("wq", "wk", "wv"))
        wo = k.sb(own, "wo", [P, 8, D])
        st = attention_state(k, own, hd)
        norm(k, h[:], x[:], 1e-5, ahead=[(wq[:], rows(d["L1_attn_w_q_t"])), (wk[:], rows(d["L1_attn_w_k_t"])), (wv[:], rows(d["L1_attn_w_v_t"])),
                 (wo[:], rows(d["L1_attn_w_o"]))])
        with nc.Fori(0, B) as b:
            copy_batch(k, hb[:], h, b)
            project(k, qb, hb, 2, wq, 8, S)
            project(k, kt, hb, 2, wk, 8, S)
            project_tokens(k, val, hb, 2, wv, 2, 1024)
            attention_start(k, st)
            attend(k, hd, st, qb, kt, val)
            attention_end(k, hd, st, ot, b)
        project(k, h, ot, 8, wo, 2, T, vec=(0.0, ALU.add, h, ALU.add))
        with k.stage() as block:
            @block.vector
            def _(v):
                nc.vector.tensor_tensor(x[:], x[:], h[:], ALU.add)


def l1_ffn(k, x):
    d = k.d
    with ExitStack() as own:
        h = k.sb(own, "h", [P, 2, T])
        w1, w2 = k.sb(own, "w1", [P, 2, 1024]), k.sb(own, "w2", [P, 2, 1024])
        h1, h2, w3 = k.sb(own, "h1", [P, 8, 1024]), k.sb(own, "h2", [P, 8, 1024]), k.sb(own, "w3", [P, 8, D])
        a1, a2 = k.sb(own, "a1", [P, 8, T]), k.sb(own, "a2", [P, 8, T])
        h1_rows = rows(d["L1_ffn_h1_t"])
        norm(k, h[:], x[:], 1e-5, ahead=[(w1[:], rows(d["L1_ffn_w1_t"])), (w2[:], rows(d["L1_ffn_w2_t"]))])
        project(k, a1, h, 2, w1, 8, T, func=ACT.Silu, scale=k.vec("L1_ffn_w1_s"), ahead=[(h1[:, 0:4], h1_rows[:, 0:4])])
        project(k, a1, h, 2, w2, 8, T, vec=(k.vec("L1_ffn_w2_s"), ALU.mult, a1, ALU.mult), ahead=[(h1[:, 4:8], h1_rows[:, 4:8])])
        project(k, a2, a1, 8, h1, 8, T, func=ACT.Gelu, scale=k.vec("L1_ffn_h1_s"),
                ahead=[(h2[:], rows(d["L1_ffn_h2_t"])), (w3[:], rows(d["L1_ffn_w3_t"]))])
        project(k, a1, a2, 8, h2, 8, T, func=ACT.Gelu, scale=k.vec("L1_ffn_h2_s"))
        project(k, x, a1, 8, w3, 2, T, vec=(k.vec("L1_ffn_w3_s"), ALU.mult, x, ALU.add))




def blocks_with_segments(k, count, work, row):
    nc, d = k.nc, k.d
    top_i, low, top, bad = work
    with k.stage() as block:
        @block.sync
        def _(sp):
            sp.dma_start(row, d["seg_row"]).then_inc(k.loaded, 16)

        @block.vector
        def _(v):
            step = Steps(v, k.vec_step)
            v.wait_ge(k.loaded, 16)
            step(nc.vector.tensor_reduce(top_i, row, AX, ALU.max))
            step(nc.vector.tensor_reduce(top, row, AX, ALU.max))
            step(nc.vector.tensor_reduce(low, row, AX, ALU.min))
            step(nc.vector.tensor_scalar(top_i, top_i, KB.bit_length() - 1, None, ALU.arith_shift_right))
            step(nc.vector.tensor_scalar(low, low, 0.0, float(SK // KB), ALU.is_lt, ALU.mult))
            step(nc.vector.tensor_scalar(bad, top, float(SK - 1), float(SK // KB), ALU.is_gt, ALU.mult))
            step(nc.vector.tensor_tensor(bad, bad, low, ALU.add))
            step(nc.vector.tensor_copy(top, top_i))
            step(nc.vector.tensor_scalar(top, top, 1.0, 1.0, ALU.add, ALU.max))
            step(nc.vector.tensor_tensor(top, top, bad, ALU.add))
            step(nc.vector.tensor_scalar(top, top, float(SK // KB), None, ALU.min))
            nc.vector.tensor_copy(count, top)
    return nc.values_load(count, min_val=1, max_val=SK // KB)


def feed_forward(k, xx, h, a, wg, wu, wd, loads=()):
    nc = k.nc
    with ExitStack() as own:
        ps_g, ps_u, ps_d = (k.ps(own, n, [P, 2, T]) for n in ("gate_ps", "up_ps", "down_ps"))
        with k.stage() as block:
            @block.sync
            def _(sp):
                for to, fr in loads:
                    sp.dma_start(to, fr).then_inc(k.loaded, 16)
                if loads:
                    sp.wait_ge(k.loaded, 16 * len(loads))

            @block.tensor
            def _(pe):
                def down(f):
                    pe.wait_ge(k.vec_done, f + 1)
                    for m in range(2):
                        mm = nc.tensor.matmul(ps_d[:, m, :], wd[:, f, m * P:(m + 1) * P], a[:, f, :], start=(f == 0), stop=(f == 7))
                    return mm

                for f in range(8):
                    if f >= 2:
                        pe.wait_ge(k.act_done, f - 1)
                    for c in range(2):
                        mm = nc.tensor.matmul(ps_g[:, f % 2, :], wg[:, c, f * P:(f + 1) * P], h[:, c, :], start=(c == 0), stop=(c == 1))
                    mm.then_inc(k.products, 1)
                    if f >= 2:
                        pe.wait_ge(k.vec_done, f - 1)
                    for c in range(2):
                        mm = nc.tensor.matmul(ps_u[:, f % 2, :], wu[:, c, f * P:(f + 1) * P], h[:, c, :], start=(c == 0), stop=(c == 1))
                    mm.then_inc(k.scored, 1)
                    if f >= 1:
                        down(f - 1)
                down(7).then_inc(k.weighted, 1)

            @block.scalar
            def _(act):
                for f in range(8):
                    act.wait_ge(k.products, f + 1)
                    nc.scalar.activation(a[:, f, :], ps_g[:, f % 2, :], ACT.Silu).then_inc(k.act_done, 1)

            @block.vector
            def _(v):
                for f in range(8):
                    v.wait_ge(k.act_done, f + 1)
                    v.wait_ge(k.scored, f + 1)
                    nc.vector.tensor_tensor(a[:, f, :], a[:, f, :], ps_u[:, f % 2, :], ALU.mult).then_inc(k.vec_done, 1)
                v.wait_ge(k.weighted, 1)
                nc.vector.tensor_tensor(xx[:], xx[:], ps_d[:], ALU.add)


def l2_cross(k, x):
    nc, d = k.nc, k.d
    with ExitStack() as own:
        xx = k.sb(own, "xx", [P, 2, T])
        h = k.sb(own, "h", [P, 2, T])
        kt = k.sb(own, "kt", [P, 2, T])
        ot = k.sb(own, "ot", [P, 2, T])
        wqk = k.sb(own, "wqk", [P, 2, 1024])
        wv, wo, wqc, wkc, wvc, woc = (k.sb(own, n, [P, 2, D]) for n in ("wv", "wo", "wqc", "wkc", "wvc", "woc"))
        lv = k.sb(own, "lv", [P, 18])
        seg_i = k.sb(own, "seg_i", [P, 2 * B], mybir.dt.int32)
        seg_cols = k.sb(own, "seg_cols", [P, 2 * B])
        seg_rows = k.sb(own, "seg_rows", [P, T])
        key_index = k.sb(own, "key_index", [P, 2])
        first_key = k.sb(own, "first_key", [P, 1])
        causal, causal_t = (k.sb(own, n, [P, 2, S], BF16) for n in ("causal", "causal_t"))
        mask = k.sb(own, "mask", [P, 2 * B, KB], BF16)

        def col(name):
            a, b = LAYER_VECS[name]
            return lv[:, a:b]

        count = k.sb(own, "count", [1, 1], mybir.dt.int32)
        with ExitStack() as inner:
            row = k.sb(inner, "seg_row", [1, T], mybir.dt.int32)
            top_i = k.sb(inner, "top_i", [1, 1], mybir.dt.int32)
            small = [k.sb(inner, n, [1, 1]) for n in ("low", "top", "bad")]
            key_blocks = blocks_with_segments(k, count[:], [top_i[:]] + [t[:] for t in small], row[:])
            rows_i = k.sb(inner, "rows_i", [P, T], mybir.dt.int32)
            wide = k.sb(inner, "wide", [P, 4, S])
            with k.stage() as block:
                @block.sync
                def _(sp):
                    sp.dma_start(seg_i[:], d["seg_cols"]).then_inc(k.loaded, 16)
                    sp.dma_start(rows_i[:], d["seg_row"].broadcast_to([P, T])).then_inc(k.loaded, 16)
                    sp.dma_start(wide[:], d["const_causal"]).then_inc(k.loaded, 16)
                    sp.wait_ge(k.loaded, 48)

                @block.vector
                def _(v):
                    v.wait_ge(k.loaded, 48)
                    nc.vector.tensor_copy(seg_cols[:], seg_i[:])
                    nc.vector.tensor_copy(seg_rows[:], rows_i[:])
                    nc.vector.tensor_copy(causal[:], wide[:, 0:2, :])
                    nc.vector.tensor_copy(causal_t[:], wide[:, 2:4, :])
        at = Narrow(k, own)

        def self_weights(layer):
            return [(wqk[:], rows(d["L2_qk"][layer])), (wv[:], rows(d["L2_wv"][layer])), (wo[:], rows(d["L2_wo"][layer])),
                    (lv[:], d["L2_vecs"][layer])]

        norm(k, xx[:], x[:], 1e-5, ahead=self_weights(0))
        with nc.Fori(0, 4) as layer:
            norm(k, h[:], xx[:], 1e-6, mean=False, w=col("n1"))
            rotated_projections(k, at, kt, h, wqk, col("bqk"))
            project_tokens(k, at.val, h, 2, wv, 4, D, strips_of=16, meanwhile=lambda v: at.start(k))
            narrow_maxima(k, at, lambda c, b: kt[:, c, b * S:(b + 1) * S], lambda b, qt: causal[:, qt, :], causal=True)
            narrow_turn(k, at)
            narrow_sums(k, at, lambda c, b, kc: kt[:, c, b * S + kc * P:b * S + (kc + 1) * P], lambda b, kc: causal_t[:, kc, :], causal=True,
                        loads=[(wqc[:], rows(d["L2_wqc"][layer])), (wkc[:], rows(d["L2_wkc"][layer])),
                               (wvc[:], rows(d["L2_wvc"][layer])), (woc[:], rows(d["L2_woc"][layer]))])
            narrow_end(k, at, ot, bias=col("bv"))
            project(k, xx, ot, 2, wo, 2, T, vec=(col("bo"), ALU.add, xx, ALU.add))
            norm(k, h[:], xx[:], 1e-6, mean=False, w=col("n2"))
            with ExitStack() as inner:
                keys = k.sb(inner, "keys", [P, 2, B * SK])
                ctx = k.sb(inner, "ctx", [P, 2, B * KB])
                work = k.sb(inner, "work", [P, 3, KB])

                def ctx_block(j):
                    return [(ctx[:, :, b * KB:(b + 1) * KB], rows(d["ctx_t"][b])[:, :, bass.ds(j * KB, KB)]) for b in range(B)]

                def queries_and_keys(v):
                    nc.vector.memset(first_key[:], 0.0)
                    nc.vector.tensor_copy(key_index[:], k.key_index[:])
                    at.spread_and_start(k, kt)(v)

                project(k, kt, h, 2, wqc, 2, T, meanwhile=queries_and_keys)
                with nc.Fori(0, key_blocks) as j:
                    project(k, keys[:, :, bass.ds(j * B * KB, B * KB)], ctx, 2, wkc, 2, T, loads=ctx_block(j),
                            meanwhile=window_by_query(k, mask, seg_cols, first_key[:], work))
                    narrow_maxima(k, at, lambda c, b: keys[:, c, bass.ds(j * B * KB + b * KB, KB)], lambda b, qt: mask[:, 2 * b + qt, :])
                narrow_turn(k, at)
                with nc.Fori(0, key_blocks) as j:
                    project_tokens(k, at.val, ctx, 2, wvc, 4, D, loads=ctx_block(j), strips_of=16, meanwhile=window_by_key(
                        k, mask, seg_rows, key_index[:], work, kt[:], keys[:, :, bass.ds(j * B * KB, B * KB)]))
                    narrow_sums(k, at, lambda c, b, kc: kt[:, c, b * S + kc * P:b * S + (kc + 1) * P], lambda b, kc: mask[:, 2 * b + kc, :])
                narrow_end(k, at, ot)
            project(k, xx, ot, 2, woc, 2, T, vec=(0.0, ALU.add, xx, ALU.add))
            with ExitStack() as inner:
                wg, wu, wd = k.sb(inner, "wg", [P, 2, 1024]), k.sb(inner, "wu", [P, 2, 1024]), k.sb(inner, "wd", [P, 8, D])
                a = k.sb(inner, "a", [P, 8, T])
                norm(k, h[:], xx[:], 1e-6, mean=False, w=col("n3"), ahead=[
                    (wg[:], rows(d["L2_wg"][layer])), (wu[:], rows(d["L2_wu"][layer])), (wd[:], rows(d["L2_wd"][layer]))])
                feed_forward(k, xx, h, a, wg, wu, wd, loads=self_weights(layer + 1))
        norm(k, x[:], xx[:], 1e-6, mean=False, w=k.vec("L2_xattn_nf"), plus=x)


def l2_self(k, x):
    nc, d = k.nc, k.d
    nh, dim = 16, 16
    with ExitStack() as own:
        h = k.sb(own, "h", [P, 2, T])
        wq, wk, wv, wo = (k.sb(own, n, [P, 2, D]) for n in ("wq", "wk", "wv", "wo"))
        rb = k.sb(own, "rb", [P, 5, D])
        q, key, val = (k.sb(own, n, [P, 4, D]) for n in ("q", "key", "val"))
        rel = k.sb(own, "rel", [P, 6, nh])
        gw = k.sb(own, "gw", [P, dim, 8])
        gb = k.sb(own, "gb", [P, 8])
        ga = k.sb(own, "ga", [P, nh])
        gws = k.sb(own, "gws", [P, dim])
        gbs = k.sb(own, "gbs", [P, 1])
        gate = k.sb(own, "gate", [P, 4, nh])
        prod = k.sb(own, "prod", [P, D])
        sc = k.sb(own, "sc", [P, 4, 3, nh])
        mx = k.sb(own, "mx", [P, 4, nh])
        o = k.sb(own, "o", [P, 4, D])
        ot = k.sb(own, "ot", [P, 2, T])

        def all_rows(src, n):
            return src.unsqueeze(0).broadcast_to([P, n])

        bucket = {-1: 1, 0: 0, 1: 17, 2: 18}
        norm(k, h[:], x[:], 1e-5, ahead=[(wq[:], rows(d["L2_attn_q_w"])), (wk[:], rows(d["L2_attn_k_w"])), (wv[:], rows(d["L2_attn_v_w"])),
                 (wo[:], rows(d["L2_attn_out_w"]))]
             + [(rb[:, i, :], all_rows(d[n], D)) for i, n in enumerate(
                 ["L2_attn_q_b", "L2_attn_k_b", "L2_attn_v_b", "L2_attn_bias_k_row", "L2_attn_bias_v_row"])]
             + [(rel[:, 3 * t + s, :], all_rows(d["L2_attn_rel_emb"][bucket[s - t]], nh)) for t in range(2) for s in range(3)]
             + [(gw[:].rearrange("p a b -> p (a b)"), all_rows(d["L2_attn_grep_w_row"], 128)), (gb[:], all_rows(d["L2_attn_grep_b"], 8)),
                (ga[:], all_rows(d["L2_attn_grep_a_row"], nh))])
        project_tokens(k, q, h, 2, wq, 4, D, bias_rows=rb[:, 0, :])
        project_tokens(k, key, h, 2, wk, 4, D, bias_rows=rb[:, 1, :])
        project_tokens(k, val, h, 2, wv, 4, D, bias_rows=rb[:, 2, :])

        def heads(flat):
            return flat.rearrange("p (h x) -> p h x", h=nh)

        qq = k.sb(own, "qq", [P, 2, 2 * D])
        kk, vv = k.sb(own, "kk", [P, 2, 3 * D]), k.sb(own, "vv", [P, 2, 3 * D])

        def part(flat, n, i):
            return flat.rearrange("p (h n x) -> p h n x", h=nh, n=n)[:, :, i, :]

        with k.stage() as block:
            @block.vector
            def _(v):
                step = Steps(v, k.vec_step)
                step(nc.vector.reduce_sum(gws[:], gw[:], AX))
                step(nc.vector.reduce_sum(gbs[:], gb[:], AX))
                for t in range(4):
                    batch, tile = t // 2, t % 2
                    at = slice(batch * D, (batch + 1) * D)
                    for to, fr in ((qq, q), (kk, key), (vv, val)):
                        step(nc.vector.tensor_copy(to[:, tile, at], fr[:, t, :]))
                for tile in range(2):
                    for to, row in ((kk, 3), (vv, 4)):
                        step(nc.vector.tensor_copy(to[:, tile, 2 * D:3 * D], rb[:, row, :]))
                for t in range(4):
                    step(nc.vector.tensor_tensor(heads(prod[:]), part(qq[:, t % 2, :], 2, t // 2), gws[:].unsqueeze(1).broadcast_to([P, nh, dim]),
                                                 ALU.mult))
                    step(nc.vector.reduce_sum(gate[:, t, :], heads(prod[:]), AX))
                nc.vector.tensor_scalar(gate[:], gate[:], gbs[:], None, ALU.add).then_inc(k.vec_done, 1)
                v.wait_ge(k.act_done, 1)
                step(nc.vector.tensor_tensor(gate[:], gate[:], ga[:].unsqueeze(1).broadcast_to([P, 4, nh]), ALU.mult))
                for t in range(4):
                    for s in range(3):
                        step(nc.vector.tensor_tensor(heads(prod[:]), part(qq[:, t % 2, :], 2, t // 2), part(kk[:, t % 2, :], 3, s),
                                                     ALU.mult))
                        step(nc.vector.reduce_sum(mx[:, t, :], heads(prod[:]), AX))
                        step(nc.vector.tensor_tensor(sc[:, t, s, :], gate[:, t, :], rel[:, 3 * (t // 2) + s, :], ALU.mult))
                        step(nc.vector.scalar_tensor_tensor(out=sc[:, t, s, :], in0=mx[:, t, :], scalar=dim ** -0.5 / 32.0,
                                                            in1=sc[:, t, s, :], op0=ALU.mult, op1=ALU.add))
                step(nc.vector.tensor_tensor(mx[:], sc[:, :, 0, :], sc[:, :, 1, :], ALU.max))
                step(nc.vector.tensor_tensor(mx[:], mx[:], sc[:, :, 2, :], ALU.max))
                for s in range(3):
                    ins = nc.vector.tensor_tensor(sc[:, :, s, :], sc[:, :, s, :], mx[:], ALU.subtract)
                ins.then_inc(k.vec_done, 1)
                v.wait_ge(k.act_done, 2)
                step(nc.vector.tensor_tensor(mx[:], sc[:, :, 0, :], sc[:, :, 1, :], ALU.add))
                step(nc.vector.tensor_tensor(mx[:], mx[:], sc[:, :, 2, :], ALU.add))
                step(nc.vector.reciprocal(mx[:], mx[:]))
                for s in range(3):
                    step(nc.vector.tensor_tensor(sc[:, :, s, :], sc[:, :, s, :], mx[:], ALU.mult))
                for t in range(4):
                    for s in range(3):
                        to = o[:, t, :] if s == 0 else prod[:]
                        step(nc.vector.tensor_tensor(heads(to), part(vv[:, t % 2, :], 3, s), sc[:, t, s, :].unsqueeze(2).broadcast_to([P, nh, dim]),
                                                     ALU.mult))
                        if s:
                            step(nc.vector.tensor_tensor(o[:, t, :], o[:, t, :], prod[:], ALU.add))

            @block.scalar
            def _(act):
                act.wait_ge(k.vec_done, 1)
                nc.scalar.activation(gate[:], gate[:], ACT.Sigmoid).then_inc(k.act_done, 1)
                act.wait_ge(k.vec_done, 2)
                nc.scalar.activation(sc[:], sc[:], ACT.Exp).then_inc(k.act_done, 1)
        to_features(k, ot, o, 4, 2)
        project(k, x, ot, 2, wo, 2, T, vec=(k.vec("L2_attn_out_b"), ALU.add, x, ALU.add))


def to_features(k, dst, src, tiles, chunks):
    nc = k.nc
    with ExitStack() as own:
        ps = k.ps(own, "turn_ps", [P, chunks, 512])
        with k.stage() as block:
            @block.tensor
            def _(pe):
                for c in range(chunks):
                    for t in range(tiles):
                        mm = nc.tensor.transpose(ps[:, c, t * P:(t + 1) * P], src[:, t, c * P:(c + 1) * P], k.ident[:])
                mm.then_inc(k.products, 1)

            @block.scalar
            def _(act):
                act.wait_ge(k.products, 1)
                nc.scalar.activation(dst[:], ps[:, :, 0:tiles * P], ACT.Identity)


def swiglu_turn(k, x, h, bufs, e, n, ahead):
    nc, d = k.nc, k.d
    w1, w3, w2, bv, gate, h1, sig, a, y, ps = bufs
    late = list(range(2, n + ahead))
    with k.stage() as block:
        @block.sync
        def _(sp):
            def fetch(t, sem):
                i = t % 2
                sp.dma_start(bv[:, i], d["L2_ffn_vecs"][e + t]).then_inc(sem, 16)
                sp.dma_start(w1[:, i], rows(d["L2_ffn_w1"][e + t])).then_inc(sem, 16)
                sp.dma_start(w3[:, i], rows(d["L2_ffn_w3"][e + t])).then_inc(sem, 16)
                sp.dma_start(w2[:, i], rows(d["L2_ffn_w2"][e + t])).then_inc(sem, 16)
                sp.dma_start(gate[:, i], d["gate_rows"][e + t].unsqueeze(0).broadcast_to([P, T])).then_inc(sem, 16)

            if n == 0:
                fetch(0, k.loaded)
                sp.wait_ge(k.loaded, 80)
            elif n + ahead > 1:
                fetch(1, k.loaded)
            for t in late:
                sp.wait_ge(k.merged, t - 1)
                fetch(t, k.loaded_next)
            if n and n + ahead > 1:
                sp.wait_ge(k.loaded, 80)
            if late:
                sp.wait_ge(k.loaded_next, 80 * len(late))

        @block.tensor
        def _(pe):
            for t in range(n):
                if t == 1:
                    pe.wait_ge(k.loaded, 80)
                for m in range(4):
                    u = 4 * t + m
                    if u >= 3:
                        pe.wait_ge(k.shifted, u - 2)
                    for wi, w13 in enumerate((w1, w3)):
                        for c in range(2):
                            mm = nc.tensor.matmul(ps[:, 2 * (u % 3) + wi, :], w13[:, t, c, m * P:(m + 1) * P], h[:, c, :],
                                                  start=(c == 0), stop=(c == 1))
                    mm.then_inc(k.products, 1)
            for t in range(n):
                pe.wait_ge(k.vec_done, t + 1)
                if t >= 1:
                    pe.wait_ge(k.turned, t)
                for m in range(2):
                    for c in range(2):
                        mm = nc.tensor.matmul(ps[:, 6 + m, :], w2[:, t, c, m * P:(m + 1) * P], a[:, c, :],
                                              start=(c == 0), stop=(c == 1))
                mm.then_inc(k.weighted, 1)

        @block.scalar
        def _(act):
            for t in range(n):
                if t == 1:
                    act.wait_ge(k.loaded, 80)
                for m in range(4):
                    u = 4 * t + m
                    act.wait_ge(k.products, u + 1)
                    nc.scalar.activation(h1[:, t, m, :], ps[:, 2 * (u % 3), :], ACT.Identity, bias=bv[:, t, m:m + 1]).then_inc(k.act_done, 1)
                act.wait_ge(k.scored, t + 1)
                if t >= 1:
                    act.wait_ge(k.vec_done, t)
                nc.scalar.activation(sig[:], h1[:, t, 0:2, :], ACT.Sigmoid, scale=1.702).then_inc(k.exps, 1)

        @block.vector
        def _(v):
            step = Steps(v, k.vec_step)

            def output(t):
                v.wait_ge(k.weighted, t + 1)
                for m in range(2):
                    ins = nc.vector.scalar_tensor_tensor(out=y[:, m, :], in0=ps[:, 6 + m, :], scalar=bv[:, t, 8 + m:9 + m],
                                                         in1=gate[:, t], op0=ALU.add, op1=ALU.mult)
                    if m == 0:
                        step(ins)
                ins.then_inc(k.turned, 1)
                v.wait_ge(k.turned, t + 1)
                nc.vector.tensor_tensor(x[:], x[:], y[:], ALU.add).then_inc(k.merged, 1)
                v.wait_ge(k.merged, t + 1)

            for t in range(n):
                if t == 1:
                    v.wait_ge(k.loaded, 80)
                for m in range(4):
                    u = 4 * t + m
                    v.wait_ge(k.act_done, u + 1)
                    nc.vector.scalar_tensor_tensor(out=h1[:, t, m, :], in0=ps[:, 2 * (u % 3) + 1, :], scalar=bv[:, t, 4 + m:5 + m],
                                                   in1=h1[:, t, m, :], op0=ALU.add, op1=ALU.mult).then_inc(k.shifted, 1)
                v.wait_ge(k.shifted, 4 * t + 4)
                nc.vector.tensor_scalar(h1[:, t, 0:2, :], h1[:, t, 0:2, :], 7.0, None, ALU.min).then_inc(k.scored, 1)
                step(nc.vector.tensor_scalar(h1[:, t, 2:4, :], h1[:, t, 2:4, :], -7.0, 7.0, ALU.max, ALU.min))
                v.wait_ge(k.scored, t + 1)
                step(nc.vector.scalar_tensor_tensor(out=h1[:, t, 2:4, :], in0=h1[:, t, 2:4, :], scalar=1.0, in1=h1[:, t, 0:2, :],
                                                    op0=ALU.add, op1=ALU.mult))
                v.wait_ge(k.exps, t + 1)
                if t >= 1:
                    v.wait_ge(k.weighted, t)
                nc.vector.tensor_tensor(a[:], h1[:, t, 2:4, :], sig[:], ALU.mult).then_inc(k.vec_done, 1)
                if t >= 1:
                    output(t - 1)
            if n:
                output(n - 1)


def l2_experts(k, x):
    nc, d = k.nc, k.d
    with ExitStack() as own:
        h = k.sb(own, "h", [P, 2, T])
        norm(k, h[:], x[:], 1e-5)
        s, bias = router(k, own, h, "L2_ffn_gate_w_t", "L2_ffn_gate_b")
        softmax8(k, s)
        top = k.sb(own, "top", [P, 4, 8])
        biased = k.sb(own, "biased", [P, 4, 8])
        w = k.sb(own, "w", [P, 4, 8])
        wt = k.sb(own, "wt", [8, T])
        with k.stage() as block:
            @block.vector
            def _(v):
                step = Steps(v, k.vec_step)
                step(nc.vector.tensor_tensor(biased[:], s[:], bias[:].unsqueeze(1).broadcast_to([P, 4, 8]), ALU.add))
                for t in range(4):
                    step(nc.vector.max(top[:, t, :], biased[:, t, :]))
                step(nc.vector.tensor_tensor(w[:], biased[:], top[:, :, 1:2].broadcast_to([P, 4, 8]), ALU.is_ge))
                nc.vector.tensor_tensor(w[:], w[:], s[:], ALU.mult)
        gates_by_expert(k, w, wt)
        store_gates(k, wt, 1.0)
        bufs = (k.sb(own, "w1", [P, 2, 2, 512]), k.sb(own, "w3", [P, 2, 2, 512]), k.sb(own, "w2", [P, 2, 2, D]),
                k.sb(own, "bv", [P, 2, 10]), k.sb(own, "gate", [P, 2, T]), k.sb(own, "h1", [P, 2, 4, T]), k.sb(own, "sig", [P, 2, T]),
                k.sb(own, "a", [P, 2, T]), k.sb(own, "y", [P, 2, T]), k.ps(own, "swi_ps", [P, 8, 512]))
        swiglu_turn(k, x, h, bufs, 0, 0, 1)
        with nc.Fori(0, 4) as i:
            swiglu_turn(k, x, h, bufs, i * 2, 2, 1)
        swiglu_turn(k, x, h, bufs, 8, 1, 0)




def unit_rows(k, own_src, blocks, w, values, scale, outs, ctx_in=None, ln=None):
    nc = k.nc
    tiles = 4 * blocks
    n_out = len(outs(0, None, None))
    with ExitStack() as own:
        ps = k.ps(own, "kv_ps", [P, 2, 2, 512])
        ps_t = k.ps(own, "turn_ps", [P, 2, 4, P])
        kt, vt = k.sb(own, "kt", [P, 2, 4, 512]), k.sb(own, "vt", [P, 2, 4, 512])
        sq, unit = k.sb(own, "sq", [P, 2, 512]), k.sb(own, "unit", [P, 2, 512])
        length = k.sb(own, "length", [P, 2, 8])
        if own_src is None:
            ps_m = k.ps(own, "stat_ps", [P, 2, 512])
            ctx = k.sb(own, "ctx", [P, blocks, 2, 512])
            cen, squares, normed = k.sb(own, "cen", [P, 2, 2, 512]), k.sb(own, "squares", [P, 2, 512]), k.sb(own, "normed", [P, 2, 2, 512])
            root, eps = k.sb(own, "root", [P, 512]), k.sb(own, "eps", [P, 1])
        with k.stage() as block:
            @block.sync
            def _(sp):
                if own_src is None:
                    for u in range(blocks):
                        sp.dma_start(ctx[:, u], ctx_in(u)).then_inc(k.ring_in[u], 16)
                for u in range(blocks):
                    sp.wait_ge(k.unturned, 4 * u + 4)
                    if values:
                        sp.wait_ge(k.evacuated, 4 * u + 4)
                    for to, fr in outs(u, kt[:, u % 2], vt[:, u % 2]):
                        sp.dma_start(to, fr).then_inc(k.values_in[u % 2], 16)
                for s in range(min(2, blocks)):
                    sp.wait_ge(k.values_in[s], 16 * n_out * len(range(s, blocks, 2)))

            @block.tensor
            def _(pe):
                def mean(u):
                    pe.wait_ge(k.ring_in[u], 16)
                    if u >= 1:
                        pe.wait_ge(k.squared, u)
                    for c in range(2):
                        mm = nc.tensor.matmul(ps_m[:, 0, :], k.mean_mat[:], ctx[:, u, c, :], start=(c == 0), stop=(c == 1))
                    mm.then_inc(k.means, 1)

                def mean_square(u):
                    pe.wait_ge(k.squared, u + 1)
                    if u >= 1:
                        pe.wait_ge(k.roots, u)
                    for c in range(2):
                        mm = nc.tensor.matmul(ps_m[:, 1, :], k.mean_mat[:], squares[:, c, :], start=(c == 0), stop=(c == 1))
                    mm.then_inc(k.mean_squares, 1)

                def turn(i):
                    pe.wait_ge(k.shifted, i + 1)
                    if i >= 2:
                        pe.wait_ge(k.unturned, i - 1)
                    for c in range(4):
                        mm = nc.tensor.transpose(ps_t[:, i % 2, c, :], unit[:, i % 2, c * P:(c + 1) * P], k.ident[:])
                    mm.then_inc(k.turned, 1)

                if own_src is None:
                    mean(0)
                    mean_square(0)
                for i in range(tiles):
                    u, t = i // 4, i % 4
                    if own_src is None and t == 0:
                        pe.wait_ge(k.normed, u + 1)
                    src = own_src if own_src is not None else normed[:, u % 2]
                    if i >= 2:
                        pe.wait_ge(k.shifted, i - 1)
                        if values:
                            pe.wait_ge(k.evacuated, i - 1)
                    for f in range(2 if values else 1):
                        for c in range(2):
                            mm = nc.tensor.matmul(ps[:, i % 2, f, :], src[:, c, t * P:(t + 1) * P], w[:, c, f * 512:(f + 1) * 512],
                                                  start=(c == 0), stop=(c == 1))
                    mm.then_inc(k.products, 1)
                    if own_src is None and u + 1 < blocks:
                        if t == 0:
                            mean(u + 1)
                        if t == 1:
                            mean_square(u + 1)
                    if i >= 1:
                        turn(i - 1)
                turn(tiles - 1)

            @block.scalar
            def _(act):
                def root_of(u):
                    act.wait_ge(k.mean_squares, u + 1)
                    if u >= 1:
                        act.wait_ge(k.normed, u)
                    nc.scalar.activation(root[:], ps_m[:, 1, :], ACT.Sqrt, bias=eps[:]).then_inc(k.roots, 1)

                def keys_out(i):
                    act.wait_ge(k.turned, i + 1)
                    if i % 4 == 0 and i >= 8:
                        act.wait_ge(k.values_in[(i // 4) % 2], 16 * n_out * (i // 8))
                    nc.scalar.activation(kt[:, (i // 4) % 2, :, (i % 4) * P:(i % 4 + 1) * P], ps_t[:, i % 2], ACT.Identity,
                                         scale=scale).then_inc(k.unturned, 1)

                if own_src is None:
                    root_of(0)
                for i in range(tiles):
                    act.wait_ge(k.products, i + 1)
                    if i >= 2:
                        act.wait_ge(k.scored, i - 1)
                    nc.scalar.activation(sq[:, i % 2, :], ps[:, i % 2, 0, :], ACT.Square).then_inc(k.exps, 1)
                    act.wait_ge(k.scored, i + 1)
                    nc.scalar.activation(length[:, i % 2, :], length[:, i % 2, :], ACT.Sqrt).then_inc(k.act_done, 1)
                    if values:
                        if i % 4 == 0 and i >= 8:
                            act.wait_ge(k.values_in[(i // 4) % 2], 16 * n_out * (i // 8))
                        nc.scalar.activation(vt[:, (i // 4) % 2, i % 4, :], ps[:, i % 2, 1, :], ACT.Identity).then_inc(k.evacuated, 1)
                    if i >= 1:
                        keys_out(i - 1)
                    if own_src is None and i % 4 == 1 and i // 4 + 1 < blocks:
                        root_of(i // 4 + 1)
                keys_out(tiles - 1)

            @block.vector
            def _(v):
                step = Steps(v, k.vec_step)

                def centre(u):
                    v.wait_ge(k.means, u + 1)
                    step(nc.vector.tensor_tensor(cen[:, u % 2], ctx[:, u], ps_m[:, 0, :].unsqueeze(1).broadcast_to([P, 2, 512]), ALU.subtract))
                    if u >= 1:
                        v.wait_ge(k.mean_squares, u)
                    nc.vector.tensor_tensor(squares[:], cen[:, u % 2], cen[:, u % 2], ALU.mult).then_inc(k.squared, 1)

                def normalise(u):
                    v.wait_ge(k.roots, u + 1)
                    step(nc.vector.reciprocal(root[:], root[:]))
                    for c in range(2):
                        step(nc.vector.scalar_tensor_tensor(out=cen[:, u % 2, c, :], in0=cen[:, u % 2, c, :], scalar=ln[0][:, c:c + 1],
                                                            in1=root[:], op0=ALU.mult, op1=ALU.mult))
                    if u >= 2:
                        v.wait_ge(k.products, 4 * (u - 1))
                    for c in range(2):
                        ins = nc.vector.tensor_scalar(normed[:, u % 2, c, :], cen[:, u % 2, c, :], ln[1][:, c:c + 1], None, ALU.add)
                        if c == 0:
                            step(ins)
                    ins.then_inc(k.normed, 1)

                if own_src is None:
                    nc.vector.memset(eps[:], 1e-5)
                    centre(0)
                    normalise(0)
                for i in range(tiles):
                    v.wait_ge(k.exps, i + 1)
                    nc.vector.reduce_sum(length[:, i % 2, :], sq[:, i % 2, :].rearrange("p (h x) -> p h x", h=8), AX).then_inc(k.scored, 1)
                    v.wait_ge(k.act_done, i + 1)
                    step(nc.vector.tensor_scalar(length[:, i % 2, :], length[:, i % 2, :], 1e-12, None, ALU.max))
                    step(nc.vector.reciprocal(length[:, i % 2, :], length[:, i % 2, :]))
                    if i >= 2:
                        v.wait_ge(k.turned, i - 1)
                    nc.vector.tensor_tensor(unit[:, i % 2, :].rearrange("p (h x) -> p h x", h=8),
                                            ps[:, i % 2, 0, :].rearrange("p (h x) -> p h x", h=8),
                                            length[:, i % 2, :].unsqueeze(2).broadcast_to([P, 8, 64]), ALU.mult).then_inc(k.shifted, 1)
                    if own_src is None and i // 4 + 1 < blocks:
                        if i % 4 == 0:
                            centre(i // 4 + 1)
                        if i % 4 == 1:
                            normalise(i // 4 + 1)


def l3_cross(k, x):
    nc, d = k.nc, k.d
    sa = Streamed(8, 64, SK + S, 8.0, split=False)
    with ExitStack() as own:
        ot = k.sb(own, "ot", [P, 4, T])
        wo = k.sb(own, "wo", [P, 4, D])
        o = k.sb(own, "att_o", [P, 2, 512])
        with ExitStack() as inner:
            lat = k.sb(inner, "lat", [P, 2, T])
            wq, wkv = k.sb(inner, "wq", [P, 2, 512]), k.sb(inner, "wkv", [P, 2, 1024])
            norm(k, lat[:], x[:], 1e-5)
            norm(k, lat[:], lat[:], 1e-5, w=k.vec("L3_xattn_ln_l_w"), b=k.vec("L3_xattn_ln_l_b"), ahead=[(wq[:], rows(d["L3_xattn_Wq"])), (wkv[:], rows(d["L3_xattn_Wkv"])), (wo[:], rows(d["L3_xattn_Wo"]))])

            def keys_to(b, at, n):
                return rows(d["k_full"][b])[:, :, bass.ds(at, n)]

            def values_to(b, at, n):
                return d["v_full"][b][bass.ds(at, n), :].rearrange("(c p) f -> p c f", p=P)

            def latents_out(u, kt, vt):
                if kt is None:
                    return range(2 * B)
                return [(keys_to(b, SK, S), kt[:, :, b * S:(b + 1) * S]) for b in range(B)] + \
                       [(values_to(b, SK, S), vt[:, 2 * b:2 * b + 2, :]) for b in range(B)]

            def queries_out(u, kt, vt):
                return range(1) if kt is None else [(rows(d["q_full"]), kt)]

            unit_rows(k, lat[:], 1, wq, False, k.vec("q_scale2"), queries_out)
            unit_rows(k, lat[:], 1, wkv, True, k.vec("k_scale2"), latents_out)
            with nc.Fori(0, B) as b:
                with nc.Fori(0, SK // 2048) as j:
                    def context_out(u, kt, vt):
                        if kt is None:
                            return range(2)
                        return [(keys_to(b, j * 2048 + u * 512, 512), kt), (values_to(b, j * 2048 + u * 512, 512), vt)]

                    unit_rows(k, None, 4, wkv, True, k.vec("k_scale2"), context_out,
                              ctx_in=lambda u: rows(d["ctx_t"][b])[:, :, bass.ds(j * 2048 + u * 512, 512)],
                              ln=(k.vec("L3_xattn_ln_x_w"), k.vec("L3_xattn_ln_x_b")))
        with ExitStack() as inner:
            bufs = streamed_buffers(k, inner, sa, None, o)
            with nc.Fori(0, B) as b:
                mask_row(k, sa, bufs[0], "mask_BxS2_bk0", mybir.dt.uint8, b)
                heads_turns(k, sa, bufs, 0, True, False, b)
                heads_turns(k, sa, bufs, 0, False, False, b)
                heads_turns(k, sa, bufs, 1, False, True, b)
                outputs_to_features(k, o, ot, 4, b)
        with ExitStack() as inner:
            h = k.sb(inner, "h", [P, 2, T])
            project(k, h, ot, 4, wo, 2, T)
            norm(k, x[:], h[:], 1e-5, w=k.vec("L3_xattn_ln_o_w"), b=k.vec("L3_xattn_ln_o_b"), plus=x)


def l3_self(k, x):
    nc, d = k.nc, k.d
    with ExitStack() as own:
        h, hk, hv, q, kt, ot = (k.sb(own, n, [P, 2, T]) for n in ("h", "hk", "hv", "q", "kt", "ot"))
        wq, wk, wv, wl, wo = (k.sb(own, n, [P, 2, D]) for n in ("wq", "wk", "wv", "wl", "wo"))
        at = Narrow(k, own)
        norm(k, h[:], x[:], 1e-5)
        project(k, q, h, 2, wq, 2, T, bias=k.vec("L3_attn_bq"), loads=[
            (wq[:], rows(d["L3_attn_Wq"])), (wk[:], rows(d["L3_attn_Wk"])), (wv[:], rows(d["L3_attn_Wv"])),
            (wl[:], rows(d["L3_attn_Wl"])), (wo[:], rows(d["L3_attn_Wo"]))], meanwhile=at.spread_and_start(k, q))
        project(k, hk, h, 2, wk, 2, T, bias=k.vec("L3_attn_bk"))
        project(k, hv, h, 2, wv, 2, T, bias=k.vec("L3_attn_bv"))
        project(k, kt, hk, 2, wl, 2, T, bias=k.vec("L3_attn_bl"))
        project_tokens(k, at.val, hv, 2, wl, 4, D, strips_of=16)
        narrow_maxima(k, at, lambda c, b: kt[:, c, b * S:(b + 1) * S])
        narrow_turn(k, at)
        narrow_sums(k, at, lambda c, b, kc: kt[:, c, b * S + kc * P:b * S + (kc + 1) * P])
        narrow_end(k, at, ot, bias=k.vec("L3_attn_bl"))
        project(k, x, ot, 2, wo, 2, T, vec=(k.vec("L3_attn_bo"), ALU.add, x, ALU.add))


def l3_experts(k, x):
    nc = k.nc
    capacity = int(S * 2.0 / 8) + 1
    with ExitStack() as own:
        h = k.sb(own, "h", [P, 2, T])
        norm(k, h[:], x[:], 1e-5)
        s, _ = router(k, own, h, "L3_ffn_router_w_t")
        softmax8(k, s)
        st = k.sb(own, "st", [8, T])
        gates_by_expert(k, s, st)
        work = k.sb(own, "work", [8, B, 2, S])
        top = k.sb(own, "top", [8, B, 8])
        wt = k.sb(own, "wt", [8, T])
        with k.stage() as block:
            @block.vector
            def _(v):
                step = Steps(v, k.vec_step)
                for b in range(B):
                    own_scores = st[:, b * S:(b + 1) * S]
                    src = own_scores
                    for r in range((capacity - 1) // 8):
                        step(nc.vector.max(top[:, b, :], src))
                        step(nc.vector.match_replace(work[:, b, r % 2, :], top[:, b, :], src, -1.0))
                        src = work[:, b, r % 2, :]
                    step(nc.vector.max(top[:, b, :], src))
                    last = (capacity - 1) % 8
                    step(nc.vector.tensor_scalar(wt[:, b * S:(b + 1) * S], own_scores, top[:, b, last:last + 1], None, ALU.is_ge))
                nc.vector.tensor_tensor(wt[:], wt[:], st[:], ALU.mult)
        store_gates(k, wt)
        experts_gelu(k, x, h, 8, "L3_ffn_w1", "L3_ffn_w2", "L3_ffn_vecs")


SUBLAYERS = [l0_cross, l0_scan, l0_experts, l1_cross, l1_self, l1_ffn, l2_cross, l2_self, l2_experts,
             l3_cross, l3_self, l3_experts]


def build(nc, d, out, sublayers=tuple(range(len(SUBLAYERS)))):
    with ExitStack() as ctx:
        k = Core(nc, d, ctx)
        x = k.sb(ctx, "x", [P, 2, T])
        k.vecs = k.sb(ctx, "vecs", [P, N_VECS])
        k.ident = k.sb(ctx, "ident", [P, P])
        k.mean_mat = k.sb(ctx, "mean_mat", [P, P])
        k.fold = k.sb(ctx, "fold", [P, 17])
        k.cos, k.sin, k.iota = (k.sb(ctx, n, [P, S]) for n in ("cos", "sin", "iota"))
        k.head_rows = k.sb(ctx, "head_rows", [P, 8])
        k.key_index = k.sb(ctx, "key_index", [P, 2])
        k.ident_b = k.sb(ctx, "ident_b", [P, P], BF16)
        k.pick_head = k.sb(ctx, "pick_head", [32, 16, P], BF16)
        load(k, [(x[:], rows(d["x_t"])), (k.vecs[:], d["vecs"]), (k.ident[:], d["const_ident"]),
                 (k.mean_mat[:], d["const_mean"]), (k.cos[:], d["const_cos"]),
                 (k.sin[:], d["const_sin"]), (k.iota[:], d["const_iota"]), (k.fold[:], d["const_fold"]), (k.head_rows[:], d["const_head_rows"]),
                 (k.key_index[:], d["const_key_index"])])
        with ExitStack() as inner:
            pick = k.sb(inner, "pick", [32, 16])
            with k.stage() as block:
                @block.sync
                def _(sp):
                    sp.dma_start(pick[:], d["const_pick"]).then_inc(k.loaded, 16)

                @block.vector
                def _(v):
                    nc.vector.tensor_copy(k.ident_b[:], k.ident[:])
                    v.wait_ge(k.loaded, 16)
                    nc.vector.tensor_copy(k.pick_head[:], pick[:].unsqueeze(2).broadcast_to([32, 16, P]))
        for i in sublayers:
            SUBLAYERS[i](k, x)
        with nc.Block() as block:
            @block.sync
            def _(sp):
                sp.dma_start(rows(out), x[:]).then_inc(k.stored, 16)
                sp.wait_ge(k.stored, 16)




def turned(w):
    h = w.reshape(w.shape[:-1] + (16, 2, 8))
    return np.ascontiguousarray(h[..., ::-1, :]).reshape(w.shape)


def columns(v):
    return np.swapaxes(v.reshape(v.shape[:-1] + (-1, P)), -1, -2)


def constants():
    f = np.float32
    c = {"const_ident": np.eye(P, dtype=f), "const_mean": np.full((P, P), 1.0 / D, f),
         "const_fold": np.tile(np.eye(32, 17, dtype=f), (4, 1)),
         "const_iota": np.broadcast_to(np.arange(KB, dtype=f), (P, KB)).copy()}
    inv = 1.0 / 10000.0 ** (np.arange(0, 16, 2).astype(f) / f(16))
    ang = (np.arange(S, dtype=f)[:, None] * inv[None, :].astype(f)).astype(f)
    cos, sin = np.zeros((8, 16, S), f), np.zeros((8, 16, S), f)
    cos[:, 0:8], cos[:, 8:16] = np.cos(ang).T, np.cos(ang).T
    sin[:, 0:8], sin[:, 8:16] = -np.sin(ang).T, np.sin(ang).T
    c["const_cos"], c["const_sin"] = cos.reshape(P, S), sin.reshape(P, S)
    place, other = np.arange(S).reshape(2, P).T[:, :, None], np.arange(S)[None, None, :]
    c["const_causal"] = np.concatenate([np.where(other <= place, 0.0, NEG), np.where(place <= other, 0.0, NEG)], 1).astype(f)
    c["const_head_rows"] = np.kron(np.eye(8), np.ones((16, 1))).astype(f)
    c["const_key_index"] = np.ascontiguousarray(np.arange(KB, dtype=f).reshape(2, P).T)
    c["const_pick"] = np.tile(np.eye(16, dtype=f), (2, 1))
    return c


def layouts(i):
    t = lambda a: np.swapaxes(a, -1, -2)
    cat = np.concatenate
    a = {"x_t": i["x"].transpose(2, 0, 1).reshape(D, T), "ctx_t": i["ctx_1024"].transpose(0, 2, 1),
         "mask_BxS2_ik1": i["mask_BxS2_ik1"], "mask_BxS2_bk0": i["mask_BxS2_bk0"],
         "seg_row": i["itok_BxS_0_255"].reshape(1, T), "seg_cols": i["itok_BxS_0_255"].reshape(2 * B, P).T}
    for n in ("L0_xattn_Wq", "L0_xattn_Wk", "L0_xattn_Wv", "L0_xattn_Wo", "L0_ffn_gate_bias", "ctx_1024", "L1_xattn_Wk", "L1_attn_w_o", "L2_attn_q_w", "L2_attn_k_w", "L2_attn_v_w",
              "L2_attn_out_w", "L2_attn_q_b", "L2_attn_k_b", "L2_attn_v_b", "L2_attn_rel_emb", "L2_attn_grep_b", "L2_ffn_gate_b",
              "L3_xattn_Wq", "L3_xattn_Wkv", "L3_xattn_Wo", "L3_attn_Wq", "L3_attn_Wk", "L3_attn_Wv", "L3_attn_Wl", "L3_attn_Wo",
              "L3_ffn_w1", "L3_ffn_w2"):
        a[n] = i[n]
    for n in ("L0_attn_w_in", "L0_attn_w_out", "L0_attn_w_dt", "L0_ffn_gate_w", "L1_xattn_Wv", "L1_xattn_Wq",
              "L1_xattn_Wo", "L2_ffn_gate_w", "L3_ffn_router_w"):
        a[n + "_t"] = t(i[n])
    a["L0_attn_w_xproj_t"] = cat([t(i["L0_attn_w_xproj"]), np.zeros((512, 32), np.float32)], 1)
    a["L0_ffn_up"] = t(cat([i["L0_ffn_Wu"], i["L0_ffn_sWu"][None]]))
    a["L0_ffn_down"] = t(cat([i["L0_ffn_Wd"], i["L0_ffn_sWd"][None]]))
    a["L0_ffn_vecs"] = columns(cat([cat([i["L0_ffn_bu"], i["L0_ffn_sbu"][None]]), cat([i["L0_ffn_bd"], i["L0_ffn_sbd"][None]])], 1))
    for n in "qkv":
        a[f"L1_attn_w_{n}_t"] = i[f"L1_attn_w_{n}"].transpose(1, 0, 2).reshape(D, 1024)
    for n in ("w1", "w2", "h1", "h2", "w3"):
        a[f"L1_ffn_{n}_t"] = t(i[f"L1_ffn_{n}_w"])
    wqkv, bqkv = t(i["L2_xattn_Wqkv"]), i["L2_xattn_bqkv"]
    a["L2_qk"] = cat([wqkv[..., 0:D], turned(wqkv[..., 0:D]), wqkv[..., D:2 * D], turned(wqkv[..., D:2 * D])], -1)
    a["L2_wv"], a["L2_wo"] = wqkv[..., 2 * D:], t(i["L2_xattn_Wo"])
    a["L2_wqc"], a["L2_wkc"] = t(i["L2_xattn_Wq_c"]), t(i["L2_xattn_Wkv_c"][:, 0:D])
    a["L2_wvc"], a["L2_woc"] = t(i["L2_xattn_Wkv_c"][:, D:]), t(i["L2_xattn_Wo_c"])
    a["L2_wg"], a["L2_wu"], a["L2_wd"] = t(i["L2_xattn_Wg"]), t(i["L2_xattn_Wu"]), t(i["L2_xattn_Wd"])
    a["L2_vecs"] = columns(cat([bqkv[:, 0:D], turned(bqkv[:, 0:D]), bqkv[:, D:2 * D], turned(bqkv[:, D:2 * D]), bqkv[:, 2 * D:], i["L2_xattn_bo"], i["L2_xattn_n1"],
                                i["L2_xattn_n2"], i["L2_xattn_n3"]], 1))
    for n in ("L2_qk", "L2_wv", "L2_wo", "L2_vecs"):
        a[n] = cat([a[n], a[n][:1]])
    a["L2_attn_bias_k_row"], a["L2_attn_bias_v_row"] = i["L2_attn_bias_k"].reshape(D), i["L2_attn_bias_v"].reshape(D)
    a["L2_attn_grep_w_row"], a["L2_attn_grep_a_row"] = i["L2_attn_grep_w"].reshape(128), i["L2_attn_grep_a"].reshape(16)
    halves = lambda w: cat([w[:, 0::2], w[:, 1::2]], 1)
    for n in ("1", "3"):
        a[f"L2_ffn_w{n}"] = t(halves(cat([i[f"L2_ffn_w{n}"], i[f"L2_ffn_sw{n}"][None]])))
    a["L2_ffn_w2"] = t(cat([i["L2_ffn_w2"], i["L2_ffn_sw2"][None]]))
    a["L2_ffn_vecs"] = columns(cat([halves(cat([i["L2_ffn_b1"], i["L2_ffn_sb1"][None]])),
                                    halves(cat([i["L2_ffn_b3"], i["L2_ffn_sb3"][None]])),
                                    cat([i["L2_ffn_b2"], i["L2_ffn_sb2"][None]])], 1))
    a["L3_ffn_vecs"] = columns(cat([i["L3_ffn_b1"], i["L3_ffn_b2"]], 1))
    conv = i["L0_attn_w_conv"].reshape(4, P, 4).transpose(1, 0, 2).reshape(P, 16)
    a_log = i["L0_attn_A_log"].reshape(4, P, 16).transpose(1, 2, 0).reshape(P, 64)
    own = {"q_scale2": np.tile(i["L3_xattn_q_scale"], 2)[:, None], "k_scale2": np.tile(i["L3_xattn_k_scale"], 2)[:, None],
           "conv": conv, "A_log": a_log, "eps_5": np.full((P, 1), 1e-5, np.float32), "eps_6": np.full((P, 1), 1e-6, np.float32)}
    a["vecs"] = cat([own[n] if n in own else columns(i[n]) for n, _ in VECS], 1)
    return {n: np.ascontiguousarray(v) for n, v in a.items()}


SCRATCH = (("bc_rows", (32, T), F32), ("gate_rows", (9, T), F32), ("k_parts", (3, D, SK), BF16), ("q_parts", (3, D, T), BF16),
           ("k_full", (B, 512, SK + S), F32), ("q_full", (512, T), F32), ("v_full", (B, SK + S, 512), F32))


def kernel(**inputs):
    import concourse.bacc as bacc
    from concourse.bass_utils import run_bass_kernel_spmd

    arrays = {**layouts({n: np.asarray(v) for n, v in inputs.items()}), **constants()}
    nc = bacc.Bacc("TRN2", target_bir_lowering=False, num_devices=1)
    d = {n: nc.dram_tensor(n, v.shape, mybir.dt.from_np(v.dtype), kind="ExternalInput").ap() for n, v in arrays.items()}
    for name, shape, dt in SCRATCH:
        d[name] = nc.dram_tensor(name, shape, dt, kind="Internal").ap()
    out = nc.dram_tensor("out_t", (D, T), F32, kind="ExternalOutput").ap()
    build(nc, d, out)
    r = run_bass_kernel_spmd(nc, [arrays], core_ids=[0])
    return np.ascontiguousarray(r.results[0]["out_t"].reshape(D, B, S).transpose(1, 2, 0))
```
